# Optimizing a Trainium2 kernel written in Bass

```python
import numpy as np
import jax
import jax.numpy as jnp

def _softmax(x, axis=-1):
    return jax.nn.softmax(x, axis=axis)

def _gelu(x):
    return jax.nn.gelu(x, approximate=True)

def _silu(x):
    return jax.nn.silu(x)

def _sigmoid(x):
    return jax.nn.sigmoid(x)

def _layernorm(x, axis=-1, eps=1e-05):
    m = jnp.mean(x, axis=axis, keepdims=True)
    v = jnp.var(x, axis=axis, keepdims=True)
    return (x - m) / jnp.sqrt(v + eps)

def _scatter_add(tgt, idx, src, axis=0):
    return tgt.at[idx].add(src)

def _segment_sum(src, seg, n):
    return jax.ops.segment_sum(src, seg, n)
kernel_name = 'mk_seq_postln_d2_jaxref_r4_8dbd4f'

def setup_inputs(seed: int=0):
    np.random.seed(seed)
    _w = jnp.asarray

    def _L0_attn_setup():
        import jax, jax.numpy as jnp
        from jax import lax
        import numpy as np
        D_MODEL = 256
        D_STATE = 64
        D_CONV = 4
        EXPAND = 2
        HEADDIM = 64
        D_INNER = EXPAND * D_MODEL
        NHEADS = D_INNER // HEADDIM
        CHUNK = 64
        CONV_DIM = D_INNER + 2 * D_STATE
        D_IN_PROJ = 2 * D_INNER + 2 * D_STATE + NHEADS
        B_SZ = 4
        SEQLEN = 512
        EPS = 1e-05

        def _silu(x):
            return x * jax.nn.sigmoid(x)

        def _segsum(x):
            T = x.shape[-1]
            xe = jnp.broadcast_to(x[..., None], x.shape + (T,))
            strict_lower = jnp.tril(jnp.ones((T, T), bool), -1)
            xe = jnp.where(strict_lower, xe, 0.0)
            s = jnp.cumsum(xe, axis=-2)
            lower = jnp.tril(jnp.ones((T, T), bool), 0)
            return jnp.where(lower, s, -jnp.inf)
        key = jax.random.key(seed)
        ks = jax.random.split(key, 5)
        u = jax.random.normal(ks[0], (B_SZ, SEQLEN, D_MODEL), jnp.float32)
        W_in = jax.random.normal(ks[1], (D_IN_PROJ, D_MODEL), jnp.float32) * 0.02
        conv_w = jax.random.normal(ks[2], (CONV_DIM, 1, D_CONV), jnp.float32) * 0.2
        conv_b = jnp.zeros((CONV_DIM,), jnp.float32)
        dt_bias = jax.random.uniform(ks[3], (NHEADS,), jnp.float32, -1.0, 1.0)
        A_log = jnp.log(jnp.linspace(1.0, float(NHEADS), NHEADS)).astype(jnp.float32)
        D = jnp.ones((NHEADS,), jnp.float32)
        norm_w = jnp.ones((D_INNER,), jnp.float32)
        W_out = jax.random.normal(ks[4], (D_MODEL, D_INNER), jnp.float32) * 0.02
        return dict(u=u, W_in=W_in, conv_w=conv_w, conv_b=conv_b, dt_bias=dt_bias, A_log=A_log, D=D, norm_w=norm_w, W_out=W_out)
    _L0_attn_in = _L0_attn_setup()

    def _L0_ffn_setup():
        import jax, jax.numpy as jnp
        import numpy as np
        B, S, DIM = (4, 1024, 256)
        BASE_COUPLING = 0.1
        NUM_CYCLES = 3

        def _gelu(x):
            return jax.nn.gelu(x, approximate=False)

        def _coupling_net(h, w1, b1, w2, b2, w3, b3, w4, b4):
            h = _gelu(h @ w1 + b1)
            h = _gelu(h @ w2 + b2)
            h = _gelu(h @ w3 + b3)
            return jax.nn.sigmoid(h @ w4 + b4)

        def _global_net(h, w1, b1, w2, b2, w3, b3):
            h = _gelu(h @ w1 + b1)
            h = _gelu(h @ w2 + b2)
            return jax.nn.sigmoid(h @ w3 + b3)

        def _twist(x):
            o_r, o_i, p_r, p_i = jnp.split(x, 4, axis=-1)
            return jnp.concatenate([p_r, -p_i, -o_r, o_i], axis=-1)
        key = jax.random.key(seed)
        ks = jax.random.split(key, 9)
        d = DIM

        def w(k, fan_in, fan_out):
            return jax.random.normal(k, (fan_in, fan_out), dtype=jnp.float32) / np.sqrt(fan_in).astype(np.float32)
        inp = {'x': jax.random.normal(ks[0], (B, S, d), dtype=jnp.float32)}
        cn_dims = [(d, d), (d, d // 2), (d // 2, d // 4), (d // 4, 1)]
        for i, (a, b) in enumerate(cn_dims):
            inp[f'cn_w{i + 1}'] = w(ks[1 + i], a, b)
            inp[f'cn_b{i + 1}'] = jnp.zeros((b,), dtype=jnp.float32)
        gc_dims = [(d, d // 2), (d // 2, d // 4), (d // 4, 1)]
        for i, (a, b) in enumerate(gc_dims):
            inp[f'gc_w{i + 1}'] = w(ks[5 + i], a, b)
            inp[f'gc_b{i + 1}'] = jnp.zeros((b,), dtype=jnp.float32)
        inp['adaptive_range'] = jnp.full((1,), 0.2, dtype=jnp.float32)
        return inp
    _L0_ffn_in = _L0_ffn_setup()

    def _L1_attn_setup():
        import jax, jax.numpy as jnp
        import numpy as np
        HIDDEN = 256
        STATE = 16
        BATCH = 4
        SEQ = 512
        LN_EPS = 1e-05

        def _selective_scan(x_ssm, dt, A, Bm, Cm):
            Bsz, L, D = x_ssm.shape
            N = A.shape[1]

            def step(h, inp):
                xt, dtt, bt, ct = inp
                dA = jnp.exp(A[None] * dtt[..., None])
                dB = dtt[..., None] * bt[:, None, :]
                h = dA * h + dB * xt[..., None]
                y = jnp.sum(h * ct[:, None, :], axis=-1)
                return (h, y)
            h0 = jnp.zeros((Bsz, D, N), x_ssm.dtype)
            xs = (jnp.swapaxes(x_ssm, 0, 1), jnp.swapaxes(dt, 0, 1), jnp.swapaxes(Bm, 0, 1), jnp.swapaxes(Cm, 0, 1))
            _, ys = jax.lax.scan(step, h0, xs)
            return jnp.swapaxes(ys, 0, 1)
        key = jax.random.key(seed)
        ks = jax.random.split(key, 16)
        D, N = (HIDDEN, STATE)
        s = 0.02
        return {'x': jax.random.normal(ks[0], (BATCH, SEQ, D), dtype=jnp.float32), 'w_in': jax.random.normal(ks[1], (2 * D, D), dtype=jnp.float32) * s, 'b_in': jnp.zeros((2 * D,), jnp.float32), 'w_dt': jax.random.normal(ks[2], (D, D), dtype=jnp.float32) * s, 'b_dt': jnp.zeros((D,), jnp.float32), 'A_log': jax.random.normal(ks[3], (D, N), dtype=jnp.float32), 'w_B': jax.random.normal(ks[4], (N, D), dtype=jnp.float32) * s, 'b_B': jnp.zeros((N,), jnp.float32), 'w_C': jax.random.normal(ks[5], (N, D), dtype=jnp.float32) * s, 'b_C': jnp.zeros((N,), jnp.float32), 'D': jnp.ones((D,), jnp.float32), 'w_out': jax.random.normal(ks[6], (D, D), dtype=jnp.float32) * s, 'b_out': jnp.zeros((D,), jnp.float32), 'gamma': jnp.ones((D,), jnp.float32), 'beta': jnp.zeros((D,), jnp.float32)}
    _L1_attn_in = _L1_attn_setup()

    def _L1_ffn_setup():
        import jax, jax.numpy as jnp
        import numpy as np
        B, S, H, F, G = (8, 512, 256, 1024, 128)
        EPS = 1e-05

        def _dequant(q, scales, g):
            K, N = q.shape
            w = (q.astype(jnp.float32) - 128.0).reshape(K // g, g, N) * scales[:, None, :]
            return w.reshape(K, N)
        key = jax.random.key(seed)
        ks = jax.random.split(key, 8)
        x = jax.random.normal(ks[0], (B, S, H), dtype=jnp.float32)
        ln_gamma = jnp.ones((H,), jnp.float32)
        ln_beta = jnp.zeros((H,), jnp.float32)
        fc1_q = jax.random.randint(ks[1], (H, F), 0, 64, dtype=jnp.int32)
        fc2_q = jax.random.randint(ks[2], (F, H), 0, 64, dtype=jnp.int32)
        fc1_scales = jax.random.uniform(ks[3], (H // G, F), jnp.float32) * 0.02 + 0.001
        fc2_scales = jax.random.uniform(ks[4], (F // G, H), jnp.float32) * 0.02 + 0.001
        fc1_bias = jax.random.normal(ks[5], (F,), jnp.float32) * 0.02
        fc2_bias = jax.random.normal(ks[6], (H,), jnp.float32) * 0.02
        return {'x': x, 'ln_gamma': ln_gamma, 'ln_beta': ln_beta, 'fc1_q': fc1_q, 'fc1_scales': fc1_scales, 'fc1_bias': fc1_bias, 'fc2_q': fc2_q, 'fc2_scales': fc2_scales, 'fc2_bias': fc2_bias}
    _L1_ffn_in = _L1_ffn_setup()
    _d = {'L0_attn_u': _L0_attn_in['u'], 'L0_attn_W_in': _L0_attn_in['W_in'], 'L0_attn_conv_w': _L0_attn_in['conv_w'], 'L0_attn_conv_b': _L0_attn_in['conv_b'], 'L0_attn_dt_bias': _L0_attn_in['dt_bias'], 'L0_attn_A_log': _L0_attn_in['A_log'], 'L0_attn_D': _L0_attn_in['D'], 'L0_attn_norm_w': _L0_attn_in['norm_w'], 'L0_attn_W_out': _L0_attn_in['W_out'], 'L0_ffn_cn_w1': _L0_ffn_in['cn_w1'], 'L0_ffn_cn_b1': _L0_ffn_in['cn_b1'], 'L0_ffn_cn_w2': _L0_ffn_in['cn_w2'], 'L0_ffn_cn_b2': _L0_ffn_in['cn_b2'], 'L0_ffn_cn_w3': _L0_ffn_in['cn_w3'], 'L0_ffn_cn_b3': _L0_ffn_in['cn_b3'], 'L0_ffn_cn_w4': _L0_ffn_in['cn_w4'], 'L0_ffn_cn_b4': _L0_ffn_in['cn_b4'], 'L0_ffn_gc_w1': _L0_ffn_in['gc_w1'], 'L0_ffn_gc_b1': _L0_ffn_in['gc_b1'], 'L0_ffn_gc_w2': _L0_ffn_in['gc_w2'], 'L0_ffn_gc_b2': _L0_ffn_in['gc_b2'], 'L0_ffn_gc_w3': _L0_ffn_in['gc_w3'], 'L0_ffn_gc_b3': _L0_ffn_in['gc_b3'], 'L0_ffn_adaptive_range': _L0_ffn_in['adaptive_range'], 'L1_attn_w_in': _L1_attn_in['w_in'], 'L1_attn_b_in': _L1_attn_in['b_in'], 'L1_attn_w_dt': _L1_attn_in['w_dt'], 'L1_attn_b_dt': _L1_attn_in['b_dt'], 'L1_attn_A_log': _L1_attn_in['A_log'], 'L1_attn_w_B': _L1_attn_in['w_B'], 'L1_attn_b_B': _L1_attn_in['b_B'], 'L1_attn_w_C': _L1_attn_in['w_C'], 'L1_attn_b_C': _L1_attn_in['b_C'], 'L1_attn_D': _L1_attn_in['D'], 'L1_attn_w_out': _L1_attn_in['w_out'], 'L1_attn_b_out': _L1_attn_in['b_out'], 'L1_attn_gamma': _L1_attn_in['gamma'], 'L1_attn_beta': _L1_attn_in['beta'], 'L1_ffn_ln_gamma': _L1_ffn_in['ln_gamma'], 'L1_ffn_ln_beta': _L1_ffn_in['ln_beta'], 'L1_ffn_fc1_q': _L1_ffn_in['fc1_q'], 'L1_ffn_fc1_scales': _L1_ffn_in['fc1_scales'], 'L1_ffn_fc1_bias': _L1_ffn_in['fc1_bias'], 'L1_ffn_fc2_q': _L1_ffn_in['fc2_q'], 'L1_ffn_fc2_scales': _L1_ffn_in['fc2_scales'], 'L1_ffn_fc2_bias': _L1_ffn_in['fc2_bias']}
    _x0 = _d['L0_attn_u']
    _d['L0_attn_u'] = jax.random.normal(jax.random.fold_in(jax.random.key(seed), 1), (1, 4096, 256), dtype=_x0.dtype)
    del _x0
    return _d

def reference(L0_attn_u, L0_attn_W_in, L0_attn_conv_w, L0_attn_conv_b, L0_attn_dt_bias, L0_attn_A_log, L0_attn_D, L0_attn_norm_w, L0_attn_W_out, L0_ffn_cn_w1, L0_ffn_cn_b1, L0_ffn_cn_w2, L0_ffn_cn_b2, L0_ffn_cn_w3, L0_ffn_cn_b3, L0_ffn_cn_w4, L0_ffn_cn_b4, L0_ffn_gc_w1, L0_ffn_gc_b1, L0_ffn_gc_w2, L0_ffn_gc_b2, L0_ffn_gc_w3, L0_ffn_gc_b3, L0_ffn_adaptive_range, L1_attn_w_in, L1_attn_b_in, L1_attn_w_dt, L1_attn_b_dt, L1_attn_A_log, L1_attn_w_B, L1_attn_b_B, L1_attn_w_C, L1_attn_b_C, L1_attn_D, L1_attn_w_out, L1_attn_b_out, L1_attn_gamma, L1_attn_beta, L1_ffn_ln_gamma, L1_ffn_ln_beta, L1_ffn_fc1_q, L1_ffn_fc1_scales, L1_ffn_fc1_bias, L1_ffn_fc2_q, L1_ffn_fc2_scales, L1_ffn_fc2_bias):

    def _L0_attn_ref(u, W_in, conv_w, conv_b, dt_bias, A_log, D, norm_w, W_out):
        import jax, jax.numpy as jnp
        from jax import lax
        import numpy as np
        D_MODEL = 256
        D_STATE = 64
        D_CONV = 4
        EXPAND = 2
        HEADDIM = 64
        D_INNER = EXPAND * D_MODEL
        NHEADS = D_INNER // HEADDIM
        CHUNK = 64
        CONV_DIM = D_INNER + 2 * D_STATE
        D_IN_PROJ = 2 * D_INNER + 2 * D_STATE + NHEADS
        B_SZ = 4
        SEQLEN = 512
        EPS = 1e-05

        def _silu(x):
            return x * jax.nn.sigmoid(x)

        def _segsum(x):
            T = x.shape[-1]
            xe = jnp.broadcast_to(x[..., None], x.shape + (T,))
            strict_lower = jnp.tril(jnp.ones((T, T), bool), -1)
            xe = jnp.where(strict_lower, xe, 0.0)
            s = jnp.cumsum(xe, axis=-2)
            lower = jnp.tril(jnp.ones((T, T), bool), 0)
            return jnp.where(lower, s, -jnp.inf)
        b, s, _ = u.shape
        A = -jnp.exp(A_log)
        zxbcdt = u @ W_in.T
        z = zxbcdt[..., :D_INNER]
        xBC = zxbcdt[..., D_INNER:D_INNER + CONV_DIM]
        dt = jax.nn.softplus(zxbcdt[..., D_INNER + CONV_DIM:] + dt_bias)
        xc = lax.conv_general_dilated(xBC.transpose(0, 2, 1), conv_w, window_strides=(1,), padding=[(D_CONV - 1, 0)], feature_group_count=CONV_DIM, dimension_numbers=('NCH', 'OIH', 'NCH'))
        xBC = _silu(xc.transpose(0, 2, 1) + conv_b)
        x = xBC[..., :D_INNER].reshape(b, s, NHEADS, HEADDIM)
        Bm = xBC[..., D_INNER:D_INNER + D_STATE]
        Cm = xBC[..., D_INNER + D_STATE:]
        nch = s // CHUNK
        xs = (x * dt[..., None]).reshape(b, nch, CHUNK, NHEADS, HEADDIM)
        Ad = (A * dt).reshape(b, nch, CHUNK, NHEADS)
        Br = Bm.reshape(b, nch, CHUNK, D_STATE)
        Cr = Cm.reshape(b, nch, CHUNK, D_STATE)
        A_ch = Ad.transpose(0, 1, 3, 2)
        A_cum = jnp.cumsum(A_ch, axis=-1)
        L = jnp.exp(_segsum(A_ch))
        Y_diag = jnp.einsum('bcln,bcsn,bchls,bcshp->bclhp', Cr, Br, L, xs)
        decay_states = jnp.exp(A_cum[..., -1:] - A_cum)
        states = jnp.einsum('bchl,bcln,bclhp->bchpn', decay_states, Br, xs)
        init = jnp.zeros((b, 1, NHEADS, HEADDIM, D_STATE), xs.dtype)
        states = jnp.concatenate([init, states], axis=1)
        total_decay = jnp.pad(A_cum[..., -1].transpose(0, 2, 1), ((0, 0), (0, 0), (1, 0)))
        decay_chunk = jnp.exp(_segsum(total_decay))
        new_states = jnp.einsum('bhzc,bchpn->bzhpn', decay_chunk, states)
        states = new_states[:, :-1]
        state_decay_out = jnp.exp(A_cum)
        Y_off = jnp.einsum('bcln,bchpn,bchl->bclhp', Cr, states, state_decay_out)
        y = (Y_diag + Y_off).reshape(b, s, NHEADS, HEADDIM)
        y = y + x * D[:, None]
        y = y.reshape(b, s, D_INNER)
        y = y * _silu(z)
        y = y * lax.rsqrt(jnp.mean(y * y, axis=-1, keepdims=True) + EPS) * norm_w
        return y @ W_out.T

    def _L0_ffn_ref(x, cn_w1, cn_b1, cn_w2, cn_b2, cn_w3, cn_b3, cn_w4, cn_b4, gc_w1, gc_b1, gc_w2, gc_b2, gc_w3, gc_b3, adaptive_range):
        import jax, jax.numpy as jnp
        import numpy as np
        B, S, DIM = (4, 1024, 256)
        BASE_COUPLING = 0.1
        NUM_CYCLES = 3

        def _gelu(x):
            return jax.nn.gelu(x, approximate=False)

        def _coupling_net(h, w1, b1, w2, b2, w3, b3, w4, b4):
            h = _gelu(h @ w1 + b1)
            h = _gelu(h @ w2 + b2)
            h = _gelu(h @ w3 + b3)
            return jax.nn.sigmoid(h @ w4 + b4)

        def _global_net(h, w1, b1, w2, b2, w3, b3):
            h = _gelu(h @ w1 + b1)
            h = _gelu(h @ w2 + b2)
            return jax.nn.sigmoid(h @ w3 + b3)

        def _twist(x):
            o_r, o_i, p_r, p_i = jnp.split(x, 4, axis=-1)
            return jnp.concatenate([p_r, -p_i, -o_r, o_i], axis=-1)
        global_context = x.mean(axis=1, keepdims=True)
        gf = _global_net(global_context, gc_w1, gc_b1, gc_w2, gc_b2, gc_w3, gc_b3)
        out = x
        for _ in range(NUM_CYCLES):
            tf = _coupling_net(out, cn_w1, cn_b1, cn_w2, cn_b2, cn_w3, cn_b3, cn_w4, cn_b4)
            combined = 0.7 * gf + 0.3 * tf
            coupling = BASE_COUPLING + adaptive_range * (combined - 0.5) * 2.0
            out = out + coupling * _twist(out)
        return out

    def _L1_attn_ref(x, w_in, b_in, w_dt, b_dt, A_log, w_B, b_B, w_C, b_C, D, w_out, b_out, gamma, beta):
        import jax, jax.numpy as jnp
        import numpy as np
        HIDDEN = 256
        STATE = 16
        BATCH = 4
        SEQ = 512
        LN_EPS = 1e-05

        def _selective_scan(x_ssm, dt, A, Bm, Cm):
            Bsz, L, D = x_ssm.shape
            N = A.shape[1]

            def step(h, inp):
                xt, dtt, bt, ct = inp
                dA = jnp.exp(A[None] * dtt[..., None])
                dB = dtt[..., None] * bt[:, None, :]
                h = dA * h + dB * xt[..., None]
                y = jnp.sum(h * ct[:, None, :], axis=-1)
                return (h, y)
            h0 = jnp.zeros((Bsz, D, N), x_ssm.dtype)
            xs = (jnp.swapaxes(x_ssm, 0, 1), jnp.swapaxes(dt, 0, 1), jnp.swapaxes(Bm, 0, 1), jnp.swapaxes(Cm, 0, 1))
            _, ys = jax.lax.scan(step, h0, xs)
            return jnp.swapaxes(ys, 0, 1)
        residual = x
        xz = x @ w_in.T + b_in
        x_ssm, z = jnp.split(xz, 2, axis=-1)
        z = jax.nn.silu(z)
        dt = jax.nn.softplus(x_ssm @ w_dt.T + b_dt)
        Bm = x_ssm @ w_B.T + b_B
        Cm = x_ssm @ w_C.T + b_C
        A = -jnp.exp(A_log)
        y = _selective_scan(x_ssm, dt, A, Bm, Cm)
        y = y + D[None, None, :] * x_ssm
        y = y * z
        y = y @ w_out.T + b_out
        pre = y + residual
        mu = jnp.mean(pre, axis=-1, keepdims=True)
        var = jnp.mean(jnp.square(pre - mu), axis=-1, keepdims=True)
        return (pre - mu) * jax.lax.rsqrt(var + LN_EPS) * gamma + beta

    def _L1_ffn_ref(x, ln_gamma, ln_beta, fc1_q, fc1_scales, fc1_bias, fc2_q, fc2_scales, fc2_bias):
        import jax, jax.numpy as jnp
        import numpy as np
        B, S, H, F, G = (8, 512, 256, 1024, 128)
        EPS = 1e-05

        def _dequant(q, scales, g):
            K, N = q.shape
            w = (q.astype(jnp.float32) - 128.0).reshape(K // g, g, N) * scales[:, None, :]
            return w.reshape(K, N)
        residual = x
        mu = jnp.mean(x, axis=-1, keepdims=True)
        var = jnp.mean(jnp.square(x - mu), axis=-1, keepdims=True)
        h = (x - mu) * jax.lax.rsqrt(var + EPS) * ln_gamma + ln_beta
        hf = h.reshape(-1, H)
        w1 = _dequant(fc1_q, fc1_scales, G)
        y = hf @ w1 + fc1_bias
        y = jax.nn.silu(y)
        w2 = _dequant(fc2_q, fc2_scales, G)
        z = y @ w2 + fc2_bias
        return residual + 0.5 * z.reshape(residual.shape)
    x = L0_attn_u
    x = _layernorm(x + _L0_attn_ref(x, L0_attn_W_in, L0_attn_conv_w, L0_attn_conv_b, L0_attn_dt_bias, L0_attn_A_log, L0_attn_D, L0_attn_norm_w, L0_attn_W_out), axis=-1)
    x = _layernorm(x + _L0_ffn_ref(x, L0_ffn_cn_w1, L0_ffn_cn_b1, L0_ffn_cn_w2, L0_ffn_cn_b2, L0_ffn_cn_w3, L0_ffn_cn_b3, L0_ffn_cn_w4, L0_ffn_cn_b4, L0_ffn_gc_w1, L0_ffn_gc_b1, L0_ffn_gc_w2, L0_ffn_gc_b2, L0_ffn_gc_w3, L0_ffn_gc_b3, L0_ffn_adaptive_range), axis=-1)
    x = _layernorm(x + _L1_attn_ref(x, L1_attn_w_in, L1_attn_b_in, L1_attn_w_dt, L1_attn_b_dt, L1_attn_A_log, L1_attn_w_B, L1_attn_b_B, L1_attn_w_C, L1_attn_b_C, L1_attn_D, L1_attn_w_out, L1_attn_b_out, L1_attn_gamma, L1_attn_beta), axis=-1)
    x = _layernorm(x + _L1_ffn_ref(x, L1_ffn_ln_gamma, L1_ffn_ln_beta, L1_ffn_fc1_q, L1_ffn_fc1_scales, L1_ffn_fc1_bias, L1_ffn_fc2_q, L1_ffn_fc2_scales, L1_ffn_fc2_bias), axis=-1)
    return x

_drawn_inputs = setup_inputs


def setup_inputs(seed=0):
    import zlib

    import numpy as np

    out = dict(_drawn_inputs(seed))
    spreads = {'L0_attn_conv_b': (0.0, 0.1),
     'L0_attn_D': (1.0, 0.6),
     'L0_attn_norm_w': (1.0, 0.2),
     'L0_ffn_cn_b1': (0.0, 0.8),
     'L0_ffn_cn_b2': (0.0, 0.8),
     'L0_ffn_cn_b3': (0.0, 0.8),
     'L0_ffn_gc_b1': (0.0, 0.8),
     'L0_ffn_gc_b2': (0.0, 0.8),
     'L1_attn_b_in': (0.0, 0.8),
     'L1_attn_b_dt': (0.0, 0.8),
     'L1_attn_b_B': (0.0, 0.8),
     'L1_attn_b_C': (0.0, 0.8),
     'L1_attn_D': (1.0, 0.6),
     'L1_attn_b_out': (0.0, 0.481),
     'L1_attn_gamma': (1.0, 0.2),
     'L1_attn_beta': (0.0, 0.1),
     'L1_ffn_ln_gamma': (1.0, 0.2),
     'L1_ffn_ln_beta': (0.0, 0.1)}
    factors = {'L0_attn_dt_bias': 8.0,
     'L0_attn_A_log': 8.0,
     'L0_ffn_cn_w1': 8.0,
     'L0_ffn_cn_w2': 8.0,
     'L0_ffn_cn_w3': 8.0,
     'L0_ffn_cn_w4': 8.0,
     'L0_ffn_gc_w1': 8.0,
     'L0_ffn_gc_w2': 8.0,
     'L0_ffn_gc_w3': 8.0,
     'L1_attn_w_in': 8.0,
     'L1_attn_w_dt': 8.0,
     'L1_attn_A_log': 8.0,
     'L1_attn_w_B': 8.0,
     'L1_attn_w_C': 8.0,
     'L1_attn_w_out': 8.0,
     'L1_ffn_fc1_bias': 8.0,
     'L1_ffn_fc2_bias': 8.0}
    for name, (base, spread) in spreads.items():
        noise = np.random.default_rng([zlib.crc32(name.encode()), seed]).standard_normal(out[name].shape)
        drawn = base * np.exp(spread * noise) if base else spread * noise
        out[name] = jnp.asarray(drawn.astype(out[name].dtype))
    for name, factor in factors.items():
        out[name] = (out[name] * factor).astype(out[name].dtype)
    return out
```

```python
import concourse.bass as bass
from concourse import mybir
from contextlib import ExitStack

F32 = mybir.dt.float32
BF16 = mybir.dt.bfloat16
I32 = mybir.dt.int32
ALU = mybir.AluOpType
ACT = mybir.ActivationFunctionType

P = 128
T, DM = 4096, 256
TB = 512
NB = T // TB
CH = 128
NC = TB // CH
KD = DM // P
DI, DS, NH, HD, TAPS = 512, 64, 8, 64, 4
NX = (DI + 2 * DS) // P
DIN = 2 * DI + 2 * DS + NH
NS = 16
FF = 1024
KF = FF // P
GQ = 128
EPS = 1e-5
COLUMNS = [("cn_b1", KD), ("cn_b2", 1), ("cn_b3", 1), ("cn_w4", 1), ("gc_b1", 1), ("gc_b2", 1), ("gc_w3", 1),
           ("conv_b", NX), ("conv_w", NX * TAPS), ("norm_w", DI // P),
           ("c_b_in", 2 * KD), ("c_b_dt", KD), ("c_b_bc", 1), ("c_D", KD), ("c_A_log", KD * NS),
           ("f_gamma", KD), ("f_beta", KD), ("f_b1", KF)]
EVERYWHERE = [("cn_b4", 1), ("gc_b3", 1), ("adaptive_range", 1), ("dt_bias", NH), ("A_log", NH), ("D", NH),
              ("c_gamma", DM), ("c_beta", DM), ("c_b_out", DM), ("f_b2", DM)]
PE, SA, VE, PO, SP = "pe", "act", "dve", "pool", "sp"
DMAS = 16


class Block:

    def __init__(self, j, off):
        self.j, self.off = j, off

    def token(self):
        return self.off * TB if self.j is None else self.j * (2 * TB) + self.off * TB


class Stage:

    def __init__(self, top, name, build):
        self.name, self.sem, self.count, self.place = name, {}, {}, {}
        self.steps = [[], []]
        for parity in (0, 1):
            self.building = self.steps[parity]
            build(self, parity)
        for step in self.steps[0]:
            engine, label, n = step[0], step[1], step[4]
            if n:
                self.sem[label] = [top.sem(f"{name}_{label}{q}") for q in (0, 1)]
                self.place[label] = (None, n)
            else:
                if engine not in self.sem:
                    self.sem[engine] = top.sem(f"{name}_{engine}")
                self.count[engine] = self.count.get(engine, 0) + 1
                self.place[label] = (engine, self.count[engine])
        top.stages[name] = self

    def do(self, engine, label, work, *after, dmas=0, alone=False):
        self.building.append((engine, label, work, after, dmas, alone))


class Program:
    def __init__(self, nc, ctx):
        self.nc, self.ctx, self.stages = nc, ctx, {}
        self.apart = self.sem("apart")

    def sem(self, name):
        return self.ctx.enter_context(self.nc.semaphore(name))

    def level(self, stage, label, block):
        engine, at = stage.place[label]
        if engine is None:
            q = block.off % 2
            return stage.sem[label][q], DMAS * at, ((block.off - q) // 2 + 2) * DMAS * at
        n = stage.count[engine]
        return stage.sem[engine], 2 * n, (block.off + 2) * n + at

    def emit(self, me, eng, work, j, seen):
        for stage, block, step in work:
            engine, label, fn, after, n, alone = step
            waited = False
            if engine != me:
                continue
            for name in after:
                name, _, lag = name.partition("@")
                of, _, what = name.rpartition(".")
                of = self.stages[of] if of else stage
                then = Block(j, block.off + int(lag or 0))
                sem, a, c = self.level(of, what, then)
                if seen.get(sem.name, 0) >= c:
                    continue
                seen[sem.name] = c
                eng.wait_ge(sem, c if j is None else j * a + c)
                waited = j is not None
                if waited and me == SP:
                    eng.sem_inc(self.apart, 1)
            if waited and (me == PO or alone):
                eng.sem_inc(self.apart, 1)
            if n:
                done = fn(eng, block)
                done = done if isinstance(done, list) else [done]
                assert len(done) == n
                for d in done:
                    d.then_inc(stage.sem[label][block.off % 2], DMAS)
            else:
                fn(eng, block).then_inc(stage.sem[engine], 1)

    def body(self, plan, j, t):
        work = []
        for name, lag, lo, hi in plan:
            stage = self.stages[name]
            if j is None and not 0 <= t - lag < NB:
                continue
            steps = stage.steps[(t - lag) % 2]
            for n, step in enumerate(steps):
                work.append((lo + (hi - lo) * n / len(steps), stage, Block(j, t - lag), step))
        work.sort(key=lambda w: w[0])
        return [w[1:] for w in work]

    def credit(self, me, eng, names):
        for name in names:
            stage = self.stages[name]
            for label, (engine, n) in stage.place.items():
                if engine is None and me == SP:
                    for q in (0, 1):
                        eng.sem_inc(stage.sem[label][q], DMAS * n)
            if me in stage.count:
                eng.sem_inc(stage.sem[me], 2 * stage.count[me])

    def run(self, me, eng, plan):
        lag = max(p[1] for p in plan)
        first = lag + lag % 2 if lag > 1 else 2
        self.credit(me, eng, [p[0] for p in plan])
        seen = {}
        for t in range(first):
            self.emit(me, eng, self.body(plan, None, t), None, seen)
        with eng.Fori(0, (NB - first) // 2) as j:
            seen = {}
            for t in (first, first + 1):
                self.emit(me, eng, self.body(plan, j, t), j, seen)
        seen = {}
        for t in range(NB, NB + lag):
            self.emit(me, eng, self.body(plan, None, t), None, seen)


def build(nc, d, out):
    with ExitStack() as ctx:
        top = Program(nc, ctx)

        def sb(name, shape, dt=F32, within=ctx):
            return within.enter_context(nc.sbuf_tensor(name, shape, dt))

        def psum(within, n):
            return [within.enter_context(nc.psum_tensor(f"{n}{i}", [P, 512], F32)) for i in range(8)]

        ident, upper, below, ones = (sb(n, [P, P]) for n in ("ident", "upper", "below", "ones"))
        mhalf, sign = sb("mhalf", [P, NC]), sb("sign", [P, 1])
        x1T = sb("x1T", [P, KD, T])
        x1sum = sb("x1sum", [P, KD, T // CH])
        cn_w1, cn_w2 = sb("cn_w1", [P, KD, DM]), sb("cn_w2", [P, KD, P])
        cn_w3 = sb("cn_w3", [P, 64])
        gc_w1, gc_w2 = sb("gc_w1", [P, KD, P]), sb("gc_w2", [P, 64])
        columns, everywhere = sb("columns", [P, sum(n for _, n in COLUMNS)]), sb("everywhere", [P, sum(n for _, n in EVERYWHERE)])
        vec_at = {}
        for held, names in ((columns, COLUMNS), (everywhere, EVERYWHERE)):
            at = 0
            for name, n in names:
                vec_at[name] = held[:, at:at + n]
                at += n
        cn_b1, cn_b2, cn_b3, cn_b4 = (vec_at[n] for n in ("cn_b1", "cn_b2", "cn_b3", "cn_b4"))
        gc_b1, gc_b2, gc_b3, rng = (vec_at[n] for n in ("gc_b1", "gc_b2", "gc_b3", "adaptive_range"))
        cw4 = sb("cw4", [64, P])
        gw3 = sb("gw3", [64, P])
        hb4, hg3 = sb("hb4", [P, 1]), sb("hg3", [P, 1])
        slope, shift = sb("slope", [P, 1]), sb("shift", [P, 1])
        ready = top.sem("ready")

        def rows(v):
            return v.rearrange("(k p) n -> p k n", p=P)

        c_sem, w_sem = top.sem("const"), top.sem("weights")
        with nc.Block() as block:
            early = [(cn_w1, rows(d["cn_w1"])), (cn_w2, rows(d["cn_w2"])),
                     (cn_w3, d["cn_w3"]), (gc_w1, rows(d["gc_w1"])), (gc_w2, d["gc_w2"]),
                     (columns, d["columns"]),
                     (everywhere, d["everywhere"].rearrange("(a n) -> a n", a=1).to_broadcast([P, everywhere.shape[1]]))]

            @block.sync
            def _(e):
                for dst, src in early:
                    e.dma_start(dst[tuple(slice(None) for _ in dst.shape)], src).then_inc(w_sem, DMAS)
                e.wait_ge(w_sem, DMAS * len(early))

            @block.gpsimd
            def _(e):
                e.memset(ident[:, :], 0.0).then_inc(c_sem, 1)
                e.memset(upper[:, :], 1.0).then_inc(c_sem, 1)
                e.memset(below[:, :], 1.0).then_inc(c_sem, 1)
                e.memset(ones[:, :], 1.0).then_inc(c_sem, 1)
                e.memset(mhalf[:, :], -0.5).then_inc(c_sem, 1)
                e.memset(sign[:, :], 1.0).then_inc(c_sem, 1)
                e.wait_ge(c_sem, 6)
                e.affine_select(out=ident[:, :], in_=ident[:, :], compare_op=ALU.not_equal, fill=1.0,
                                base=0, pattern=[[-1, P]], channel_multiplier=1)
                e.affine_select(out=upper[:, :], in_=upper[:, :], compare_op=ALU.is_ge, fill=0.0,
                                base=0, pattern=[[1, P]], channel_multiplier=-1)
                e.affine_select(out=below[:, :], in_=below[:, :], compare_op=ALU.is_ge, fill=0.0,
                                base=-1, pattern=[[-1, P]], channel_multiplier=1)
                e.affine_select(out=sign[:, :], in_=sign[:, :], compare_op=ALU.is_ge, fill=-1.0,
                                base=P // 2 - 1, pattern=[[0, 1]], channel_multiplier=-1).then_inc(c_sem, 1)

            @block.vector
            def _(e):
                e.wait_ge(w_sem, DMAS * len(early))
                e.tensor_copy(cw4[:, :], vec_at["cn_w4"][0:64, :].to_broadcast([64, P]))
                e.tensor_copy(gw3[:, :], vec_at["gc_w3"][0:64, :].to_broadcast([64, P]))
                e.tensor_scalar(hb4[:, :], cn_b4, 0.5, None, ALU.mult)
                e.tensor_scalar(hg3[:, :], gc_b3, 0.5, None, ALU.mult)

        def layer_norm(s, tag, src, dst, st, mv, ve, rs, src_ready, dst_free, on=VE):
            for c in range(NC):
                s.do(VE, f"{tag}_st{c}", lambda e, b, c=c: e.bn_stats(st[:, c, :], src(c)), *src_ready(c),
                     f"{tag}_ve@-1")
                s.do(VE, f"{tag}_mv{c}", lambda e, b, c=c: e.bn_aggr(mv[:, c, :], st[:, c, :]), alone=True, *[f"{tag}_st{c}",
                     f"{tag}_n{NC - 1}@-1"])
            s.do(VE, f"{tag}_ve", lambda e, b: e.tensor_scalar(ve[:, :], mv[:, :, 1], EPS, None, ALU.add),
                 f"{tag}_mv{NC - 1}", f"{tag}_rs@-1")
            s.do(PO, f"{tag}_rs", lambda e, b: e.tensor_tensor(rs[:, :], ve[:, :], mhalf[:, :], ALU.pow),
                 f"{tag}_ve", f"{tag}_n{NC - 1}@-1")
            for c in range(NC):
                s.do(VE, f"{tag}_n{c}",
                     lambda e, b, c=c: e.tensor_scalar(dst(c), src(c), mv[:, c, 0:1], rs[:, c:c + 1],
                                                       ALU.subtract, ALU.mult),
                     f"{tag}_rs", *dst_free)

        with ExitStack() as pa:
            W_in = sb("W_in", [P, KD, DIN], within=pa)
            W_out, W_raw = sb("W_out", [P, DI // P, DM], within=pa), sb("W_raw", [P, DI // P, DM], within=pa)
            cw, cb = vec_at["conv_w"].rearrange("p (m j) -> p m j", m=NX), vec_at["conv_b"]
            nw, dtb1, D1 = vec_at["norm_w"], vec_at["dt_bias"], vec_at["D"]
            dtb, negA, Dsk = (sb(n, [P, NC, NH], within=pa) for n in ("dtb", "negA", "Dsk"))
            expA = sb("expA", [P, NH], within=pa)
            uT = [sb(f"uT{q}", [P, KD, TB], within=pa) for q in (0, 1)]
            u = [sb(f"u{q}", [P, NC, DM], within=pa) for q in (0, 1)]
            raw = [sb(f"raw{q}", [P, NX, TB + TAPS - 1], within=pa) for q in (0, 1)]
            con = sb("con", [P, NX, TB], within=pa)
            xf = [sb(f"xf{q}", [P, NX, TB], within=pa) for q in (0, 1)]
            Cf = [sb(f"Cf{q}", [DS, TB], within=pa) for q in (0, 1)]
            zr = sb("zr", [P, NC, DI], within=pa)
            zs = [sb(f"zs{q}", [P, NC, DI], within=pa) for q in (0, 1)]
            sp_x, sp_a, sp_y, sp_l, sp_d, sp_r = (sb(n, [P, NC * NH], within=pa) for n in
                                                  ("sp_x", "sp_a", "sp_y", "sp_l", "sp_d", "sp_r"))
            dt = [sb(f"dt{q}", [P, NC, NH], within=pa) for q in (0, 1)]
            dA = [sb(f"dA{q}", [P, NC, NH], within=pa) for q in (0, 1)]
            dec = sb("dec", [P, 3, NC, NH], within=pa)
            dAU, L, M = (sb(n, [P, NH, CH], within=pa) for n in ("dAU", "L", "M"))
            xt, xs, xd, xD = (sb(n, [P, DI], within=pa) for n in ("xt", "xs", "xd", "xD"))
            Bt, CB = sb("Bt", [P, DS], within=pa), sb("CB", [P, CH], within=pa)
            S, Sd = sb("S", [DS, DI], within=pa), sb("Sd", [DS, DI], within=pa)
            yo, y1, y2, sq = (sb(n, [P, DI], within=pa) for n in ("yo", "y1", "y2", "sq"))
            yT = sb("yT", [P, DI // P, CH], within=pa)
            ssq, rms = sb("ssq", [P, 1], within=pa), sb("rms", [P, 1], within=pa)
            ssn = sb("ssn", [P, 1], within=pa)
            r1 = sb("r1", [P, DM], within=pa)
            x1 = sb("x1", [P, DM], within=pa)
            st1, mv1, ve1, rs1 = sb("st1", [P, 6], within=pa), sb("mv1", [P, 2], within=pa), sb("ve1", [P, 1], within=pa), sb("rs1", [P, 1], within=pa)
            pb = psum(pa, "pa")

            wa = [(W_in, rows(d["W_inT"])), (W_raw, rows(d["W_outT"]))]
            wa_sem, wa_act, wa_dve = top.sem("wa_sem"), top.sem("wa_act"), top.sem("wa_dve")
            with nc.Block() as block:
                @block.sync
                def _(e):
                    for dst, src in wa:
                        e.dma_start(dst[tuple(slice(None) for _ in dst.shape)], src).then_inc(wa_sem, DMAS)
                    e.wait_ge(wa_sem, DMAS * len(wa))

                @block.scalar
                def _(e):
                    e.preload_act_table_set("natural_log_exp_and_others")
                    e.wait_ge(wa_sem, DMAS * len(wa))
                    e.activation(expA[:, :], vec_at["A_log"], ACT.Exp).then_inc(wa_act, 1)

                @block.vector
                def _(e):
                    e.memset(S[:, :], 0.0)
                    e.memset(raw[1][:, :, TB:TB + TAPS - 1], 0.0)
                    e.wait_ge(wa_sem, DMAS * len(wa))
                    for k in range(DI // P):
                        e.tensor_scalar(W_out[:, k, :], W_raw[:, k, :], nw[:, k:k + 1], None, ALU.mult)
                    for c in range(NC):
                        e.tensor_copy(dtb[:, c, :], dtb1)
                        e.tensor_copy(Dsk[:, c, :], D1)
                    e.wait_ge(wa_act, 1)
                    for c in range(NC):
                        e.tensor_scalar(negA[:, c, :], expA[:, :], -1.0, None, ALU.mult)

            def loads(s, q):
                s.do(SP, "uT", lambda e, b: e.dma_start(
                    uT[q][:, :, :], d["uT"].rearrange("(k p) t -> p k t", p=P)[:, :, bass.ds(b.token(), TB)]),
                    "proj.dt@-2", f"proj.z{NC - 1}@-2", dmas=1)
                s.do(SP, "u", lambda e, b: e.dma_start(
                    u[q][:, :, :], d["u"].rearrange("(n p) f -> p n f", p=P)[:, bass.ds(b.off * NC if b.j is None else b.j * (2 * NC) + b.off * NC, NC), :]),
                    f"ssd.r{NC - 1}@-2", dmas=1)

            def proj(s, q):
                s.do(PO, "halo", lambda e, b: e.tensor_copy(raw[q][:, :, 0:TAPS - 1], raw[1 - q][:, :, TB:TB + TAPS - 1]),
                     f"ev{NX - 1}@-1", f"t{NX - 1}_0@-2")
                for m in range(NX):
                    def mm(e, b, m=m):
                        for k in range(KD):
                            i = e.matmul(pb[m % 2][:, :], W_in[:, k, DI + m * P:DI + (m + 1) * P], uT[q][:, k, :],
                                         start=(k == 0), stop=(k == KD - 1))
                        return i
                    free = [f"c{m - 2}"] if m > 1 else ["spx@-1" if m == (NX + NC) % 2 else f"zc{NC - 1}@-1"]
                    s.do(PE, f"x{m}", mm, "loads.uT", *free)
                    s.do(SA, f"ev{m}", lambda e, b, m=m: e.activation(raw[q][:, m, TAPS - 1:TB + TAPS - 1], pb[m % 2][:, :], ACT.Copy),
                         f"x{m}", f"t{m}_0@-2", "halo@-1")
                    s.do(SA, f"c{m}", lambda e, b, m=m: e.activation(con[:, m, :], pb[m % 2][:, :], ACT.Identity, bias=cb[:, m:m + 1],
                                                                     scale=cw[:, m, TAPS - 1:TAPS]), f"x{m}", f"act.x{m}@-1")
                    for j in range(TAPS - 2, -1, -1):
                        s.do(VE, f"t{m}_{j}", lambda e, b, m=m, j=j: e.scalar_tensor_tensor(
                            con[:, m, :], raw[q][:, m, j:j + TB], cw[:, m, j:j + 1], con[:, m, :], ALU.mult, ALU.add),
                            f"c{m}", f"t{m}_{j + 1}" if j < TAPS - 2 else f"ev{m}", "halo")
                for c in range(NC):
                    def mm(e, b, c=c):
                        for k in range(KD):
                            i = e.matmul(pb[(NX + c) % 2][:, :], uT[q][:, k, c * CH:(c + 1) * CH], W_in[:, k, 0:DI],
                                         start=(k == 0), stop=(k == KD - 1))
                        return i
                    s.do(PE, f"z{c}", mm, f"zc{c - 2}" if c > 1 else f"c{NX - 2 + c}")
                    s.do(SA, f"zc{c}", lambda e, b, c=c: e.activation(zr[:, c, :], pb[(NX + c) % 2][:, :], ACT.Copy),
                         f"z{c}", f"act.z{c}@-1")
                def dt_mm(e, b):
                    for c in range(NC):
                        for k in range(KD):
                            i = e.matmul(pb[(NX + NC) % 2][:, c * NH:(c + 1) * NH], uT[q][:, k, c * CH:(c + 1) * CH],
                                         W_in[:, k, DIN - NH:DIN], start=(k == 0), stop=(k == KD - 1))
                    return i
                s.do(PE, "dt", dt_mm, f"zc{NC - 2}")
                s.do(VE, "spx", lambda e, b: e.tensor_tensor(sp_x[:, :], pb[(NX + NC) % 2][:, 0:NC * NH],
                                                             dtb[:, :, :].rearrange("p c h -> p (c h)"), ALU.add), "dt", "spa@-1", "spr@-1")
                s.do(SA, "spa", lambda e, b: e.activation(sp_a[:, :], sp_x[:, :], ACT.Abs), "spx", "spy@-1")
                s.do(SA, "spy", lambda e, b: e.activation(sp_y[:, :], sp_a[:, :], ACT.Exp, scale=-1.0), "spa", "spe@-1")
                s.do(SA, "spl", lambda e, b: e.activation(sp_l[:, :], sp_y[:, :], ACT.Ln, bias=1.0), "spy", "sps@-1")
                s.do(VE, "spd", lambda e, b: e.tensor_scalar(sp_d[:, :], sp_y[:, :], 1.0, -1.0, ALU.add, ALU.add), "spy", "sps@-1")
                s.do(VE, "spr", lambda e, b: e.tensor_scalar(sp_r[:, :], sp_x[:, :], 0.0, None, ALU.max), "spx", "spt@-1")
                s.do(VE, "spe", lambda e, b: e.tensor_tensor(sp_d[:, :], sp_y[:, :], sp_d[:, :], ALU.subtract), "spd")
                s.do(VE, "sps", lambda e, b: e.tensor_tensor(sp_d[:, :], sp_l[:, :], sp_d[:, :], ALU.add), "spl", "spe")
                s.do(VE, "spt", lambda e, b: e.tensor_tensor(dt[q][:, :, :].rearrange("p c h -> p (c h)"), sp_r[:, :],
                                                             sp_d[:, :], ALU.add), "sps", "spr", f"ssd.xs{NC - 1}@-2", "spA@-2")
                s.do(VE, "spA", lambda e, b: e.tensor_tensor(dA[q][:, :, :], dt[q][:, :, :], negA[:, :, :], ALU.mult),
                     "spt", f"ssd.au{NC - 1}@-2", "ssd.sums@-2")

            def act(s, q):
                for m in range(NX - 1, -1, -1):
                    s.do(SA, f"x{m}", lambda e, b, m=m: e.activation(xf[q][:, m, :], con[:, m, :], ACT.Silu),
                         f"proj.t{m}_0", f"ssd.xt{NC - 1}@-2", f"ssd.bt{NC - 1}@-2", f"ssd.cb{NC - 1}@-2", "C@-2")
                    if m == NX - 1:
                        s.do(SP, "C", lambda e, b: e.dma_start(Cf[q][:, :], xf[q][DS:2 * DS, NX - 1, :]), f"x{NX - 1}",
                             f"ssd.off{NC - 1}@-2", f"ssd.cb{NC - 1}@-2", dmas=1)
                for c in range(NC):
                    s.do(SA, f"z{c}", lambda e, b, c=c: e.activation(zs[q][:, c, :], zr[:, c, :], ACT.Silu),
                         f"proj.zc{c}", f"ssd.gate{c}@-2")

            def ssd(s, q):
                def heads(x):
                    return x.rearrange("p (h f) -> p h f", h=NH)

                def by_head(v, n, parts=P):
                    return v.rearrange("p (h o) -> p h o", o=1).to_broadcast([parts, NH, n])

                def sums(e, b):
                    v = dA[q][:, :, :].rearrange("p c h -> p (c h)")
                    for n, w in enumerate((below, upper, ones)):
                        i = e.matmul(pb[3][:, 256 + n * NC * NH:256 + (n + 1) * NC * NH], w[:, :], v, start=True, stop=True)
                    return i
                s.do(PE, "sums", sums, "proj.spA", f"o{KD - 1}_{NC - 1}@-1")
                s.do(SA, "dec", lambda e, b: e.activation(dec[:, :, :, :].rearrange("p a c h -> p (a c h)"),
                                                          pb[3][:, 256:256 + 3 * NC * NH], ACT.Exp),
                     "sums", f"Sd{NC - 1}@-1", f"yo{NC - 1}@-1", f"xd{NC - 1}@-1")
                prev = lambda n, c: f"{n}{c - 1}" if c else f"{n}{NC - 1}@-1"
                for c in range(NC):
                    cs = slice(c * CH, (c + 1) * CH)
                    def tx(e, b, cs=cs):
                        for m in range(NX - 1):
                            i = e.transpose(pb[7][:, m * P:(m + 1) * P], xf[q][:, m, cs], ident[:, :])
                        return i
                    s.do(PE, f"xt{c}", tx, "act.x0", prev("r", c))
                    s.do(PE, f"bt{c}", lambda e, b, cs=cs: e.transpose(pb[2][:, 0:P], xf[q][:, NX - 1, cs], ident[:, :]),
                         f"act.x{NX - 1}", prev("cbm", c))
                    s.do(PE, f"cb{c}", lambda e, b, cs=cs: e.matmul(pb[2][:, P:2 * P], xf[q][0:DS, NX - 1, cs], Cf[q][:, cs],
                                                                    start=True, stop=True), "act.C", prev("cbm", c))
                    s.do(SA, f"btc{c}", lambda e, b: e.activation(Bt[:, :], pb[2][:, 0:DS], ACT.Copy), f"cb{c}", prev("new", c))
                    s.do(VE, f"cbm{c}", lambda e, b: e.tensor_tensor(CB[:, :], pb[2][:, P:2 * P], upper[:, :], ALU.mult),
                         f"btc{c}", prev("M", c))
                    s.do(SA, f"xtc{c}", lambda e, b: e.activation(xt[:, :], pb[7][:, :], ACT.Copy), f"xt{c}", prev("xs", c), prev("xD", c))
                    s.do(PO, f"au{c}", lambda e, b, c=c: e.tensor_tensor(
                        dAU[:, :, :], by_head(dA[q][:, c, :], CH),
                        upper[:, :].rearrange("p (o l) -> p o l", o=1).to_broadcast([P, NH, CH]), ALU.mult),
                        "proj.spA", prev("seg1_", c))
                    s.do(PO, f"xs{c}", lambda e, b, c=c: e.tensor_tensor(heads(xs[:, :]), heads(xt[:, :]), by_head(dt[q][:, c, :], HD), ALU.mult),
                         f"xtc{c}", prev("diag", c), prev("xd", c))
                    s.do(PO, f"xd{c}", lambda e, b, c=c: e.tensor_tensor(heads(xd[:, :]), heads(xs[:, :]), by_head(dec[:, 0, c, :], HD), ALU.mult),
                         f"xs{c}", "dec", prev("new", c))
                    s.do(PO, f"xD{c}", lambda e, b, c=c: e.tensor_tensor(heads(xD[:, :]), heads(xt[:, :]), by_head(Dsk[:, c, :], HD), ALU.mult),
                         f"xtc{c}", prev("y1_", c))
                    for g in (0, 1):
                        s.do(PE, f"seg{g}_{c}", lambda e, b, g=g: e.matmul(
                            pb[4 + g][:, :], below[:, :], dAU[:, 4 * g:4 * g + 4, :].rearrange("p h l -> p (h l)"), start=True, stop=True),
                            f"au{c}", prev(f"L{g}_", c))
                        s.do(SA, f"L{g}_{c}", lambda e, b, g=g: e.activation(
                            L[:, 4 * g:4 * g + 4, :].rearrange("p h l -> p (h l)"), pb[4 + g][:, :], ACT.Exp),
                            f"seg{g}_{c}", prev("M", c))
                    s.do(VE, f"M{c}", lambda e, b: e.tensor_tensor(
                        M[:, :, :], L[:, :, :], CB[:, :].rearrange("p (o l) -> p o l", o=1).to_broadcast([P, NH, CH]), ALU.mult),
                        f"L1_{c}", f"cbm{c}", prev("diag", c))
                    s.do(PE, f"off{c}", lambda e, b, cs=cs: e.matmul(pb[6][:, :], Cf[q][:, cs], S[:, :], start=True, stop=True),
                         "act.C", prev("S", c), prev("y1a", c))
                    s.do(VE, f"yo{c}", lambda e, b, c=c: e.tensor_tensor(heads(yo[:, :]), heads(pb[6][:, :]), by_head(dec[:, 1, c, :], HD), ALU.mult),
                         f"off{c}", "dec", prev("y1_", c))

                    def diag(e, b):
                        for h in range(NH):
                            i = e.matmul(pb[6][:, h * HD:(h + 1) * HD], M[:, h, :], xs[:, h * HD:(h + 1) * HD], start=True, stop=True)
                        return i
                    s.do(PE, f"diag{c}", diag, f"M{c}", f"xs{c}", f"yo{c}")
                    s.do(PE, f"new{c}", lambda e, b: e.matmul(pb[7][0:DS, :], Bt[:, :], xd[:, :], start=True, stop=True),
                         f"btc{c}", f"xd{c}", f"xtc{c}")
                    s.do(VE, f"Sd{c}", lambda e, b, c=c: e.tensor_tensor(heads(Sd[:, :]), heads(S[:, :]), by_head(dec[0:DS, 2, c, :], HD, DS), ALU.mult),
                         "dec", prev("S", c))
                    s.do(VE, f"S{c}", lambda e, b: e.tensor_tensor(S[:, :], Sd[:, :], pb[7][0:DS, :], ALU.add), f"Sd{c}", f"new{c}", f"off{c}")
                    s.do(PO, f"y1_{c}", lambda e, b: e.tensor_tensor(y1[:, :], yo[:, :], xD[:, :], ALU.add), f"yo{c}", f"xD{c}", prev("y1a", c))
                    s.do(VE, f"y1a{c}", lambda e, b: e.tensor_tensor(y2[:, :], y1[:, :], pb[6][:, :], ALU.add), f"y1_{c}", f"diag{c}", prev("tyT", c), prev("gate", c))
                    s.do(VE, f"gate{c}", lambda e, b, c=c: e.tensor_tensor(y2[:, :], y2[:, :], zs[q][:, c, :], ALU.mult), f"y1a{c}", f"act.z{c}")
                    s.do(SA, f"sq{c}", lambda e, b: e.activation(sq[:, :], y2[:, :], ACT.Square, accum_out=ssq[:, :]), f"gate{c}", prev("ssn", c))

                    def ty(e, b):
                        for m in range(DI // P):
                            i = e.transpose(pb[7][:, m * P:(m + 1) * P], y2[:, m * P:(m + 1) * P], ident[:, :])
                        return i
                    s.do(PE, f"tyT{c}", ty, f"gate{c}", f"S{c}")
                    s.do(SA, f"yT{c}", lambda e, b: e.activation(yT[:, :, :].rearrange("p k l -> p (k l)"), pb[7][:, :], ACT.Copy), f"tyT{c}", prev("op", c))
                    s.do(VE, f"ssn{c}", lambda e, b: e.tensor_scalar(ssn[:, :], ssq[:, :], 1.0 / DI, EPS, ALU.mult, ALU.add), f"sq{c}", prev("rms", c))
                    s.do(PO, f"rms{c}", lambda e, b: e.tensor_tensor(rms[:, :], ssn[:, :], mhalf[:, 0:1], ALU.pow), f"ssn{c}", prev("r", c))

                    def op(e, b):
                        for k in range(DI // P):
                            i = e.matmul(pb[7][:, 0:DM], yT[:, k, :], W_out[:, k, :], start=(k == 0), stop=(k == DI // P - 1))
                        return i
                    s.do(PE, f"op{c}", op, f"yT{c}")
                    s.do(VE, f"r{c}", lambda e, b, c=c: e.scalar_tensor_tensor(r1[:, :], pb[7][:, 0:DM], rms[:, 0:1], u[q][:, c, :], ALU.mult, ALU.add),
                         f"op{c}", f"rms{c}", "loads.u", prev("n", c))
                    s.do(VE, f"st{c}", lambda e, b: e.bn_stats(st1[:, :], r1[:, :]), f"r{c}", prev("mv", c))
                    s.do(VE, f"mv{c}", lambda e, b: e.bn_aggr(mv1[:, :], st1[:, :]), f"st{c}", prev("n", c), alone=True)
                    s.do(VE, f"ve{c}", lambda e, b: e.tensor_scalar(ve1[:, :], mv1[:, 1:2], EPS, None, ALU.add), f"mv{c}", prev("rs", c))
                    s.do(PO, f"rs{c}", lambda e, b: e.tensor_tensor(rs1[:, :], ve1[:, :], mhalf[:, 0:1], ALU.pow), f"ve{c}", prev("n", c))
                    s.do(VE, f"n{c}", lambda e, b: e.tensor_scalar(x1[:, :], r1[:, :], mv1[:, 0:1], rs1[:, 0:1], ALU.subtract, ALU.mult),
                         f"rs{c}", prev("tx", c))

                    def tx1(e, b):
                        for k in range(KD):
                            i = e.transpose(pb[3][:, k * P:(k + 1) * P], x1[:, k * P:(k + 1) * P], ident[:, :])
                        return i
                    s.do(PE, f"tx{c}", tx1, f"n{c}", prev("o1_", c), "dec")
                    for k in range(KD):
                        s.do(SA, f"o{k}_{c}", lambda e, b, k=k, c=c: e.activation(
                            x1T[:, k, bass.ds(b.token() + c * CH, CH)], pb[3][:, k * P:(k + 1) * P], ACT.Copy), f"tx{c}")

            Stage(top, "loads", loads)
            Stage(top, "proj", proj)
            Stage(top, "act", act)
            Stage(top, "ssd", ssd)
            plan = [("loads", 0, 0, 0.1), ("proj", 1, 0, 0.8), ("ssd", 2, 0, 0.8), ("act", 1, 0.8, 1)]
            with nc.Block() as block:
                block.sync(lambda e: top.run(SP, e, plan))
                block.tensor(lambda e: top.run(PE, e, plan))
                block.vector(lambda e: top.run(VE, e, plan))
                block.gpsimd(lambda e: top.run(PO, e, plan))
                block.scalar(lambda e: top.run(SA, e, plan))

        with ExitStack() as pg:
            mean, g1, g2 = sb("mean", [P, KD], within=pg), sb("g1", [P, 1], within=pg), sb("g2", [64, 1], within=pg)
            gt, k0 = sb("gt", [P, 1], within=pg), sb("k0", [P, 1], within=pg)
            pb = psum(pg, "pg")
            gv, gp, ga = top.sem("gv"), top.sem("gp"), top.sem("ga")
            with nc.Block() as block:
                @block.vector
                def _(e):
                    for k in range(KD):
                        e.reduce_sum(mean[:, k:k + 1], x1T[:, k, :], mybir.AxisListType.X).then_inc(gv, 1)
                    e.tensor_scalar(slope[:, :], rng, 0.3, None, ALU.mult).then_inc(gv, 1)
                    e.wait_ge(gv, 3)
                    e.tensor_tensor(slope[:, :], slope[:, :], sign[:, :], ALU.mult).then_inc(gv, 1)
                    e.wait_ge(ga, 3)
                    e.tensor_scalar(k0[:, :], gt[:, :], 0.7, None, ALU.mult).then_inc(gv, 1)
                    e.wait_ge(gv, 5)
                    e.tensor_scalar(shift[:, :], k0[:, :], rng[:, 0:1], 0.1, ALU.mult, ALU.add).then_inc(gv, 1)
                    e.wait_ge(gv, 6)
                    e.tensor_tensor(k0[:, :], shift[:, :], sign[:, :], ALU.mult).then_inc(gv, 1)
                    e.wait_ge(gv, 7)
                    e.tensor_copy(shift[:, :], k0[:, :])

                @block.tensor
                def _(e):
                    e.wait_ge(gv, 2)
                    for k in range(KD):
                        i = e.matmul(pb[0][:, 0:1], gc_w1[:, k, :], mean[:, k:k + 1], start=(k == 0), stop=(k == KD - 1))
                    i.then_inc(gp, 1)
                    e.wait_ge(ga, 1)
                    e.matmul(pb[1][0:64, 0:1], gc_w2[:, :], g1[:, :], start=True, stop=True).then_inc(gp, 1)
                    e.wait_ge(ga, 2)
                    e.matmul(pb[2][:, 0:1], gw3[:, :], g2[:, :], start=True, stop=True).then_inc(gp, 1)

                @block.scalar
                def _(e):
                    e.wait_ge(gp, 1)
                    e.activation(g1[:, :], pb[0][:, 0:1], ACT.Gelu, bias=gc_b1[:, 0:1], scale=1.0 / T).then_inc(ga, 1)
                    e.wait_ge(gp, 2)
                    e.activation(g2[:, :], pb[1][0:64, 0:1], ACT.Gelu, bias=gc_b2[0:64, :]).then_inc(ga, 1)
                    e.wait_ge(gp, 3)
                    e.activation(gt[:, :], pb[2][:, 0:1], ACT.Tanh, bias=hg3[:, 0:1], scale=0.5).then_inc(ga, 1)

        with ExitStack() as pc:
            def t(name, shape, dt=F32):
                return sb(name, shape, dt, within=pc)

            w_xz, w_dt, w_bc, w_o = t("w_xz", [P, KD, 2 * DM]), t("w_dt", [P, KD, DM]), t("w_bc", [P, KD, 3, 2, NS]), t("w_o", [P, KD, DM])
            b_in, b_dt, b_bc, Dc, lg, lb, b1 = (vec_at[n] for n in ("c_b_in", "c_b_dt", "c_b_bc", "c_D", "f_gamma", "f_beta", "f_b1"))
            gam, bet, b_o = (vec_at[n] for n in ("c_gamma", "c_beta", "c_b_out"))
            A = t("A", [P, KD, NS])
            w1, w2, hb2 = t("w1", [P, KD, FF]), t("w2", [P, KF, DM]), t("hb2", [P, DM])
            sel = t("sel", [3 * 2 * NS, 2 * NS, P], BF16)
            pb = psum(pc, "pc")
            ws = [(w_xz, rows(d["c_w_inT"])), (w_dt, rows(d["c_w_dtT"])), (w_o, rows(d["c_w_outT"]))]
            with ExitStack() as pq:
                q1, s1 = sb("q1", [P, KD, FF], I32, within=pq), sb("s1", [P, KD, FF], within=pq)
                q2, s2 = sb("q2", [P, KF, DM], I32, within=pq), sb("s2", [P, KF, DM], within=pq)
                f1, f2 = sb("f1", [P, KD, FF], within=pq), sb("f2", [P, KF, DM], within=pq)
                ld, pv, aa = top.sem("ld"), top.sem("pv"), top.sem("aa")
                with nc.Block() as block:
                    @block.sync
                    def _(e):
                        n = 0
                        for dst, src in ws + [(q1, rows(d["f_q1"])), (q2, rows(d["f_q2"]))]:
                            e.dma_start(dst[tuple(slice(None) for _ in dst.shape)], src).then_inc(ld, DMAS)
                            n += 1
                        for k in range(KD):
                            e.dma_start(s1[:, k, :], d["f_s1"][k:k + 1, :].to_broadcast([P, FF])).then_inc(ld, DMAS)
                            n += 1
                        for k in range(KF):
                            e.dma_start(s2[:, k, :], d["f_s2"][k:k + 1, :].to_broadcast([P, DM])).then_inc(ld, DMAS)
                            n += 1
                        for g in range(3):
                            for m, w in enumerate(("c_w_B", "c_w_C")):
                                e.dma_start(w_bc[:, :, g, m, :], rows(d[w + "T"])).then_inc(ld, DMAS)
                                n += 1
                        e.wait_ge(ld, DMAS * n)
                        e.sem_inc(pv, 1)

                    @block.gpsimd
                    def _(e):
                        e.memset(sel[:, :, :], 0.0).then_inc(aa, 1)
                        for g in range(3):
                            e.wait_ge(aa, g + 1)
                            e.affine_select(out=sel[:, :, :], in_=sel[:, :, :], compare_op=ALU.not_equal, fill=1.0,
                                            base=-2 * NS * g, pattern=[[-1, 2 * NS], [0, P]], channel_multiplier=1).then_inc(aa, 1)

                    @block.scalar
                    def _(e):
                        e.wait_ge(pv, 1)
                        e.activation(A[:, :, :].rearrange("p k n -> p (k n)"), vec_at["c_A_log"], ACT.Exp).then_inc(pv, 1)

                    @block.vector
                    def _(e):
                        e.wait_ge(pv, 1)
                        e.tensor_scalar(f1[:, :, :], q1[:, :, :], -128.0, None, ALU.add).then_inc(pv, 1)
                        e.tensor_scalar(f2[:, :, :], q2[:, :, :], -128.0, None, ALU.add).then_inc(pv, 1)
                        e.wait_ge(pv, 4)
                        e.tensor_tensor(w1[:, :, :], f1[:, :, :], s1[:, :, :], ALU.mult)
                        e.tensor_tensor(w2[:, :, :], f2[:, :, :], s2[:, :, :], ALU.mult)
                        e.tensor_scalar(A[:, :, :], A[:, :, :], -1.0, None, ALU.mult)
                        e.tensor_scalar(hb2[:, :], vec_at["f_b2"], 0.5, None, ALU.mult)

            o = t("o", [P, KD, TB])
            h1, h2 = t("h1", [P, KD, TB]), t("h2", [P, TB])
            h3 = h2[0:64, :]
            cS, tw = t("cS", [P, TB]), t("tw", [P, KD, TB])
            lnb = [[t(f"{n}_{i}", sh) for n, sh in (("st", [P, NC, 6]), ("mv", [P, NC, 2]), ("ve", [P, NC]), ("rs", [P, NC]))]
                   for i in range(5)]
            x2 = [t(f"x2_{q}", [P, NC, DM]) for q in (0, 1)]
            x2T = t("x2T", [P, KD, TB])
            xc, zc = t("xc", [P, KD, TB]), t("zc", [P, KD, TB])
            va, vl, vd, dtc, uc = (t(n, [P, KD, TB]) for n in ("va", "vl", "vd", "dtc", "uc"))
            bcf, parts = t("bcf", [96, TB]), t("parts", [96, TB], BF16)
            part = t("part", [96, TB], BF16)
            h0 = t("h0", [P, NS, KD])
            av = [t(f"av{i}", [P, KD, TB]) for i in range(2)]
            bv, gv_ = ([t(f"{n}{i}", [P, KD, TB]) for i in range(2)] for n in ("bv", "gv"))
            acc = t("acc", [P, KD, TB])
            xl = t("xl", [P, NC, DM])
            x3 = [t(f"x3_{q}", [P, NC, DM]) for q in (0, 1)]
            nT = t("nT", [P, KD, TB])
            f_h = t("f_h", [P, KF, TB])
            x3b = t("x3b", [P, NC, DM])

            def vec(x):
                return x.rearrange("p k t -> p (k t)")

            def transposes(s, label, bank, src, dst, evac, after, free, scale=None):
                for c in range(NC):
                    def tr(e, b, c=c):
                        for k in range(KD):
                            i = e.transpose(bank[:, k * P:(k + 1) * P], src(c)[:, k * P:(k + 1) * P], ident[:, :])
                        return i
                    s.do(PE, f"{label}{c}", tr, *after(c), f"{label}e{c - 1}" if c else f"{label}e{NC - 1}@-1")
                    for k in range(KD):
                        lab = f"{label}e{c}" if k == KD - 1 else f"{label}f{c}"
                        if scale is None:
                            s.do(SA, lab, lambda e, b, c=c, k=k: e.activation(
                                dst[:, k, c * CH:(c + 1) * CH], bank[:, k * P:(k + 1) * P], ACT.Copy), f"{label}{c}", *free)
                        else:
                            s.do(SA, lab, lambda e, b, c=c, k=k: e.activation(
                                dst[:, k, c * CH:(c + 1) * CH], bank[:, k * P:(k + 1) * P], ACT.Identity,
                                bias=scale[1][:, k:k + 1], scale=scale[0][:, k:k + 1]), f"{label}{c}", *free)

            def couple(s, q):
                for y in range(3):
                    src = (lambda b, k: x1T[:, k, bass.ds(b.token(), TB)]) if y == 0 else (lambda b, k: o[:, k, :])
                    ready = f"add{y - 1}" if y else None
                    last = lambda n: f"{n}{y - 1}" if y else f"{n}2@-1"
                    for m in range(KD):
                        def mm(e, b, m=m, src=src):
                            for k in range(KD):
                                i = e.matmul(pb[m][:, :], cn_w1[:, k, m * P:(m + 1) * P], src(b, k), start=(k == 0), stop=(k == KD - 1))
                            return i
                        s.do(PE, f"m1_{m}_{y}", mm, *([ready] if ready else []), *([last("a2_"), f"couple_norm.bTe{NC - 1}@-1"] if m == 0 else [last("ta"), f"couple_norm.l2_n{NC - 1}@-1"]))
                        s.do(SA, f"a1_{m}_{y}", lambda e, b, m=m: e.activation(h1[:, m, :], pb[m][:, :], ACT.Gelu, bias=cn_b1[:, m:m + 1]),
                             f"m1_{m}_{y}", last("m2_"))

                    def mm2(e, b):
                        for k in range(KD):
                            i = e.matmul(pb[0][:, :], cn_w2[:, k, :], h1[:, k, :], start=(k == 0), stop=(k == KD - 1))
                        return i
                    s.do(PE, f"m2_{y}", mm2, f"a1_1_{y}", f"a1_0_{y}")
                    s.do(SA, f"a2_{y}", lambda e, b: e.activation(h2[:, :], pb[0][:, :], ACT.Gelu, bias=cn_b2[:, 0:1]), f"m2_{y}", last("m4_"))
                    s.do(PE, f"m3_{y}", lambda e, b: e.matmul(pb[1][0:64, :], cn_w3[:, :], h2[:, :], start=True, stop=True), f"a2_{y}")
                    s.do(SA, f"a3_{y}", lambda e, b: e.activation(h3, pb[1][0:64, :], ACT.Gelu, bias=cn_b3[0:64, :]), f"m3_{y}", last("m4_"))
                    s.do(PE, f"m4_{y}", lambda e, b: e.matmul(pb[1][:, :], cw4[:, :], h3, start=True, stop=True), f"a3_{y}")
                    s.do(SA, f"ta{y}", lambda e, b: e.activation(cS[:, :], pb[1][:, :], ACT.Tanh, bias=hb4[:, 0:1], scale=0.5), f"m4_{y}", last("t1_"))
                    s.do(VE, f"cs{y}", lambda e, b: e.tensor_scalar(cS[:, :], cS[:, :], slope[:, 0:1], shift[:, 0:1], ALU.mult, ALU.add), f"ta{y}", last("t1_"))
                    for k in range(KD):
                        s.do(VE, f"t{k}_{y}", lambda e, b, k=k, src=src: e.tensor_tensor(tw[:, k, :], cS[:, :], src(b, 1 - k), ALU.mult), f"cs{y}", last("add"))
                    s.do(PO, f"ad{y}", lambda e, b, src=src: e.tensor_tensor(o[:, 0, :], src(b, 0), tw[:, 0, :], ALU.add),
                         f"t1_{y}", *([] if y else [f"couple_norm.bt{NC - 1}@-1"]), *([f"ad{y - 1}"] if y else []))
                    s.do(PO, f"add{y}", lambda e, b, src=src: e.tensor_tensor(o[:, 1, :], src(b, 1), tw[:, 1, :], ALU.subtract),
                         f"t1_{y}", *([f"add{y - 1}"] if y else []))
                s.do(PO, "res", lambda e, b: e.tensor_tensor(o[:, :, :], o[:, :, :], x1T[:, :, bass.ds(b.token(), TB)], ALU.add), "add2", "ad2")

            def couple_norm(s, q):
                for c in range(NC):
                    def tr(e, b, c=c):
                        for k in range(KD):
                            i = e.transpose(pb[c // 2][:, (c % 2) * DM + k * P:(c % 2) * DM + (k + 1) * P], o[:, k, c * CH:(c + 1) * CH], ident[:, :])
                        return i
                    s.do(PE, f"bt{c}", tr, "couple.res", "couple.ta2")
                layer_norm(s, "l2", lambda c: pb[c // 2][:, (c % 2) * DM:(c % 2 + 1) * DM], lambda c: x2[q][:, c, :], *lnb[0],
                           lambda c: [f"bt{c | 1}"], ["scan_out.xl_b@-2"])
                transposes(s, "bT", pb[0], lambda c: x2[q][:, c, :], x2T, SA, lambda c: [f"l2_n{NC - 1}"], ["scan_in.bc@-1", "scan_in.z1@-1"])

            def scan_in(s, q):
                def project(m, bank):
                    def mm(e, b):
                        for k in range(KD):
                            i = e.matmul(bank[:, :], w_xz[:, k, m * P:(m + 1) * P], x2T[:, k, :], start=(k == 0), stop=(k == KD - 1))
                        return i
                    return mm
                ready = f"couple_norm.bTe{NC - 1}"
                for m in range(KD):
                    s.do(PE, f"x{m}", project(m, pb[2]), ready, f"xe{m - 1}" if m else f"scan_out.pre{NC - 1}@-1")
                    s.do(SA, f"xe{m}", lambda e, b, m=m: e.activation(xc[:, m, :], pb[2][:, :], ACT.Identity, bias=b_in[:, m:m + 1]),
                         f"x{m}", "scan_out.dx1@-1")
                for m in range(KD):
                    s.do(PE, f"z{m}", project(KD + m, pb[2]), ready, f"ze{m - 1}" if m else f"xe{KD - 1}")
                    s.do(SA, f"ze{m}", lambda e, b, m=m: e.activation(zc[:, m, :], pb[2][:, :], ACT.Identity, bias=b_in[:, KD + m:KD + m + 1]),
                         f"z{m}", f"scan_out.o{NC - 1}@-1")
                for m in range(KD):
                    def mm(e, b, m=m):
                        for k in range(KD):
                            i = e.matmul(pb[2][:, :], w_dt[:, k, m * P:(m + 1) * P], xc[:, k, :], start=(k == 0), stop=(k == KD - 1))
                        return i
                    s.do(PE, f"d{m}", mm, f"xe{KD - 1}", *([f"ze{KD - 1}"] if m == 0 else [f"va{m - 1}", f"vr{m - 1}"]))
                    s.do(SA, f"va{m}", lambda e, b, m=m: e.activation(va[:, m, :], pb[2][:, :], ACT.Abs, bias=b_dt[:, m:m + 1]), f"d{m}", "ve@-1")
                    s.do(VE, f"vr{m}", lambda e, b, m=m: e.tensor_scalar(dtc[:, m, :], pb[2][:, :], b_dt[:, m:m + 1], 0.0, ALU.add, ALU.max), f"va{m}",
                         f"core.a{NS - 1}_1@-1", "u@-1")

                def bc(e, b):
                    for k in range(KD):
                        i = e.matmul(pb[2][0:96, :], w_bc[:, k, :, :, :].rearrange("p g m n -> p (g m n)"), xc[:, k, :], start=(k == 0), stop=(k == KD - 1))
                    return i
                s.do(PE, "bc", bc, "va1", "vr1")
                s.do(SA, "bce", lambda e, b: e.activation(bcf[:, :], pb[2][0:96, :], ACT.Identity, bias=b_bc[0:96, :]), "bc", "pl@-1")
                s.do(SA, "vy", lambda e, b: e.activation(vec(va[:, :, :]), vec(va[:, :, :]), ACT.Exp, scale=-1.0), "va1")
                s.do(SA, "vl", lambda e, b: e.activation(vec(vl[:, :, :]), vec(va[:, :, :]), ACT.Ln, bias=1.0), "vy", "vs@-1")
                s.do(VE, "vd", lambda e, b: e.tensor_scalar(vec(vd[:, :, :]), vec(va[:, :, :]), 1.0, -1.0, ALU.add, ALU.add), "vy", "vt@-1")
                s.do(VE, "ve", lambda e, b: e.tensor_tensor(vec(vd[:, :, :]), vec(va[:, :, :]), vec(vd[:, :, :]), ALU.subtract), "vd")
                s.do(VE, "vs", lambda e, b: e.tensor_tensor(vec(vd[:, :, :]), vec(vl[:, :, :]), vec(vd[:, :, :]), ALU.add), "vl", "ve")
                s.do(VE, "vt", lambda e, b: e.tensor_tensor(vec(dtc[:, :, :]), vec(dtc[:, :, :]), vec(vd[:, :, :]), ALU.add), "vs", "vr1")
                s.do(PO, "u", lambda e, b: e.tensor_tensor(vec(uc[:, :, :]), vec(dtc[:, :, :]), vec(xc[:, :, :]), ALU.mult), "vt", f"core.b{NS - 1}@-1")
                s.do(VE, "ph", lambda e, b: e.tensor_copy(part[:, :], bcf[:, :]), "bce", "p0@-1", "pr@-1", "pr2@-1")
                s.do(VE, "p0", lambda e, b: e.tensor_copy(parts[0:32, :], part[0:32, :]), "ph", f"core.C{NS - 1}@-1")
                s.do(VE, "pr", lambda e, b: e.tensor_tensor(bcf[:, :], bcf[:, :], part[:, :], ALU.subtract), "ph", "pl@-1")
                s.do(VE, "pm", lambda e, b: e.tensor_copy(part[:, :], bcf[:, :]), "pr", "p0")
                s.do(VE, "p1", lambda e, b: e.tensor_copy(parts[32:64, :], part[32:64, :]), "pm", f"core.C{NS - 1}@-1")
                s.do(VE, "pr2", lambda e, b: e.tensor_tensor(bcf[:, :], bcf[:, :], part[:, :], ALU.subtract), "pm", "p1")
                s.do(VE, "pl", lambda e, b: e.tensor_copy(parts[64:96, :], bcf[64:96, :]), "pr2")

            def scan_z(s, q):
                s.do(SA, "z", lambda e, b: e.activation(vec(zc[:, :, :]), vec(zc[:, :, :]), ACT.Silu), "scan_in.ze1")

            def core(s, q):
                for n in range(NS):
                    i2 = n % 2
                    two = lambda l, n=n: f"{l}{n - 2}" if n > 1 else f"{l}{NS - 2 + n}@-1"
                    s.do(PE, f"B{n}", lambda e, b, n=n, i2=i2: e.matmul(pb[4 + i2][:, :], sel[:, n, :], parts[:, :], start=True, stop=True),
                         "scan_in.pl", "scan_in.p1", "scan_in.p0", two("b"))
                    s.do(PE, f"C{n}", lambda e, b, n=n, i2=i2: e.matmul(pb[6 + i2][:, :], sel[:, NS + n, :], parts[:, :], start=True, stop=True), two("g"))
                    for k in range(KD):
                        s.do(SA, f"a{n}_{k}", lambda e, b, n=n, k=k, i2=i2: e.activation(av[i2][:, k, :], dtc[:, k, :], ACT.Exp, scale=A[:, k, n:n + 1]),
                             "scan_in.vt", f"s{n - 2}_{k}" if n > 1 else f"s{NS - 2 + n}_{k}@-1")

                    def wide(x):
                        return x.rearrange("p (o t) -> p o t", o=1).to_broadcast([P, KD, TB])
                    s.do(VE, f"b{n}", lambda e, b, i2=i2: e.tensor_tensor(bv[i2][:, :, :], uc[:, :, :], wide(pb[4 + i2][:, :]), ALU.mult),
                         "scan_in.u", f"B{n}", two("g"), two("hs"))
                    for k in range(KD):
                        s.do(VE, f"s{n}_{k}", lambda e, b, n=n, k=k, i2=i2: e.tensor_tensor_scan(
                            bv[i2][:, k, :], av[i2][:, k, :], bv[i2][:, k, :], h0[:, n, k:k + 1], ALU.mult, ALU.add),
                            f"b{n}", f"a{n}_{k}", f"hs{n}@-1")
                    s.do(PO, f"hs{n}", lambda e, b, n=n, i2=i2: e.tensor_copy(h0[:, n, :], bv[i2][:, :, TB - 1]), f"s{n}_1")
                    dst = acc if n == 0 else gv_[i2]
                    s.do(VE, f"g{n}", lambda e, b, i2=i2, dst=dst: e.tensor_tensor(dst[:, :, :], bv[i2][:, :, :], wide(pb[6 + i2][:, :]), ALU.mult),
                         f"s{n}_1", f"C{n}", f"+{n - 2}" if n > 2 else (f"+{NS - n}@-1" if n else "scan_out.gate@-1"))
                    if n:
                        s.do(PO, f"+{n}", lambda e, b, i2=i2: e.tensor_tensor(vec(acc[:, :, :]), vec(acc[:, :, :]), vec(gv_[i2][:, :, :]), ALU.add),
                             f"g{n}", f"+{n - 1}" if n > 1 else "g0")

            def scan_out(s, q):
                for k in range(KD):
                    s.do(VE, f"dx{k}", lambda e, b, k=k: e.scalar_tensor_tensor(acc[:, k, :], xc[:, k, :], Dc[:, k:k + 1], acc[:, k, :], ALU.mult, ALU.add),
                         f"core.+{NS - 1}")
                s.do(VE, "gate", lambda e, b: e.tensor_tensor(vec(zc[:, :, :]), vec(acc[:, :, :]), vec(zc[:, :, :]), ALU.mult), "dx1", "dx0", "scan_z.z")
                for c in range(NC):
                    s.do(PO, f"xb{c}", lambda e, b, c=c: e.tensor_tensor(xl[:, c, :], x2[q][:, c, :], b_o, ALU.add),
                         f"couple_norm.l2_n{NC - 1}", f"l4_n{NC - 1}@-1")
                for c in range(NC):
                    def mm(e, b, c=c):
                        for k in range(KD):
                            i = e.matmul(pb[2][:, 0:DM], zc[:, k, c * CH:(c + 1) * CH], w_o[:, k, :], start=(k == 0), stop=(k == KD - 1))
                        return i
                    s.do(PE, f"o{c}", mm, "gate", f"pre{c - 1}" if c else "scan_in.bce")
                    s.do(VE, f"pre{c}", lambda e, b, c=c: e.tensor_tensor(xl[:, c, :], pb[2][:, 0:DM], xl[:, c, :], ALU.add), f"o{c}", f"xb{c}")
                layer_norm(s, "l3", lambda c: xl[:, c, :], lambda c: xl[:, c, :], *lnb[1], lambda c: [f"pre{c}"], [f"pre{NC - 1}"])
                every = lambda v: v.rearrange("p (o f) -> p o f", o=1).to_broadcast([P, NC, DM])
                s.do(PO, "xl_g", lambda e, b: e.tensor_tensor(xl[:, :, :], xl[:, :, :], every(gam), ALU.mult), f"l3_n{NC - 1}")
                s.do(PO, "xl_a", lambda e, b: e.tensor_tensor(xl[:, :, :], xl[:, :, :], every(bet), ALU.add), "xl_g")
                s.do(PO, "xl_b", lambda e, b: e.tensor_tensor(xl[:, :, :], xl[:, :, :], x2[q][:, :, :], ALU.add), "xl_a")
                layer_norm(s, "l4", lambda c: xl[:, c, :], lambda c: x3[q][:, c, :], *lnb[2], lambda c: ["xl_b"], ["ffn_in.l5_n3@-2", "ffn_out.xb@-2"])

            def ffn_in(s, q):
                layer_norm(s, "l5", lambda c: x3[q][:, c, :], lambda c: xn[:, c, :], *lnb[3], lambda c: [f"scan_out.l4_n{NC - 1}"], [f"fT{NC - 1}@-1"])
                transposes(s, "fT", pb[3], lambda c: xn[:, c, :], nT, SA, lambda c: [f"l5_n{NC - 1}"] + (["ffn_out.o3@-1", "ffn_out.w3@-1"] if c == 0 else []),
                           [f"ffn_up.u{KF - 1}@-1"], scale=(lg, lb))

            def ffn_up(s, q):
                for m in range(KF):
                    def mm(e, b, m=m):
                        for k in range(KD):
                            i = e.matmul(pb[3][:, :], w1[:, k, m * P:(m + 1) * P], nT[:, k, :], start=(k == 0), stop=(k == KD - 1))
                        return i
                    s.do(PE, f"u{m}", mm, f"ffn_in.fTe{NC - 1}", *([f"si{m - 1}"] if m else []))
                    s.do(SA, f"si{m}", lambda e, b, m=m: e.activation(f_h[:, m, :], pb[3][:, :], ACT.Silu, bias=b1[:, m:m + 1]), f"u{m}", "ffn_out.o3@-1")

            def ffn_out(s, q):
                for c in range(NC):
                    s.do(PO, f"xa{c}", lambda e, b, c=c: e.tensor_tensor(x3b[:, c, :], x3[q][:, c, :], hb2[:, :], ALU.add), f"scan_out.l4_n{NC - 1}", "store@-1")
                s.do(PO, "xb", lambda e, b: e.tensor_tensor(x3b[:, :, :], x3b[:, :, :], x3[q][:, :, :], ALU.add), f"xa{NC - 1}")
                for c in range(NC):
                    def mm(e, b, c=c):
                        for k in range(KF):
                            i = e.matmul(pb[3][:, 0:DM], f_h[:, k, c * CH:(c + 1) * CH], w2[:, k, :], start=(k == 0), stop=(k == KF - 1))
                        return i
                    s.do(PE, f"o{c}", mm, f"ffn_up.si{KF - 1}", *([f"w{c - 1}"] if c else []))
                    s.do(VE, f"w{c}", lambda e, b, c=c: e.scalar_tensor_tensor(x3b[:, c, :], pb[3][:, 0:DM], 0.5, x3b[:, c, :], ALU.mult, ALU.add), f"o{c}", "xb")
                layer_norm(s, "l6", lambda c: x3b[:, c, :], lambda c: x3b[:, c, :], *lnb[4], lambda c: [f"w{c}"], [])
                s.do(SP, "store", lambda e, b: e.dma_start(
                    out.rearrange("(n p) f -> p n f", p=P)[:, bass.ds(b.off * NC if b.j is None else b.j * (2 * NC) + b.off * NC, NC), :], x3b[:, :, :]),
                    f"l6_n{NC - 1}", dmas=1)

            xn = t("xn", [P, NC, DM])
            z_sem = top.sem("z_sem")
            for name, fn in (("couple", couple), ("couple_norm", couple_norm), ("scan_in", scan_in), ("scan_z", scan_z), ("core", core),
                             ("scan_out", scan_out), ("ffn_in", ffn_in), ("ffn_up", ffn_up), ("ffn_out", ffn_out)):
                Stage(top, name, fn)
            plan = [("couple", 0, 0, 0.1), ("couple_norm", 0, 0.1, 0.2), ("scan_in", 0, 0.2, 0.3), ("scan_z", 0, 0.3, 0.31),
                    ("core", 0, 0.31, 0.6), ("scan_out", 0, 0.6, 0.7), ("ffn_in", 0, 0.7, 0.8), ("ffn_up", 0, 0.8, 0.9), ("ffn_out", 0, 0.9, 1)]
            with nc.Block() as block:
                block.vector(lambda e: e.memset(h0[:, :, :], 0.0))
            with nc.Block() as block:
                def sp(e):
                    top.run(SP, e, plan)
                    for q in (0, 1):
                        e.wait_ge(top.stages["ffn_out"].sem["store"][q], DMAS * (NB // 2 + 1))
                block.sync(sp)
                block.tensor(lambda e: top.run(PE, e, plan))
                block.vector(lambda e: top.run(VE, e, plan))
                block.gpsimd(lambda e: top.run(PO, e, plan))
                block.scalar(lambda e: top.run(SA, e, plan))


def kernel(**inputs):
    import numpy as np
    import concourse.bacc as bacc
    from concourse.bass_utils import run_bass_kernel_spmd

    a = {k: np.asarray(v) for k, v in inputs.items()}
    L0, L1 = "L0_attn_", "L1_attn_"
    F0, F1 = "L0_ffn_", "L1_ffn_"

    def column(v):
        v = v.reshape(v.shape[0], -1)
        if v.shape[0] < P:
            v = np.concatenate([v, np.zeros((P - v.shape[0], v.shape[1]), v.dtype)])
        return v.reshape(-1, P, v.shape[1]).transpose(1, 0, 2).reshape(P, -1)

    down = {"cn_b1": a[F0 + "cn_b1"], "cn_b2": a[F0 + "cn_b2"], "cn_b3": a[F0 + "cn_b3"], "cn_w4": a[F0 + "cn_w4"],
            "gc_b1": a[F0 + "gc_b1"], "gc_b2": a[F0 + "gc_b2"], "gc_w3": a[F0 + "gc_w3"],
            "conv_b": a[L0 + "conv_b"], "conv_w": a[L0 + "conv_w"], "norm_w": a[L0 + "norm_w"],
            "c_b_in": a[L1 + "b_in"], "c_b_dt": a[L1 + "b_dt"], "c_b_bc": np.concatenate([a[L1 + "b_B"], a[L1 + "b_C"]] * 3),
            "c_D": a[L1 + "D"], "c_A_log": a[L1 + "A_log"],
            "f_gamma": a[F1 + "ln_gamma"], "f_beta": a[F1 + "ln_beta"], "f_b1": a[F1 + "fc1_bias"]}
    every = {"cn_b4": a[F0 + "cn_b4"], "gc_b3": a[F0 + "gc_b3"], "adaptive_range": a[F0 + "adaptive_range"],
             "dt_bias": a[L0 + "dt_bias"], "A_log": a[L0 + "A_log"], "D": a[L0 + "D"],
             "c_gamma": a[L1 + "gamma"], "c_beta": a[L1 + "beta"], "c_b_out": a[L1 + "b_out"], "f_b2": a[F1 + "fc2_bias"]}
    arrays = {
        "u": a[L0 + "u"][0], "uT": a[L0 + "u"][0].T, "W_inT": a[L0 + "W_in"].T, "W_outT": a[L0 + "W_out"].T,
        **{n: a[F0 + n] for n in ("cn_w1", "cn_w2", "cn_w3", "gc_w1", "gc_w2")},
        **{f"c_{n}T": a[L1 + n].T for n in ("w_in", "w_dt", "w_B", "w_C", "w_out")},
        "f_q1": a[F1 + "fc1_q"], "f_s1": a[F1 + "fc1_scales"], "f_q2": a[F1 + "fc2_q"], "f_s2": a[F1 + "fc2_scales"],
        "columns": np.concatenate([column(down[n]) for n, _ in COLUMNS], axis=1),
        "everywhere": np.concatenate([every[n].reshape(-1) for n, _ in EVERYWHERE]),
    }
    arrays = {f"in_{k}": np.ascontiguousarray(v) for k, v in arrays.items()}
    nc = bacc.Bacc("TRN2", target_bir_lowering=False, num_devices=1)
    dram = {k[3:]: nc.dram_tensor(k, v.shape, mybir.dt.from_np(v.dtype), kind="ExternalInput").ap() for k, v in arrays.items()}
    out = nc.dram_tensor("out", (T, DM), F32, kind="ExternalOutput").ap()
    build(nc, dram, out)
    r = run_bass_kernel_spmd(nc, [arrays], core_ids=[0])
    return r.results[0]["out"].reshape(1, T, DM)
```

```python
import concourse.bass as bass
from concourse import mybir
from contextlib import ExitStack
from math import ceil

F32 = mybir.dt.float32
F32R = mybir.dt.float32r
BF16 = mybir.dt.bfloat16
I32 = mybir.dt.int32
ALU = mybir.AluOpType
ACT = mybir.ActivationFunctionType

P = 128
T, DM = 4096, 256
TB = 512
NB = T // TB
CH = 128
NC = TB // CH
KD = DM // P
DI, DS, NH, HD, TAPS = 512, 64, 8, 64, 4
NX = (DI + 2 * DS) // P
DIN = 2 * DI + 2 * DS + NH
NS = 16
FF = 1024
KF = FF // P
GQ = 128
EPS = 1e-5
COLUMNS = [("cn_b1", KD), ("cn_b2", 1), ("cn_b3", 1), ("cn_w4", 1), ("gc_b1", 1), ("gc_b2", 1), ("gc_w3", 1),
           ("conv_b", NX), ("conv_w", NX * TAPS), ("norm_w", DI // P),
           ("c_b_in", 2 * KD), ("c_b_dt", KD), ("c_b_bc", 1), ("c_D", KD), ("c_A_log", KD * NS),
           ("f_gamma", KD), ("f_beta", KD), ("f_b1", KF)]
EVERYWHERE = [("cn_b4", 1), ("gc_b3", 1), ("adaptive_range", 1), ("dt_bias", NH), ("A_log", NH), ("D", NH),
              ("c_gamma", DM), ("c_beta", DM), ("c_b_out", DM), ("f_b2", DM)]
PE, SA, VE, PO, SP = "pe", "act", "dve", "pool", "sp"
AHEAD = 4
DMAS = 16


class Block:

    def __init__(self, j, off):
        self.j, self.off = j, off

    def chunk(self):
        return self.off * NC if self.j is None else self.j * (2 * NC) + self.off * NC

    def token(self):
        return self.off * TB if self.j is None else self.j * (2 * TB) + self.off * TB


class Stage:

    def __init__(self, top, name, build):
        self.name, self.sem, self.count, self.place = name, {}, {}, {}
        self.steps = [[], []]
        for parity in (0, 1):
            self.building = self.steps[parity]
            build(self, parity)
        for step in self.steps[0]:
            engine, label, n = step[0], step[1], step[4]
            if n:
                self.sem[label] = [top.sem(f"{name}_{label}{q}") for q in (0, 1)]
                self.place[label] = (None, n)
            else:
                if engine not in self.sem:
                    self.sem[engine] = top.sem(f"{name}_{engine}")
                self.count[engine] = self.count.get(engine, 0) + 1
                self.place[label] = (engine, self.count[engine])
        top.stages[name] = self

    def do(self, engine, label, work, *after, dmas=0, alone=False):
        self.building.append((engine, label, work, after, dmas, alone))


class Program:
    def __init__(self, nc, ctx):
        self.nc, self.ctx, self.stages = nc, ctx, {}
        self.apart = self.sem("apart")

    def sem(self, name):
        return self.ctx.enter_context(self.nc.semaphore(name))

    def level(self, stage, label, block):
        engine, at = stage.place[label]
        if engine is None:
            q = block.off % 2
            return stage.sem[label][q], DMAS * at, ((block.off - q) // 2 + 2) * DMAS * at
        n = stage.count[engine]
        return stage.sem[engine], 2 * n, (block.off + 2) * n + at

    def emit(self, me, eng, work, j, seen):
        for stage, block, step in work:
            engine, label, fn, after, n, alone = step
            waited = False
            if engine != me:
                continue
            for name in after:
                name, _, lag = name.partition("@")
                of, _, what = name.rpartition(".")
                of = self.stages[of] if of else stage
                then = Block(j, block.off + int(lag or 0))
                if j is None and then.off >= NB:
                    continue
                sem, a, c = self.level(of, what, then)
                if seen.get(sem.name, 0) >= c:
                    continue
                seen[sem.name] = c
                eng.wait_ge(sem, c if j is None else j * a + c)
                waited = j is not None
                if waited and me == SP:
                    eng.sem_inc(self.apart, 1)
            if waited and (me == PO or alone):
                eng.sem_inc(self.apart, 1)
            if n:
                done = fn(eng, block)
                done = done if isinstance(done, list) else [done]
                assert len(done) == n
                for d in done:
                    d.then_inc(stage.sem[label][block.off % 2], DMAS)
            else:
                fn(eng, block).then_inc(stage.sem[engine], 1)

    def body(self, plan, j, t):
        work = []
        for name, lo, hi in plan:
            stage = self.stages[name]
            assert hi - lo <= 1
            for n in range(len(stage.steps[0])):
                at = lo + (hi - lo) * n / len(stage.steps[0])
                block = t - int(at)
                if j is None and not 0 <= block < NB:
                    continue
                work.append((at % 1, block, stage, Block(j, block), stage.steps[block % 2][n]))
        work.sort(key=lambda w: w[:2])
        return [w[2:] for w in work]

    def credit(self, me, eng, names):
        for name in names:
            stage = self.stages[name]
            for label, (engine, n) in stage.place.items():
                if engine is None and me == SP:
                    for q in (0, 1):
                        eng.sem_inc(stage.sem[label][q], DMAS * n)
            if me in stage.count:
                eng.sem_inc(stage.sem[me], 2 * stage.count[me])

    def run(self, me, eng, plan):
        lag = max(ceil(hi) - 1 for _, _, hi in plan)
        first = lag + lag % 2
        self.credit(me, eng, [p[0] for p in plan])
        seen = {}
        for t in range(first):
            self.emit(me, eng, self.body(plan, None, t), None, seen)
        with eng.Fori(0, (NB - first) // 2) as j:
            seen = {}
            for t in (first, first + 1):
                self.emit(me, eng, self.body(plan, j, t), j, seen)
        seen = {}
        for t in range(NB, NB + lag):
            self.emit(me, eng, self.body(plan, None, t), None, seen)


def passes(e, out, pairs):
    for n, (w, x) in enumerate(pairs):
        i = e.matmul(out, w, x, start=(n == 0), stop=(n == len(pairs) - 1))
    return i


def build(nc, d, out, x2_dram):
    with ExitStack() as ctx:
        top = Program(nc, ctx)

        def sb(name, shape, dt=F32, within=ctx):
            return within.enter_context(nc.sbuf_tensor(name, shape, dt))

        def psum(within, n):
            return [within.enter_context(nc.psum_tensor(f"{n}{i}", [P, 512], F32)) for i in range(8)]

        ident, upper, below, ones = (sb(n, [P, P]) for n in ("ident", "upper", "below", "ones"))
        mhalf, sign = sb("mhalf", [P, NC]), sb("sign", [P, 1])
        x1T = sb("x1T", [P, KD, T])
        cn_w1, cn_w2 = sb("cn_w1", [P, KD, DM]), sb("cn_w2", [P, KD, P])
        cn_w3 = sb("cn_w3", [P, 64])
        gc_w1, gc_w2 = sb("gc_w1", [P, KD, P]), sb("gc_w2", [P, 64])
        columns, everywhere = sb("columns", [P, sum(n for _, n in COLUMNS)]), sb("everywhere", [P, sum(n for _, n in EVERYWHERE)])
        vec_at = {}
        for held, names in ((columns, COLUMNS), (everywhere, EVERYWHERE)):
            at = 0
            for name, n in names:
                vec_at[name] = held[:, at:at + n]
                at += n
        cn_b1, cn_b2, cn_b3, cn_b4 = (vec_at[n] for n in ("cn_b1", "cn_b2", "cn_b3", "cn_b4"))
        gc_b1, gc_b2, gc_b3, rng = (vec_at[n] for n in ("gc_b1", "gc_b2", "gc_b3", "adaptive_range"))
        cw4 = sb("cw4", [64, P])
        gw3 = sb("gw3", [64, P])
        hb4, hg3 = sb("hb4", [P, 1]), sb("hg3", [P, 1])
        slope, shift = sb("slope", [P, 1]), sb("shift", [P, 1])
        ready = top.sem("ready")

        def rows(v):
            return v.rearrange("(k p) n -> p k n", p=P)

        c_sem, w_sem = top.sem("const"), top.sem("weights")
        with nc.Block() as block:
            early = [(cn_w1, rows(d["cn_w1"])), (cn_w2, rows(d["cn_w2"])),
                     (cn_w3, d["cn_w3"]), (gc_w1, rows(d["gc_w1"])), (gc_w2, d["gc_w2"]),
                     (columns, d["columns"]),
                     (everywhere, d["everywhere"].rearrange("(a n) -> a n", a=1).to_broadcast([P, everywhere.shape[1]]))]

            @block.sync
            def _(e):
                for dst, src in early:
                    e.dma_start(dst[tuple(slice(None) for _ in dst.shape)], src).then_inc(w_sem, DMAS)
                e.wait_ge(w_sem, DMAS * len(early))

            @block.gpsimd
            def _(e):
                e.memset(ident[:, :], 0.0).then_inc(c_sem, 1)
                e.memset(upper[:, :], 1.0).then_inc(c_sem, 1)
                e.memset(below[:, :], 1.0).then_inc(c_sem, 1)
                e.memset(ones[:, :], 1.0).then_inc(c_sem, 1)
                e.memset(mhalf[:, :], -0.5).then_inc(c_sem, 1)
                e.memset(sign[:, :], 1.0).then_inc(c_sem, 1)
                e.wait_ge(c_sem, 6)
                e.affine_select(out=ident[:, :], in_=ident[:, :], compare_op=ALU.not_equal, fill=1.0,
                                base=0, pattern=[[-1, P]], channel_multiplier=1)
                e.affine_select(out=upper[:, :], in_=upper[:, :], compare_op=ALU.is_ge, fill=0.0,
                                base=0, pattern=[[1, P]], channel_multiplier=-1)
                e.affine_select(out=below[:, :], in_=below[:, :], compare_op=ALU.is_ge, fill=0.0,
                                base=-1, pattern=[[-1, P]], channel_multiplier=1)
                e.affine_select(out=sign[:, :], in_=sign[:, :], compare_op=ALU.is_ge, fill=-1.0,
                                base=P // 2 - 1, pattern=[[0, 1]], channel_multiplier=-1).then_inc(c_sem, 1)

            @block.vector
            def _(e):
                e.wait_ge(w_sem, DMAS * len(early))
                e.tensor_copy(cw4[:, :], vec_at["cn_w4"][0:64, :].to_broadcast([64, P]))
                e.tensor_copy(gw3[:, :], vec_at["gc_w3"][0:64, :].to_broadcast([64, P]))
                e.tensor_scalar(hb4[:, :], cn_b4, 0.5, None, ALU.mult)
                e.tensor_scalar(hg3[:, :], gc_b3, 0.5, None, ALU.mult)

        def layer_norm(s, tag, src, dst, st, mv, ve, rs, src_ready, dst_free, on=VE):
            for c in range(NC):
                s.do(VE, f"{tag}_st{c}", lambda e, b, c=c: e.bn_stats(st[:, c, :], src(c)), *src_ready(c),
                     f"{tag}_ve@-1")
                s.do(VE, f"{tag}_mv{c}", lambda e, b, c=c: e.bn_aggr(mv[:, c, :], st[:, c, :]), alone=True, *[f"{tag}_st{c}",
                     f"{tag}_n{NC - 1}@-1"])
            s.do(VE, f"{tag}_ve", lambda e, b: e.tensor_scalar(ve[:, :], mv[:, :, 1], EPS, None, ALU.add),
                 f"{tag}_mv{NC - 1}", f"{tag}_rs@-1")
            s.do(PO, f"{tag}_rs", lambda e, b: e.tensor_tensor(rs[:, :], ve[:, :], mhalf[:, :], ALU.pow),
                 f"{tag}_ve", f"{tag}_n{NC - 1}@-1")
            for c in range(NC):
                s.do(VE, f"{tag}_n{c}",
                     lambda e, b, c=c: e.tensor_scalar(dst(c), src(c), mv[:, c, 0:1], rs[:, c:c + 1],
                                                       ALU.subtract, ALU.mult),
                     f"{tag}_rs", *dst_free)

        with ExitStack() as pa:
            def a(name, shape, dt=F32):
                return sb(name, shape, dt, within=pa)

            def two(name, shape, dt=F32):
                return [a(f"{name}{q}", shape, dt) for q in (0, 1)]

            Wh, Wl = a("Wh", [P, KD, DIN], F32R), a("Wl", [P, KD, DIN], F32R)
            W_out = a("W_out", [P, DI // P, DM])
            cw, cb = vec_at["conv_w"].rearrange("p (m j) -> p m j", m=NX), vec_at["conv_b"]
            nw, dtb1, D1 = vec_at["norm_w"], vec_at["dt_bias"], vec_at["D"]
            dtb, negA = a("dtb", [P, NC, NH]), a("negA", [P, NC, NH])
            expA = a("expA", [P, NH])
            belowr = a("belowr", [P, P], F32R)
            S, raw = a("S", [DS, DI]), a("raw", [P, NX, TB + TAPS - 1])

            wa_sem, wa_act, wa_dve, wa_pool = (top.sem(n) for n in ("wa_sem", "wa_act", "wa_dve", "wa_pool"))
            with ExitStack() as pw:
                W_in, W_raw = sb("W_in", [P, KD, DIN], within=pw), sb("W_raw", [P, DI // P, DM], within=pw)
                with nc.Block() as block:
                    @block.sync
                    def _(e):
                        e.dma_start(W_in[:, :, :], rows(d["W_inT"])).then_inc(wa_sem, DMAS)
                        e.dma_start(W_raw[:, :, :], rows(d["W_outT"])).then_inc(wa_sem, DMAS)
                        e.wait_ge(wa_sem, 2 * DMAS)

                    @block.scalar
                    def _(e):
                        e.preload_act_table_set("natural_log_exp_and_others")
                        e.activation(expA[:, :], vec_at["A_log"], ACT.Exp).then_inc(wa_act, 1)
                        e.wait_ge(wa_sem, 2 * DMAS)
                        for k in range(KD):
                            e.activation(Wh[:, k, :], W_in[:, k, :], ACT.Copy).then_inc(wa_act, 1)

                    @block.vector
                    def _(e):
                        e.memset(S[:, :], 0.0)
                        e.memset(raw[:, :, TB:TB + TAPS - 1], 0.0)
                        e.tensor_copy(belowr[:, :], below[:, :])
                        for c in range(NC):
                            e.tensor_copy(dtb[:, c, :], dtb1)
                        e.wait_ge(wa_act, 1)
                        for c in range(NC):
                            e.tensor_scalar(negA[:, c, :], expA[:, :], -1.0, None, ALU.mult)
                        for k in range(KD):
                            e.wait_ge(wa_act, 2 + k)
                            e.tensor_tensor(Wl[:, k, :], W_in[:, k, :], Wh[:, k, :].bitcast(F32), ALU.subtract)

                    @block.gpsimd
                    def _(e):
                        e.wait_ge(wa_sem, 2 * DMAS)
                        for k in range(DI // P):
                            e.tensor_scalar(W_out[:, k, :], W_raw[:, k, :], nw[:, k:k + 1], None, ALU.mult)

            uT, u = a("uT", [P, KD, TB]), two("u", [P, NC, DM])
            uh, ul = two("uh", [P, KD, TB], F32R), two("ul", [P, KD, TB], F32R)
            xf, Cf, zs = two("xf", [P, NX, TB]), two("Cf", [DS, TB]), two("zs", [P, NC, DI])
            sp_x, sp_a, sp_y, sp_l, sp_d, sp_r = (a(n, [P, NC * NH]) for n in ("sp_x", "sp_a", "sp_y", "sp_l", "sp_d", "sp_r"))
            dt, dA = two("dt", [P, NC, NH]), two("dA", [P, NC, NH])
            dAh, dAl = two("dAh", [P, NC, NH], F32R), two("dAl", [P, NC, NH], F32R)
            dec = two("dec", [P, 3, NC, NH])
            aUh, aUl = a("aUh", [P, NH, CH], F32R), a("aUl", [P, NH, CH], F32R)
            L, M = a("L", [P, NH, CH]), a("M", [P, NH, CH])
            xt, xs, xd, xD = a("xt", [P, DI]), two("xs", [P, DI]), two("xd", [P, DI]), two("xD", [P, DI])
            Bt, CB = two("Bt", [P, DS]), a("CB", [P, CH])
            Sd = a("Sd", [DS, DI])
            yo, y1, y2, sq = a("yo", [P, DI]), a("y1", [P, DI]), a("y2", [P, DI]), a("sq", [P, DI])
            yT = a("yT", [P, DI // P, CH])
            ssq, ssn, rms = a("ssq", [P, 1]), a("ssn", [P, 1]), a("rms", [P, 1])
            r1, x1 = two("r1", [P, DM]), two("x1", [P, DM])
            st1, mv1, ve1, rs1 = two("st1", [P, 6]), two("mv1", [P, 2]), two("ve1", [P, 1]), two("rs1", [P, 1])
            pb = psum(pa, "pa")

            def loads(s, q):
                s.do(SP, "uT", lambda e, b: e.dma_start(
                    uT[:, :, :], d["uT"].rearrange("(k p) t -> p k t", p=P)[:, :, bass.ds(b.token(), TB)]), "proj.ul@-1", dmas=1)

            def load_u(s, q):
                s.do(SP, "u", lambda e, b: e.dma_start(
                    u[q][:, :, :], d["u"].rearrange("(n p) f -> p n f", p=P)[:, bass.ds(b.chunk(), NC), :]),
                    f"tail.r{NC - 1}@-2", dmas=1)

            def proj(s, q):
                s.do(VE, "uh", lambda e, b: e.tensor_copy(uh[q][:, :, :], uT[:, :, :]), "loads.uT", "dt@-2")
                s.do(PO, "ul", lambda e, b: e.tensor_tensor(ul[q][:, :, :], uT[:, :, :], uh[q][:, :, :].bitcast(F32), ALU.subtract), "uh", "dt@-2")
                for m in range(NX):
                    ws = slice(DI + m * P, DI + (m + 1) * P)
                    free = f"c{m - 2}" if m > 1 else "spx@-1" if m == (NX + NC) % 2 else f"zc{NC - 1}@-1"
                    s.do(PE, f"x{m}", lambda e, b, m=m, ws=ws: passes(e, pb[m % 2][:, :], [
                        (w[:, k, ws], x[:, k, :]) for w, x in ((Wh, uh[q]), (Wl, uh[q]), (Wh, ul[q])) for k in range(KD)]), "uh", "ul", free)
                    s.do(PO, f"halo{m}", lambda e, b, m=m: e.tensor_copy(raw[:, m, 0:TAPS - 1], raw[:, m, TB:TB + TAPS - 1]), f"t{m}_0@-1")
                    s.do(SA, f"ev{m}", lambda e, b, m=m: e.activation(raw[:, m, TAPS - 1:TB + TAPS - 1], pb[m % 2][:, :], ACT.Copy),
                         f"x{m}", f"halo{m}")
                    s.do(SA, f"c{m}", lambda e, b, m=m: e.activation(xf[q][:, m, :], pb[m % 2][:, :], ACT.Identity, bias=cb[:, m:m + 1],
                                                                     scale=cw[:, m, TAPS - 1:TAPS]), f"x{m}", f"pre.xt{NC - 1}@-2", f"pre.cb{NC - 1}@-2", "act.C@-2")
                    for j in range(TAPS - 2, -1, -1):
                        s.do(VE, f"t{m}_{j}", lambda e, b, m=m, j=j: e.scalar_tensor_tensor(
                            xf[q][:, m, :], raw[:, m, j:j + TB], cw[:, m, j:j + 1], xf[q][:, m, :], ALU.mult, ALU.add),
                            f"c{m}", f"t{m}_{j + 1}" if j < TAPS - 2 else f"ev{m}")
                for c in range(NC):
                    cs = slice(c * CH, (c + 1) * CH)
                    s.do(PE, f"z{c}", lambda e, b, c=c, cs=cs: passes(e, pb[(NX + c) % 2][:, :], [
                        (x[:, k, cs], w[:, k, 0:DI]) for w, x in ((Wh, uh[q]), (Wl, uh[q]), (Wh, ul[q])) for k in range(KD)]),
                        f"zc{c - 2}" if c > 1 else f"c{NX - 2 + c}")
                    s.do(SA, f"zc{c}", lambda e, b, c=c: e.activation(zs[q][:, c, :], pb[(NX + c) % 2][:, :], ACT.Copy),
                         f"z{c}", f"post.gate{c}@-2")

                def dt_mm(e, b):
                    for c in range(NC):
                        i = passes(e, pb[(NX + NC) % 2][:, c * NH:(c + 1) * NH], [
                            (x[:, k, c * CH:(c + 1) * CH], w[:, k, DIN - NH:DIN]) for w, x in ((Wh, uh[q]), (Wl, uh[q]), (Wh, ul[q])) for k in range(KD)])
                    return i
                s.do(PE, "dt", dt_mm, f"zc{NC - 2}")
                s.do(VE, "spx", lambda e, b: e.tensor_tensor(sp_x[:, :], pb[(NX + NC) % 2][:, 0:NC * NH],
                                                             dtb[:, :, :].rearrange("p c h -> p (c h)"), ALU.add), "dt", "spa@-1", "spr@-1")
                s.do(SA, "spa", lambda e, b: e.activation(sp_a[:, :], sp_x[:, :], ACT.Abs), "spx", "spy@-1")
                s.do(SA, "spy", lambda e, b: e.activation(sp_y[:, :], sp_a[:, :], ACT.Exp, scale=-1.0), "spa", "spe@-1")
                s.do(SA, "spl", lambda e, b: e.activation(sp_l[:, :], sp_y[:, :], ACT.Ln, bias=1.0), "spy", "sps@-1")
                s.do(VE, "spd", lambda e, b: e.tensor_scalar(sp_d[:, :], sp_y[:, :], 1.0, -1.0, ALU.add, ALU.add), "spy", "sps@-1")
                s.do(VE, "spr", lambda e, b: e.tensor_scalar(sp_r[:, :], sp_x[:, :], 0.0, None, ALU.max), "spx", "spt@-1")
                s.do(VE, "spe", lambda e, b: e.tensor_tensor(sp_d[:, :], sp_y[:, :], sp_d[:, :], ALU.subtract), "spd")
                s.do(VE, "sps", lambda e, b: e.tensor_tensor(sp_d[:, :], sp_l[:, :], sp_d[:, :], ALU.add), "spl", "spe")
                s.do(VE, "spt", lambda e, b: e.tensor_tensor(dt[q][:, :, :].rearrange("p c h -> p (c h)"), sp_r[:, :],
                                                             sp_d[:, :], ALU.add), "sps", "spr", f"pre.xs{NC - 1}@-2", "spA@-2")
                s.do(VE, "spA", lambda e, b: e.tensor_tensor(dA[q][:, :, :], dt[q][:, :, :], negA[:, :, :], ALU.mult), "spt", "pre.sums@-2")
                s.do(VE, "dAh", lambda e, b: e.tensor_copy(dAh[q][:, :, :], dA[q][:, :, :]), "spA", f"pre.auh{NC - 1}@-2")
                s.do(VE, "dAl", lambda e, b: e.tensor_tensor(dAl[q][:, :, :], dA[q][:, :, :], dAh[q][:, :, :].bitcast(F32), ALU.subtract),
                     "dAh", f"pre.aul{NC - 1}@-2")

            def act(s, q):
                for m in range(NX - 1, -1, -1):
                    s.do(SA, f"x{m}", lambda e, b, m=m: e.activation(xf[q][:, m, :], xf[q][:, m, :], ACT.Silu), f"proj.t{m}_0")
                    if m == NX - 1:
                        s.do(SP, "C", lambda e, b: e.dma_start(Cf[q][:, :], xf[q][DS:2 * DS, NX - 1, :]), f"x{NX - 1}",
                             f"post.off{NC - 1}@-2", f"pre.cb{NC - 1}@-2", dmas=1)
                for c in range(NC):
                    s.do(SA, f"z{c}", lambda e, b, c=c: e.activation(zs[q][:, c, :], zs[q][:, c, :], ACT.Silu), f"proj.zc{c}")

            def heads(x):
                return x.rearrange("p (h f) -> p h f", h=NH)

            def by_head(v, n, parts=P):
                return v.rearrange("p (h o) -> p h o", o=1).to_broadcast([parts, NH, n])

            def prev(name, c, back=1):
                return f"{name}{(c - back) % NC}@{(c - back) // NC}"

            def pre(s, q):
                def sums(e, b):
                    v = dA[q][:, :, :].rearrange("p c h -> p (c h)")
                    for n, w in enumerate((below, upper, ones)):
                        i = e.matmul(pb[3][:, 256 + n * NC * NH:256 + (n + 1) * NC * NH], w[:, :], v, start=True, stop=True)
                    return i
                s.do(PE, "sums", sums, "proj.spA", f"cbm{NC - 1}@-1")
                s.do(SA, "dec", lambda e, b: e.activation(dec[q][:, :, :, :].rearrange("p a c h -> p (a c h)"),
                                                          pb[3][:, 256:256 + 3 * NC * NH], ACT.Exp),
                     "sums", f"post.Sd{NC - 1}@-2", f"post.yo{NC - 1}@-2", f"xd{NC - 1}@-2")
                upper_all = upper[:, :].rearrange("p (o l) -> p o l", o=1).to_broadcast([P, NH, CH])
                for c in range(NC):
                    cs, r = slice(c * CH, (c + 1) * CH), c % 2
                    for part, src, dst in (("auh", dAh, aUh), ("aul", dAl, aUl)):
                        s.do(PO, f"{part}{c}", lambda e, b, c=c, src=src, dst=dst: e.tensor_tensor(
                            dst[:, :, :], by_head(src[q][:, c, :].bitcast(F32), CH), upper_all, ALU.mult), "proj.dAl", prev("seg1_", c))
                    def tx(e, b, cs=cs):
                        for m in range(NX - 1):
                            i = e.transpose(pb[2][:, m * P:(m + 1) * P], xf[q][:, m, cs], ident[:, :])
                        return i
                    s.do(PE, f"xt{c}", tx, "act.x0", prev("xtc", c), "tail." + prev("o", c, 3))
                    s.do(SA, f"xtc{c}", lambda e, b: e.activation(xt[:, :], pb[2][:, :], ACT.Copy), f"xt{c}", prev("xs", c), prev("xD", c))
                    s.do(PE, f"bt{c}", lambda e, b, cs=cs: e.transpose(pb[3][:, 0:P], xf[q][:, NX - 1, cs], ident[:, :]),
                         f"act.x{NX - 1}", prev("cbm", c), "dec")
                    s.do(PE, f"cb{c}", lambda e, b, cs=cs: e.matmul(pb[3][:, P:2 * P], xf[q][0:DS, NX - 1, cs], Cf[q][:, cs],
                                                                    start=True, stop=True), "act.C")
                    s.do(SA, f"btc{c}", lambda e, b, r=r: e.activation(Bt[r][:, :], pb[3][:, 0:DS], ACT.Copy), f"cb{c}", "post." + prev("new", c, 2))
                    s.do(VE, f"cbm{c}", lambda e, b: e.tensor_tensor(CB[:, :], pb[3][:, P:2 * P], upper[:, :], ALU.mult),
                         f"btc{c}", prev("M", c))
                    s.do(PO, f"xs{c}", lambda e, b, c=c, r=r: e.tensor_tensor(heads(xs[r][:, :]), heads(xt[:, :]), by_head(dt[q][:, c, :], HD), ALU.mult),
                         f"xtc{c}", "post." + prev("diag", c, 2), prev("xd", c, 2))
                    s.do(PO, f"xd{c}", lambda e, b, c=c, r=r: e.tensor_tensor(heads(xd[r][:, :]), heads(xs[r][:, :]), by_head(dec[q][:, 0, c, :], HD), ALU.mult),
                         f"xs{c}", "dec", "post." + prev("new", c, 2))
                    s.do(PO, f"xD{c}", lambda e, b, c=c, r=r: e.tensor_tensor(heads(xD[r][:, :]), heads(xt[:, :]), by_head(D1, HD), ALU.mult),
                         f"xtc{c}", "post." + prev("y1_", c, 2))
                    for g in (0, 1):
                        hs = slice(g * NH // 2, (g + 1) * NH // 2)
                        s.do(PE, f"seg{g}_{c}", lambda e, b, g=g, hs=hs: passes(e, pb[4 + g][:, :], [
                            (belowr[:, :], x[:, hs, :].rearrange("p h l -> p (h l)")) for x in (aUh, aUl)]), f"auh{c}", f"aul{c}", prev(f"L{g}_", c))
                        s.do(SA, f"L{g}_{c}", lambda e, b, g=g, hs=hs: e.activation(
                            L[:, hs, :].rearrange("p h l -> p (h l)"), pb[4 + g][:, :], ACT.Exp), f"seg{g}_{c}", prev("M", c))
                    s.do(VE, f"M{c}", lambda e, b: e.tensor_tensor(
                        M[:, :, :], L[:, :, :], CB[:, :].rearrange("p (o l) -> p o l", o=1).to_broadcast([P, NH, CH]), ALU.mult),
                        f"L1_{c}", f"cbm{c}", "post." + prev("diag", c))

            def post(s, q):
                for c in range(NC):
                    cs, r = slice(c * CH, (c + 1) * CH), c % 2
                    s.do(PE, f"off{c}", lambda e, b, cs=cs: e.matmul(pb[6][:, :], Cf[q][:, cs], S[:, :], start=True, stop=True),
                         "act.C", prev("S", c), prev("y1a", c))
                    s.do(PE, f"new{c}", lambda e, b, r=r: e.matmul(pb[7][0:DS, :], Bt[r][:, :], xd[r][:, :], start=True, stop=True),
                         f"pre.btc{c}", f"pre.xd{c}", "tail." + prev("r", c))
                    s.do(VE, f"yo{c}", lambda e, b, c=c: e.tensor_tensor(heads(yo[:, :]), heads(pb[6][:, :]), by_head(dec[q][:, 1, c, :], HD), ALU.mult),
                         f"off{c}", "pre.dec", prev("y1_", c))

                    def diag(e, b, r=r):
                        for h in range(NH):
                            i = e.matmul(pb[6][:, h * HD:(h + 1) * HD], M[:, h, :], xs[r][:, h * HD:(h + 1) * HD], start=True, stop=True)
                        return i
                    s.do(PE, f"diag{c}", diag, f"pre.M{c}", f"pre.xs{c}", f"yo{c}")
                    s.do(VE, f"Sd{c}", lambda e, b, c=c: e.tensor_tensor(heads(Sd[:, :]), heads(S[:, :]), by_head(dec[q][0:DS, 2, c, :], HD, DS), ALU.mult),
                         "pre.dec", prev("S", c))
                    s.do(VE, f"S{c}", lambda e, b: e.tensor_tensor(S[:, :], Sd[:, :], pb[7][0:DS, :], ALU.add), f"Sd{c}", f"new{c}", f"off{c}")
                    s.do(PO, f"y1_{c}", lambda e, b, r=r: e.tensor_tensor(y1[:, :], yo[:, :], xD[r][:, :], ALU.add), f"yo{c}", f"pre.xD{c}", prev("y1a", c))
                    s.do(VE, f"y1a{c}", lambda e, b: e.tensor_tensor(y2[:, :], y1[:, :], pb[6][:, :], ALU.add), f"y1_{c}", f"diag{c}", prev("tyT", c), prev("sq", c))
                    s.do(VE, f"gate{c}", lambda e, b, c=c: e.tensor_tensor(y2[:, :], y2[:, :], zs[q][:, c, :], ALU.mult), f"y1a{c}", f"act.z{c}")

                    def ty(e, b):
                        for m in range(DI // P):
                            i = e.transpose(pb[7][:, m * P:(m + 1) * P], y2[:, m * P:(m + 1) * P], ident[:, :])
                        return i
                    s.do(PE, f"tyT{c}", ty, f"gate{c}", f"S{c}")
                    s.do(SA, f"yT{c}", lambda e, b: e.activation(yT[:, :, :].rearrange("p k l -> p (k l)"), pb[7][:, :], ACT.Copy),
                         f"tyT{c}", "tail." + prev("op", c))
                    s.do(SA, f"sq{c}", lambda e, b: e.activation(sq[:, :], y2[:, :], ACT.Square, accum_out=ssq[:, :]), f"gate{c}", prev("ssn", c), prev("sq", c))
                    s.do(VE, f"ssn{c}", lambda e, b: e.tensor_scalar(ssn[:, :], ssq[:, :], 1.0 / DI, EPS, ALU.mult, ALU.add), f"sq{c}", prev("rms", c))
                    s.do(PO, f"rms{c}", lambda e, b: e.tensor_tensor(rms[:, :], ssn[:, :], mhalf[:, 0:1], ALU.pow), f"ssn{c}", "tail." + prev("r", c))

            def tail(s, q):
                for c in range(NC):
                    r = c % 2

                    def op(e, b):
                        for k in range(DI // P):
                            i = e.matmul(pb[7][:, 0:DM], yT[:, k, :], W_out[:, k, :], start=(k == 0), stop=(k == DI // P - 1))
                        return i
                    s.do(PE, f"op{c}", op, f"post.yT{c}")
                    s.do(VE, f"r{c}", lambda e, b, c=c, r=r: e.scalar_tensor_tensor(r1[r][:, :], pb[7][:, 0:DM], rms[:, 0:1], u[q][:, c, :], ALU.mult, ALU.add),
                         f"op{c}", f"post.rms{c}", "load_u.u", prev("n", c, 2))
                    s.do(VE, f"st{c}", lambda e, b, r=r: e.bn_stats(st1[r][:, :], r1[r][:, :]), f"r{c}", prev("mv", c, 2))
                    s.do(VE, f"mv{c}", lambda e, b, r=r: e.bn_aggr(mv1[r][:, :], st1[r][:, :]), f"st{c}", prev("n", c, 2), alone=True)
                    s.do(VE, f"ve{c}", lambda e, b, r=r: e.tensor_scalar(ve1[r][:, :], mv1[r][:, 1:2], EPS, None, ALU.add), f"mv{c}", prev("rs", c, 2))
                    s.do(PO, f"rs{c}", lambda e, b, r=r: e.tensor_tensor(rs1[r][:, :], ve1[r][:, :], mhalf[:, 0:1], ALU.pow), f"ve{c}", prev("n", c, 2))
                    s.do(VE, f"n{c}", lambda e, b, r=r: e.tensor_scalar(x1[r][:, :], r1[r][:, :], mv1[r][:, 0:1], rs1[r][:, 0:1], ALU.subtract, ALU.mult),
                         f"rs{c}", prev("tx", c, 2))

                    def tx1(e, b, r=r):
                        for k in range(KD):
                            i = e.transpose(pb[2][:, k * P:(k + 1) * P], x1[r][:, k * P:(k + 1) * P], ident[:, :])
                        return i
                    s.do(PE, f"tx{c}", tx1, f"n{c}", "pre." + prev("xtc", c, -2))
                    s.do(SA, f"o{c}", lambda e, b, c=c: e.activation(
                        x1T[:, :, bass.ds(b.token() + c * CH, CH)], pb[2][:, 0:DM].rearrange("p (k t) -> p k t", k=KD), ACT.Copy), f"tx{c}")

            for name, fn in (("loads", loads), ("load_u", load_u), ("proj", proj), ("act", act), ("pre", pre), ("post", post), ("tail", tail)):
                Stage(top, name, fn)
            plan = [("loads", 0.3, 0.4), ("load_u", 1.6, 1.7), ("proj", 1, 1.9), ("act", 2, 2 + 1e-6), ("pre", 2.05, 3), ("post", 2.3, 3.25), ("tail", 2.5, 3.45)]
            with nc.Block() as block:
                block.sync(lambda e: top.run(SP, e, plan))
                block.tensor(lambda e: top.run(PE, e, plan))
                block.vector(lambda e: top.run(VE, e, plan))
                block.gpsimd(lambda e: top.run(PO, e, plan))
                block.scalar(lambda e: top.run(SA, e, plan))


        mean, g1, g2 = sb("mean", [P, KD]), sb("g1", [P, 1]), sb("g2", [64, 1])
        gt, k0 = sb("gt", [P, 1]), sb("k0", [P, 1])

        def global_net(dequantise):
            q1, s1, f1, q2, s2, f2 = dequantise
            gv, gp, ga, ld, aa, pv = (top.sem(n) for n in ("gv", "gp", "ga", "ld", "aa", "pv"))
            loaded = [(w_xz, rows(d["c_w_inT"])), (w_dt, rows(d["c_w_dtT"])), (w_o, rows(d["c_w_outT"])), (q1, rows(d["f_q1"])), (q2, rows(d["f_q2"]))]
            loaded += [(s1[:, k, :], d["f_s1"][k:k + 1, :].to_broadcast([P, FF])) for k in range(KD)]
            loaded += [(s2[:, k, :], d["f_s2"][k:k + 1, :].to_broadcast([P, DM])) for k in range(KF)]
            loaded += [(w_bc[:, :, g, m, :], rows(d[w + "T"])) for g in range(3) for m, w in enumerate(("c_w_B", "c_w_C"))]
            with ExitStack() as pg, nc.Block() as block:
                pb = psum(pg, "pg")

                @block.sync
                def _(e):
                    for dst, src in loaded:
                        e.dma_start(dst[tuple(slice(None) for _ in dst.shape)], src).then_inc(ld, DMAS)
                    e.wait_ge(ld, DMAS * len(loaded))

                @block.gpsimd
                def _(e):
                    e.memset(sel[:, :, :], 0.0).then_inc(aa, 1)
                    for g in range(3):
                        e.wait_ge(aa, g + 1)
                        e.affine_select(out=sel[:, :, :], in_=sel[:, :, :], compare_op=ALU.not_equal, fill=1.0,
                                        base=-2 * NS * g, pattern=[[-1, 2 * NS], [0, P]], channel_multiplier=1).then_inc(aa, 1)

                @block.vector
                def _(e):
                    for k in range(KD):
                        e.reduce_sum(mean[:, k:k + 1], x1T[:, k, :], mybir.AxisListType.X).then_inc(gv, 1)
                    e.tensor_scalar(slope[:, :], rng, 0.3, None, ALU.mult).then_inc(gv, 1)
                    e.wait_ge(gv, 3)
                    e.tensor_tensor(slope[:, :], slope[:, :], sign[:, :], ALU.mult).then_inc(gv, 1)
                    e.wait_ge(ga, 3)
                    e.tensor_scalar(k0[:, :], gt[:, :], 0.7, None, ALU.mult).then_inc(gv, 1)
                    e.wait_ge(gv, 5)
                    e.tensor_scalar(shift[:, :], k0[:, :], rng[:, 0:1], 0.1, ALU.mult, ALU.add).then_inc(gv, 1)
                    e.wait_ge(gv, 6)
                    e.tensor_tensor(k0[:, :], shift[:, :], sign[:, :], ALU.mult).then_inc(gv, 1)
                    e.wait_ge(gv, 7)
                    e.tensor_copy(shift[:, :], k0[:, :])
                    e.wait_ge(ld, DMAS * len(loaded))
                    e.tensor_scalar(f1[:, :, :], q1[:, :, :], -128.0, None, ALU.add).then_inc(pv, 1)
                    e.tensor_scalar(f2[:, :, :], q2[:, :, :], -128.0, None, ALU.add).then_inc(pv, 1)
                    e.tensor_scalar(hb2[:, :], vec_at["f_b2"], 0.5, None, ALU.mult)
                    e.wait_ge(ga, 4)
                    e.tensor_scalar(A[:, :, :], A[:, :, :], -1.0, None, ALU.mult)
                    e.wait_ge(pv, 2)
                    e.tensor_tensor(w1[:, :, :], f1[:, :, :], s1[:, :, :], ALU.mult)
                    e.tensor_tensor(w2[:, :, :], f2[:, :, :], s2[:, :, :], ALU.mult)

                @block.tensor
                def _(e):
                    e.wait_ge(gv, 2)
                    for k in range(KD):
                        i = e.matmul(pb[0][:, 0:1], gc_w1[:, k, :], mean[:, k:k + 1], start=(k == 0), stop=(k == KD - 1))
                    i.then_inc(gp, 1)
                    e.wait_ge(ga, 1)
                    e.matmul(pb[1][0:64, 0:1], gc_w2[:, :], g1[:, :], start=True, stop=True).then_inc(gp, 1)
                    e.wait_ge(ga, 2)
                    e.matmul(pb[2][:, 0:1], gw3[:, :], g2[:, :], start=True, stop=True).then_inc(gp, 1)

                @block.scalar
                def _(e):
                    e.wait_ge(gp, 1)
                    e.activation(g1[:, :], pb[0][:, 0:1], ACT.Gelu, bias=gc_b1[:, 0:1], scale=1.0 / T).then_inc(ga, 1)
                    e.wait_ge(gp, 2)
                    e.activation(g2[:, :], pb[1][0:64, 0:1], ACT.Gelu, bias=gc_b2[0:64, :]).then_inc(ga, 1)
                    e.wait_ge(gp, 3)
                    e.activation(gt[:, :], pb[2][:, 0:1], ACT.Tanh, bias=hg3[:, 0:1], scale=0.5).then_inc(ga, 1)
                    e.activation(A[:, :, :].rearrange("p k n -> p (k n)"), vec_at["c_A_log"], ACT.Exp).then_inc(ga, 1)

        def vec(x):
            return x.rearrange("p k t -> p (k t)")

        w_xz, w_dt, w_bc, w_o = sb("w_xz", [P, KD, 2 * DM]), sb("w_dt", [P, KD, DM]), sb("w_bc", [P, KD, 3, 2, NS]), sb("w_o", [P, KD, DM])
        b_in, b_dt, b_bc, Dc, lg, lb, b1 = (vec_at[n] for n in ("c_b_in", "c_b_dt", "c_b_bc", "c_D", "f_gamma", "f_beta", "f_b1"))
        gam, bet, b_o = (vec_at[n] for n in ("c_gamma", "c_beta", "c_b_out"))
        A = sb("A", [P, KD, NS])
        w1, w2, hb2 = sb("w1", [P, KD, FF]), sb("w2", [P, KF, DM]), sb("hb2", [P, DM])
        sel = sb("sel", [3 * 2 * NS, 2 * NS, P], BF16)

        x2_tokens = x2_dram.rearrange("(n p) f -> p n f", p=P)
        with ExitStack() as pc:
            def t(name, shape, dt=F32):
                return sb(name, shape, dt, within=pc)

            def three(name, shape):
                return [t(f"{name}{y}", shape) for y in range(3)]

            with ExitStack() as pq:
                q1, s1 = sb("q1", [P, KD, FF], I32, within=pq), sb("s1", [P, KD, FF], within=pq)
                q2, s2 = sb("q2", [P, KF, DM], I32, within=pq), sb("s2", [P, KF, DM], within=pq)
                f1, f2 = sb("f1", [P, KD, FF], within=pq), sb("f2", [P, KF, DM], within=pq)
                global_net(dequantise=(q1, s1, f1, q2, s2, f2))

            o = [three(f"o{q}_", [P, KD, TB]) for q in (0, 1)]
            h1, h2, h3 = three("h1", [P, KD, TB]), three("h2", [P, TB]), three("h3", [64, TB])
            cS, tw = three("cS", [P, TB]), three("tw", [P, KD, TB])
            x2s = [t(f"x2s{q}", [P, NC, DM]) for q in (0, 1)]
            ln2 = [t(n, sh) for n, sh in (("st2", [P, NC, 6]), ("mv2", [P, NC, 2]), ("ve2", [P, NC]), ("rs2", [P, NC]))]
            pb = psum(pc, "pc")

            def cycle(y):
                def build(s, q):
                    src = (lambda b, k: x1T[:, k, bass.ds(b.token(), TB)]) if y == 0 else (lambda b, k: o[q][y - 1][:, k, :])
                    dst, b0, b1_ = o[q][y], pb[2 * y], pb[2 * y + 1]
                    ready = [f"cycle{y - 1}.add", f"cycle{y - 1}.ad"] if y else []
                    for m in range(KD):
                        bank = (b0, b1_)[m]
                        s.do(PE, f"m1_{m}", lambda e, b, m=m, bank=bank: passes(e, bank[:, :], [
                            (cn_w1[:, k, m * P:(m + 1) * P], src(b, k)) for k in range(KD)]), *ready, ("a2@-1", "ta@-1")[m])
                        s.do(SA, f"a1_{m}", lambda e, b, m=m, bank=bank: e.activation(h1[y][:, m, :], bank[:, :], ACT.Gelu, bias=cn_b1[:, m:m + 1]),
                             f"m1_{m}", "m2@-1")
                    s.do(PE, "m2", lambda e, b: passes(e, b0[:, :], [(cn_w2[:, k, :], h1[y][:, k, :]) for k in range(KD)]), "a1_1", "a1_0")
                    s.do(SA, "a2", lambda e, b: e.activation(h2[y][:, :], b0[:, :], ACT.Gelu, bias=cn_b2[:, 0:1]), "m2", "m3@-1")
                    s.do(PE, "m3", lambda e, b: e.matmul(b1_[0:64, :], cn_w3[:, :], h2[y][:, :], start=True, stop=True), "a2")
                    s.do(SA, "a3", lambda e, b: e.activation(h3[y][:, :], b1_[0:64, :], ACT.Gelu, bias=cn_b3[0:64, :]), "m3", "m4@-1")
                    s.do(PE, "m4", lambda e, b: e.matmul(b1_[:, :], cw4[:, :], h3[y][:, :], start=True, stop=True), "a3")
                    s.do(SA, "ta", lambda e, b: e.activation(cS[y][:, :], b1_[:, :], ACT.Tanh, bias=hb4[:, 0:1], scale=0.5), "m4", "t1@-1")
                    s.do(VE, "cs", lambda e, b: e.tensor_scalar(cS[y][:, :], cS[y][:, :], slope[:, 0:1], shift[:, 0:1], ALU.mult, ALU.add), "ta")
                    for k in range(KD):
                        s.do(VE, f"t{k}", lambda e, b, k=k: e.tensor_tensor(tw[y][:, k, :], cS[y][:, :], src(b, 1 - k), ALU.mult), "cs", "add@-1", "ad@-1")
                    free = f"cycle{y + 1}.add@-2" if y < 2 else f"norm.bt{NC - 1}@-2"
                    s.do(PO, "ad", lambda e, b: e.tensor_tensor(dst[:, 0, :], src(b, 0), tw[y][:, 0, :], ALU.add), "t0", free)
                    s.do(PO, "add", lambda e, b: e.tensor_tensor(dst[:, 1, :], src(b, 1), tw[y][:, 1, :], ALU.subtract), "t1", free)
                    if y == 2:
                        s.do(PO, "res", lambda e, b: e.tensor_tensor(dst[:, :, :], dst[:, :, :], x1T[:, :, bass.ds(b.token(), TB)], ALU.add), "add", "ad")
                return build

            def norm(s, q):
                for c in range(NC):
                    def tr(e, b, c=c):
                        for k in range(KD):
                            i = e.transpose(pb[6 + c // 2][:, (c % 2) * DM + k * P:(c % 2) * DM + (k + 1) * P], o[q][2][:, k, c * CH:(c + 1) * CH], ident[:, :])
                        return i
                    s.do(PE, f"bt{c}", tr, "cycle2.res", f"bTe{NC - 2 + c // 2}@-1")
                layer_norm(s, "l2", lambda c: pb[6 + c // 2][:, (c % 2) * DM:(c % 2 + 1) * DM], lambda c: x2s[q][:, c, :], *ln2,
                           lambda c: [f"bt{c | 1}"], ["store@-2", f"bT{NC - 1}@-2"])
                s.do(SP, "store", lambda e, b: e.dma_start(x2_tokens[:, bass.ds(b.chunk(), NC), :], x2s[q][:, :, :]), f"l2_n{NC - 1}", dmas=1)
                for c in range(NC):
                    bank = pb[6 + c % 2]

                    def tr(e, b, c=c, bank=bank):
                        for k in range(KD):
                            i = e.transpose(bank[:, k * P:(k + 1) * P], x2s[q][:, c, k * P:(k + 1) * P], ident[:, :])
                        return i
                    s.do(PE, f"bT{c}", tr, f"l2_n{NC - 1}", *([f"bTe{c - 2}"] if c > 1 else []))
                    s.do(SA, f"bTe{c}", lambda e, b, c=c, bank=bank: e.activation(
                        x1T[:, :, bass.ds(b.token() + c * CH, CH)], bank[:, 0:DM].rearrange("p (k t) -> p k t", k=KD), ACT.Copy), f"bT{c}", "cycle2.res")

            for y in range(3):
                Stage(top, f"cycle{y}", cycle(y))
            Stage(top, "norm", norm)
            plan = [("cycle0", 0, 0.95), ("cycle1", 1, 1.95), ("cycle2", 2, 2.95), ("norm", 3, 3.95)]
            with nc.Block() as block:
                def sp(e):
                    top.run(SP, e, plan)
                    for q in (0, 1):
                        e.wait_ge(top.stages["norm"].sem["store"][q], DMAS * (NB // 2 + 1))
                block.sync(sp)
                block.tensor(lambda e: top.run(PE, e, plan))
                block.vector(lambda e: top.run(VE, e, plan))
                block.gpsimd(lambda e: top.run(PO, e, plan))
                block.scalar(lambda e: top.run(SA, e, plan))

        x2T = x1T
        with ExitStack() as pd:
            def t(name, shape, dt=F32):
                return sb(name, shape, dt, within=pd)

            def many(name, shape, n=2, dt=F32):
                return [t(f"{name}{i}", shape, dt) for i in range(n)]

            lnb = [[t(f"{n}_{i}", sh) for n, sh in (("st", [P, NC, 6]), ("mv", [P, NC, 2]), ("ve", [P, NC]), ("rs", [P, NC]))] for i in range(4)]
            x2 = t("x2", [P, NC, DM])
            xc, zc, gated = t("xc", [P, KD, TB]), many("zc", [P, KD, TB]), t("gated", [P, KD, TB])
            va, vl, vd = (t(n, [P, KD, TB]) for n in ("va", "vl", "vd"))
            dtc, uc, acc = many("dtc", [P, KD, TB]), many("uc", [P, KD, TB]), many("acc", [P, KD, TB])
            bcf, parts = t("bcf", [96, TB]), many("parts", [96, TB], dt=BF16)
            h0 = t("h0", [P, NS, KD])
            av, bv, gv_ = many("av", [P, KD, TB], AHEAD), many("bv", [P, KD, TB]), many("gv", [P, KD, TB])
            xl, x3 = t("xl", [P, NC, DM]), many("x3_", [P, NC, DM])
            xn, nT, f_h, x3b = xl, t("nT", [P, KD, TB]), t("f_h", [P, KF, TB]), t("x3b", [P, NC, DM])
            pb = psum(pd, "pd")
            p_in, p_out, p_ffn = pb[0], pb[1], pb[2:4]

            def load_x2(s, q):
                s.do(SP, "x2", lambda e, b: e.dma_start(x2[:, :, :], x2_tokens[:, bass.ds(b.chunk(), NC), :]), "scan_out.xl_b@-1", dmas=1)

            def scan_in(s, q):
                def project(m):
                    return lambda e, b: passes(e, p_in[:, :], [(w_xz[:, k, m * P:(m + 1) * P], x2T[:, k, bass.ds(b.token(), TB)]) for k in range(KD)])
                for m in range(KD):
                    s.do(PE, f"x{m}", project(m), f"xe{m - 1}" if m else f"ze{KD - 1}@-1")
                    s.do(SA, f"xe{m}", lambda e, b, m=m: e.activation(xc[:, m, :], p_in[:, :], ACT.Identity, bias=b_in[:, m:m + 1]),
                         f"x{m}", "u@-1", "bc@-1")
                for m in range(KD):
                    s.do(PE, f"d{m}", lambda e, b, m=m: passes(e, p_in[:, :], [(w_dt[:, k, m * P:(m + 1) * P], xc[:, k, :]) for k in range(KD)]),
                         f"xe{KD - 1}", *([f"vr{m - 1}"] if m else []))
                    s.do(SA, f"va{m}", lambda e, b, m=m: e.activation(va[:, m, :], p_in[:, :], ACT.Abs, bias=b_dt[:, m:m + 1]), f"d{m}", "ve@-1")
                    s.do(SA, f"vr{m}", lambda e, b, m=m: e.activation(dtc[q][:, m, :], p_in[:, :], ACT.Relu, bias=b_dt[:, m:m + 1]), f"d{m}",
                         f"core.a{NS - 1}_1@-2", "u@-2")
                s.do(PE, "bc", lambda e, b: passes(e, p_in[0:96, :], [
                    (w_bc[:, k, :, :, :].rearrange("p g m n -> p (g m n)"), xc[:, k, :]) for k in range(KD)]), f"vr{KD - 1}")
                s.do(SA, "bce", lambda e, b: e.activation(bcf[:, :], p_in[0:96, :], ACT.Identity, bias=b_bc[0:96, :]), "bc", "p3@-1")
                s.do(SA, "vy", lambda e, b: e.activation(vec(va[:, :, :]), vec(va[:, :, :]), ACT.Exp, scale=-1.0), f"va{KD - 1}", "va0")
                s.do(SA, "vl", lambda e, b: e.activation(vec(vl[:, :, :]), vec(va[:, :, :]), ACT.Ln, bias=1.0), "vy", "vs@-1")
                s.do(VE, "vd", lambda e, b: e.tensor_scalar(vec(vd[:, :, :]), vec(va[:, :, :]), 1.0, -1.0, ALU.add, ALU.add), "vy", "vs@-1")
                s.do(VE, "ve", lambda e, b: e.tensor_tensor(vec(vd[:, :, :]), vec(va[:, :, :]), vec(vd[:, :, :]), ALU.subtract), "vd")
                s.do(PO, "vs", lambda e, b: e.tensor_tensor(vec(vl[:, :, :]), vec(vl[:, :, :]), vec(vd[:, :, :]), ALU.add), "vl", "ve")
                s.do(VE, "ph", lambda e, b: e.tensor_copy(parts[q][:, :], bcf[:, :]), "bce", f"core.C{NS - 1}@-2", "p3@-2")
                s.do(VE, "pr", lambda e, b: e.tensor_tensor(bcf[:, :], bcf[:, :], parts[q][:, :], ALU.subtract), "ph")
                s.do(VE, "vt", lambda e, b: e.tensor_tensor(vec(dtc[q][:, :, :]), vec(dtc[q][:, :, :]), vec(vl[:, :, :]), ALU.add), "vs", f"vr{KD - 1}", "vr0")
                s.do(VE, "p1", lambda e, b: e.tensor_copy(parts[q][32:64, :], bcf[32:64, :]), "pr")
                s.do(VE, "p2", lambda e, b: e.tensor_copy(parts[q][64:96, :], bcf[64:96, :]), "pr")
                s.do(PO, "u", lambda e, b: e.tensor_tensor(vec(uc[q][:, :, :]), vec(dtc[q][:, :, :]), vec(xc[:, :, :]), ALU.mult), "vt", f"core.b{NS - 1}@-2")
                s.do(VE, "pl", lambda e, b: e.tensor_tensor(bcf[64:96, :], bcf[64:96, :], parts[q][64:96, :], ALU.subtract), "p2")
                s.do(VE, "p3", lambda e, b: e.tensor_copy(parts[q][64:96, :], bcf[64:96, :]), "pl", "p1")
                for m in range(KD):
                    s.do(SA, f"dx{m}", lambda e, b, m=m: e.activation(acc[q][:, m, :], xc[:, m, :], ACT.Copy, scale=Dc[:, m:m + 1]),
                         f"xe{m}", "scan_out.gate@-2")
                for m in range(KD):
                    s.do(PE, f"z{m}", project(KD + m), f"ze{m - 1}" if m else "bce")
                    s.do(SA, f"ze{m}", lambda e, b, m=m: e.activation(zc[q][:, m, :], p_in[:, :], ACT.Identity, bias=b_in[:, KD + m:KD + m + 1]),
                         f"z{m}", "scan_out.gate@-2")

            def scan_z(s, q):
                s.do(SA, "z", lambda e, b: e.activation(vec(zc[q][:, :, :]), vec(zc[q][:, :, :]), ACT.Silu), "scan_in.ze1", "scan_in.ze0")

            def core(s, q):
                def back(label, n, by=2):
                    return f"{label.format((n - by) % NS)}@{(n - by) // NS}"

                def wide(x):
                    return x.rearrange("p (o t) -> p o t", o=1).to_broadcast([P, KD, TB])

                def decay(n):
                    for k in range(KD):
                        s.do(SA, f"a{n}_{k}", lambda e, b, n=n, k=k: e.activation(av[n % AHEAD][:, k, :], dtc[q][:, k, :], ACT.Exp, scale=A[:, k, n:n + 1]),
                             "scan_in.vt", back("s{}_%d" % k, n, AHEAD))
                for n in range(NS):
                    i2 = n % 2
                    s.do(PE, f"B{n}", lambda e, b, n=n, i2=i2: e.matmul(pb[4 + i2][:, :], sel[:, n, :], parts[q][:, :], start=True, stop=True),
                         "scan_in.p3", back("b{}", n))
                    s.do(PE, f"C{n}", lambda e, b, n=n, i2=i2: e.matmul(pb[6 + i2][:, :], sel[:, NS + n, :], parts[q][:, :], start=True, stop=True), back("g{}", n))
                    decay(n)
                    s.do(VE, f"b{n}", lambda e, b, i2=i2: e.tensor_tensor(bv[i2][:, :, :], uc[q][:, :, :], wide(pb[4 + i2][:, :]), ALU.mult),
                         "scan_in.u", f"B{n}", back("g{}", n), back("hs{}", n))
                    for k in range(KD):
                        s.do(VE, f"s{n}_{k}", lambda e, b, n=n, k=k, i2=i2: e.tensor_tensor_scan(
                            bv[i2][:, k, :], av[n % AHEAD][:, k, :], bv[i2][:, k, :], h0[:, n, k:k + 1], ALU.mult, ALU.add),
                            f"b{n}", f"a{n}_{k}", f"hs{n}@-1")
                    s.do(PO, f"hs{n}", lambda e, b, n=n, i2=i2: e.tensor_copy(h0[:, n, :], bv[i2][:, :, TB - 1]), f"s{n}_1")
                    s.do(VE, f"g{n}", lambda e, b, i2=i2: e.tensor_tensor(gv_[i2][:, :, :], bv[i2][:, :, :], wide(pb[6 + i2][:, :]), ALU.mult),
                         f"s{n}_1", f"C{n}", back("+{}", n))
                    s.do(PO, f"+{n}", lambda e, b, i2=i2: e.tensor_tensor(vec(acc[q][:, :, :]), vec(acc[q][:, :, :]), vec(gv_[i2][:, :, :]), ALU.add),
                         f"g{n}", f"+{n - 1}" if n else "scan_in.dx1")

            def scan_out(s, q):
                s.do(VE, "gate", lambda e, b: e.tensor_tensor(vec(gated[:, :, :]), vec(acc[q][:, :, :]), vec(zc[q][:, :, :]), ALU.mult),
                     f"core.+{NS - 1}", "scan_z.z", f"o{NC - 1}@-1")
                s.do(PO, "xb", lambda e, b: e.tensor_tensor(xl[:, :, :], x2[:, :, :], every(b_o), ALU.add), "load_x2.x2", f"l4_n{NC - 1}@-1", f"ffn_in.fT{NC - 1}@-1")
                for c in range(NC):
                    s.do(PE, f"o{c}", lambda e, b, c=c: passes(e, p_out[:, 0:DM], [
                        (gated[:, k, c * CH:(c + 1) * CH], w_o[:, k, :]) for k in range(KD)]), "gate", f"pre{c - 1}" if c else f"pre{NC - 1}@-1")
                    s.do(VE, f"pre{c}", lambda e, b, c=c: e.tensor_tensor(xl[:, c, :], p_out[:, 0:DM], xl[:, c, :], ALU.add), f"o{c}", "xb")
                layer_norm(s, "l3", lambda c: xl[:, c, :], lambda c: xl[:, c, :], *lnb[0], lambda c: [f"pre{c}"], [f"pre{NC - 1}"])
                s.do(PO, "xl_g", lambda e, b: e.tensor_tensor(xl[:, :, :], xl[:, :, :], every(gam), ALU.mult), f"l3_n{NC - 1}")
                s.do(PO, "xl_a", lambda e, b: e.tensor_tensor(xl[:, :, :], xl[:, :, :], every(bet), ALU.add), "xl_g")
                s.do(PO, "xl_b", lambda e, b: e.tensor_tensor(xl[:, :, :], xl[:, :, :], x2[:, :, :], ALU.add), "xl_a")
                layer_norm(s, "l4", lambda c: xl[:, c, :], lambda c: x3[q][:, c, :], *lnb[1], lambda c: ["xl_b"], ["ffn_in.l5_n3@-2", "ffn_out.xb@-2"])

            def every(v):
                return v.rearrange("p (o f) -> p o f", o=1).to_broadcast([P, NC, DM])

            def ffn_in(s, q):
                layer_norm(s, "l5", lambda c: x3[q][:, c, :], lambda c: xn[:, c, :], *lnb[2], lambda c: [f"scan_out.l4_n{NC - 1}"], [f"fT{NC - 1}@-1"])
                for c in range(NC):
                    bank = p_ffn[c % 2]

                    def tr(e, b, c=c, bank=bank):
                        for k in range(KD):
                            i = e.transpose(bank[:, k * P:(k + 1) * P], xn[:, c, k * P:(k + 1) * P], ident[:, :])
                        return i
                    s.do(PE, f"fT{c}", tr, f"l5_n{NC - 1}", f"fTe{c - 2}_1" if c > 1 else f"ffn_out.w{NC - 2 + c}@-1")
                    for k in range(KD):
                        s.do(SA, f"fTe{c}_{k}", lambda e, b, c=c, k=k, bank=bank: e.activation(
                            nT[:, k, c * CH:(c + 1) * CH], bank[:, k * P:(k + 1) * P], ACT.Identity, bias=lb[:, k:k + 1], scale=lg[:, k:k + 1]),
                            f"fT{c}", f"ffn_up.u{KF - 1}@-1")

            def ffn_up(s, q):
                for m in range(KF):
                    bank = p_ffn[m % 2]
                    s.do(PE, f"u{m}", lambda e, b, m=m, bank=bank: passes(e, bank[:, :], [
                        (w1[:, k, m * P:(m + 1) * P], nT[:, k, :]) for k in range(KD)]), f"ffn_in.fTe{NC - 1}_1", *([f"ue{m - 2}"] if m > 1 else []))
                    s.do(SA, f"ue{m}", lambda e, b, m=m, bank=bank: e.activation(f_h[:, m, :], bank[:, :], ACT.Identity, bias=b1[:, m:m + 1]),
                         f"u{m}", f"ffn_out.o{NC - 1}@-1")

            def ffn_act(s, q):
                for g in (0, 1):
                    s.do(SA, f"si{g}", lambda e, b, g=g: e.activation(vec(f_h[:, g * KF // 2:(g + 1) * KF // 2, :]), vec(f_h[:, g * KF // 2:(g + 1) * KF // 2, :]), ACT.Silu),
                         f"ffn_up.ue{KF - 1}")

            def ffn_out(s, q):
                s.do(PO, "xa", lambda e, b: e.tensor_tensor(x3b[:, :, :], x3[q][:, :, :], every(hb2[:, :]), ALU.add), f"scan_out.l4_n{NC - 1}", "store@-1")
                s.do(PO, "xb", lambda e, b: e.tensor_tensor(x3b[:, :, :], x3b[:, :, :], x3[q][:, :, :], ALU.add), "xa")
                for c in range(NC):
                    bank = p_ffn[c % 2]
                    s.do(PE, f"o{c}", lambda e, b, c=c, bank=bank: passes(e, bank[:, 0:DM], [
                        (f_h[:, k, c * CH:(c + 1) * CH], w2[:, k, :]) for k in range(KF)]), "ffn_act.si1", *([f"w{c - 2}"] if c > 1 else []))
                    s.do(VE, f"w{c}", lambda e, b, c=c, bank=bank: e.scalar_tensor_tensor(x3b[:, c, :], bank[:, 0:DM], 0.5, x3b[:, c, :], ALU.mult, ALU.add), f"o{c}", "xb")
                layer_norm(s, "l6", lambda c: x3b[:, c, :], lambda c: x3b[:, c, :], *lnb[3], lambda c: [f"w{c}"], [])
                s.do(SP, "store", lambda e, b: e.dma_start(
                    out.rearrange("(n p) f -> p n f", p=P)[:, bass.ds(b.chunk(), NC), :], x3b[:, :, :]), f"l6_n{NC - 1}", dmas=1)

            for name, fn in (("load_x2", load_x2), ("scan_in", scan_in), ("scan_z", scan_z), ("core", core), ("scan_out", scan_out),
                             ("ffn_in", ffn_in), ("ffn_up", ffn_up), ("ffn_act", ffn_act), ("ffn_out", ffn_out)):
                Stage(top, name, fn)
            point = 1e-6
            plan = [("load_x2", 1.6, 1.7), ("scan_in", 0, 0.95), ("scan_z", 1.3, 1.3 + point), ("core", 1, 2), ("scan_out", 2, 2.5),
                    ("ffn_in", 2.5, 2.8), ("ffn_up", 2.8, 3.3), ("ffn_act", 3.3, 3.3 + point), ("ffn_out", 3.3 + 2 * point, 3.9)]
            with nc.Block() as block:
                def start(e):
                    e.memset(h0[:, :, :], 0.0)
                block.vector(start)
            with nc.Block() as block:
                def sp(e):
                    top.run(SP, e, plan)
                    for q in (0, 1):
                        e.wait_ge(top.stages["ffn_out"].sem["store"][q], DMAS * (NB // 2 + 1))
                block.sync(sp)
                block.tensor(lambda e: top.run(PE, e, plan))
                block.vector(lambda e: top.run(VE, e, plan))
                block.gpsimd(lambda e: top.run(PO, e, plan))
                block.scalar(lambda e: top.run(SA, e, plan))


def kernel(**inputs):
    import numpy as np
    import concourse.bacc as bacc
    from concourse.bass_utils import run_bass_kernel_spmd

    a = {k: np.asarray(v) for k, v in inputs.items()}
    L0, L1 = "L0_attn_", "L1_attn_"
    F0, F1 = "L0_ffn_", "L1_ffn_"

    def column(v):
        v = v.reshape(v.shape[0], -1)
        if v.shape[0] < P:
            v = np.concatenate([v, np.zeros((P - v.shape[0], v.shape[1]), v.dtype)])
        return v.reshape(-1, P, v.shape[1]).transpose(1, 0, 2).reshape(P, -1)

    down = {"cn_b1": a[F0 + "cn_b1"], "cn_b2": a[F0 + "cn_b2"], "cn_b3": a[F0 + "cn_b3"], "cn_w4": a[F0 + "cn_w4"],
            "gc_b1": a[F0 + "gc_b1"], "gc_b2": a[F0 + "gc_b2"], "gc_w3": a[F0 + "gc_w3"],
            "conv_b": a[L0 + "conv_b"], "conv_w": a[L0 + "conv_w"], "norm_w": a[L0 + "norm_w"],
            "c_b_in": a[L1 + "b_in"], "c_b_dt": a[L1 + "b_dt"], "c_b_bc": np.concatenate([a[L1 + "b_B"], a[L1 + "b_C"]] * 3),
            "c_D": a[L1 + "D"], "c_A_log": a[L1 + "A_log"],
            "f_gamma": a[F1 + "ln_gamma"], "f_beta": a[F1 + "ln_beta"], "f_b1": a[F1 + "fc1_bias"]}
    every = {"cn_b4": a[F0 + "cn_b4"], "gc_b3": a[F0 + "gc_b3"], "adaptive_range": a[F0 + "adaptive_range"],
             "dt_bias": a[L0 + "dt_bias"], "A_log": a[L0 + "A_log"], "D": a[L0 + "D"],
             "c_gamma": a[L1 + "gamma"], "c_beta": a[L1 + "beta"], "c_b_out": a[L1 + "b_out"], "f_b2": a[F1 + "fc2_bias"]}
    arrays = {
        "u": a[L0 + "u"][0], "uT": a[L0 + "u"][0].T, "W_inT": a[L0 + "W_in"].T, "W_outT": a[L0 + "W_out"].T,
        **{n: a[F0 + n] for n in ("cn_w1", "cn_w2", "cn_w3", "gc_w1", "gc_w2")},
        **{f"c_{n}T": a[L1 + n].T for n in ("w_in", "w_dt", "w_B", "w_C", "w_out")},
        "f_q1": a[F1 + "fc1_q"], "f_s1": a[F1 + "fc1_scales"], "f_q2": a[F1 + "fc2_q"], "f_s2": a[F1 + "fc2_scales"],
        "columns": np.concatenate([column(down[n]) for n, _ in COLUMNS], axis=1),
        "everywhere": np.concatenate([every[n].reshape(-1) for n, _ in EVERYWHERE]),
    }
    arrays = {f"in_{k}": np.ascontiguousarray(v) for k, v in arrays.items()}
    nc = bacc.Bacc("TRN2", target_bir_lowering=False, num_devices=1)
    dram = {k[3:]: nc.dram_tensor(k, v.shape, mybir.dt.from_np(v.dtype), kind="ExternalInput").ap() for k, v in arrays.items()}
    out = nc.dram_tensor("out", (T, DM), F32, kind="ExternalOutput").ap()
    build(nc, dram, out, nc.dram_tensor("x2_tokens", (T, DM), F32, kind="Internal").ap())
    r = run_bass_kernel_spmd(nc, [arrays], core_ids=[0])
    return r.results[0]["out"].reshape(1, T, DM)
```

```python
import concourse.bass as bass
from concourse import mybir
from contextlib import ExitStack
from math import ceil

F32 = mybir.dt.float32
F32R = mybir.dt.float32r
BF16 = mybir.dt.bfloat16
I32 = mybir.dt.int32
ALU = mybir.AluOpType
ACT = mybir.ActivationFunctionType

P = 128
T, DM = 4096, 256
TB = 512
NB = T // TB
CH = 128
NC = TB // CH
KD = DM // P
DI, DS, NH, HD, TAPS = 512, 64, 8, 64, 4
NX = (DI + 2 * DS) // P
DIN = 2 * DI + 2 * DS + NH
NS = 16
FF = 1024
KF = FF // P
EPS = 1e-5
COLUMNS = [("cn_b1", KD), ("cn_b2", 1), ("cn_b3", 1), ("cn_w4", 1), ("gc_b1", 1), ("gc_b2", 1), ("gc_w3", 1),
           ("conv_b", NX), ("conv_w", NX * TAPS), ("norm_w", DI // P),
           ("c_b_in", 2 * KD), ("c_b_dt", KD), ("c_b_bc", 1), ("c_D", KD), ("c_A_log", KD * NS),
           ("f_gamma", KD), ("f_beta", KD), ("f_b1", KF)]
EVERYWHERE = [("cn_b4", 1), ("gc_b3", 1), ("adaptive_range", 1), ("dt_bias", NH), ("A_log", NH), ("D", NH),
              ("c_gamma", DM), ("c_beta", DM), ("c_b_out", DM), ("f_b2", DM)]
PE, SA, VE, PO, SP = "pe", "act", "dve", "pool", "sp"
POINT = 1e-6
ROOM = {"ffn_act.si": 1, "ffn_out.l_nb": 2, "ffn_out.o": 1, "ffn_out.w": 3, "ffn_up.ue": 2, "load_x2.x": 4,
        "loads.uT": 6, "post.ssn": 2, "pre.cb": 1, "scan_in.pr": 1, "scan_in.vr": 4, "scan_z.z": 1,
        "tail.mv": 1, "tail.o": 1}
AHEAD = 4
DMAS = 16


class Block:

    def __init__(self, j, off):
        self.j, self.off = j, off

    def chunk(self):
        return self.off * NC if self.j is None else self.j * (2 * NC) + self.off * NC

    def token(self):
        return self.off * TB if self.j is None else self.j * (2 * TB) + self.off * TB


class Stage:

    def __init__(self, top, name, build):
        self.name, self.sem, self.count, self.place = name, {}, {}, {}
        self.steps = [[], []]
        for parity in (0, 1):
            self.building, self.at, self.length = self.steps[parity], [], 0
            build(self, parity)
        for step in self.steps[0]:
            engine, label, n = step[0], step[1], step[4]
            if n:
                self.sem[label] = [top.sem(f"{name}_{label}{q}") for q in (0, 1)]
                self.place[label] = (None, n)
            else:
                if engine not in self.sem:
                    self.sem[engine] = top.sem(f"{name}_{engine}")
                self.count[engine] = self.count.get(engine, 0) + 1
                self.place[label] = (engine, self.count[engine])
        top.stages[name] = self

    def do(self, engine, label, work, *after, dmas=0, alone=False):
        self.length += ROOM.get(f"{self.name}." + "".join(x for x in label if not x.isdigit()), 0)
        self.building.append((engine, label, work, after, dmas, alone))
        self.at.append(self.length)
        self.length += 1

    def gap(self, n):
        self.length += n


class Program:
    def __init__(self, nc, ctx):
        self.nc, self.ctx, self.stages = nc, ctx, {}
        self.apart = self.sem("apart")

    def sem(self, name):
        return self.ctx.enter_context(self.nc.semaphore(name))

    def level(self, stage, label, block):
        engine, at = stage.place[label]
        if engine is None:
            q = block.off % 2
            return stage.sem[label][q], DMAS * at, ((block.off - q) // 2 + 2) * DMAS * at
        n = stage.count[engine]
        return stage.sem[engine], 2 * n, (block.off + 2) * n + at

    def emit(self, me, eng, work, j, seen):
        for stage, block, step in work:
            engine, label, fn, after, n, alone = step
            waited = False
            if engine != me:
                continue
            for name in after:
                name, _, lag = name.partition("@")
                of, _, what = name.rpartition(".")
                of = self.stages[of] if of else stage
                then = Block(j, block.off + int(lag or 0))
                if j is None and then.off >= NB:
                    continue
                sem, a, c = self.level(of, what, then)
                if seen.get(sem.name, 0) >= c:
                    continue
                seen[sem.name] = c
                eng.wait_ge(sem, c if j is None else j * a + c)
                waited = j is not None
                if waited and me == SP:
                    eng.sem_inc(self.apart, 1)
            if waited and (me == PO or alone):
                eng.sem_inc(self.apart, 1)
            if n:
                done = fn(eng, block)
                done = done if isinstance(done, list) else [done]
                assert len(done) == n
                for d in done:
                    d.then_inc(stage.sem[label][block.off % 2], DMAS)
            else:
                fn(eng, block).then_inc(stage.sem[engine], 1)

    def body(self, plan, j, t):
        work = []
        for name, lo, hi in plan:
            stage = self.stages[name]
            assert hi - lo <= 1
            for n, at in enumerate(stage.at):
                at = lo + (hi - lo) * at / stage.length
                block = t - int(at)
                if j is None and not 0 <= block < NB:
                    continue
                work.append((at % 1, block, stage, Block(j, block), stage.steps[block % 2][n]))
        work.sort(key=lambda w: w[:2])
        return [w[2:] for w in work]

    def credit(self, me, eng, names):
        for name in names:
            stage = self.stages[name]
            for label, (engine, n) in stage.place.items():
                if engine is None and me == SP:
                    for q in (0, 1):
                        eng.sem_inc(stage.sem[label][q], DMAS * n)
            if me in stage.count:
                eng.sem_inc(stage.sem[me], 2 * stage.count[me])

    def run(self, me, eng, plan):
        lag = max(ceil(hi) - 1 for _, _, hi in plan)
        first = lag + lag % 2
        self.credit(me, eng, [p[0] for p in plan])
        seen = {}
        for t in range(first):
            self.emit(me, eng, self.body(plan, None, t), None, seen)
        with eng.Fori(0, (NB - first) // 2) as j:
            seen = {}
            for t in (first, first + 1):
                self.emit(me, eng, self.body(plan, j, t), j, seen)
        seen = {}
        for t in range(NB, NB + lag):
            self.emit(me, eng, self.body(plan, None, t), None, seen)


def passes(e, out, pairs):
    for n, (w, x) in enumerate(pairs):
        i = e.matmul(out, w, x, start=(n == 0), stop=(n == len(pairs) - 1))
    return i


def build(nc, d, out, x2_dram):
    with ExitStack() as ctx:
        top = Program(nc, ctx)

        def sb(name, shape, dt=F32, within=ctx):
            return within.enter_context(nc.sbuf_tensor(name, shape, dt))

        def psum(within, n):
            return [within.enter_context(nc.psum_tensor(f"{n}{i}", [P, 512], F32)) for i in range(8)]

        ident, upper, below, ones = (sb(n, [P, P]) for n in ("ident", "upper", "below", "ones"))
        mhalf, sign = sb("mhalf", [P, NC]), sb("sign", [P, 1])
        x1T = sb("x1T", [P, KD, T])
        nets = sb("nets", [P, KD, TB])
        cn_w1, cn_w2, gc_w1 = nets[:, :, 0:DM], nets[:, :, DM:DM + P], nets[:, :, DM + P:DM + 2 * P]
        cn_w3 = sb("cn_w3", [P, 64])
        gc_w2 = sb("gc_w2", [P, 64])
        columns, everywhere = sb("columns", [P, sum(n for _, n in COLUMNS)]), sb("everywhere", [P, sum(n for _, n in EVERYWHERE)])
        vec_at = {}
        for held, names in ((columns, COLUMNS), (everywhere, EVERYWHERE)):
            at = 0
            for name, n in names:
                vec_at[name] = held[:, at:at + n]
                at += n
        cn_b1, cn_b2, cn_b3, cn_b4 = (vec_at[n] for n in ("cn_b1", "cn_b2", "cn_b3", "cn_b4"))
        gc_b1, gc_b2, gc_b3, rng = (vec_at[n] for n in ("gc_b1", "gc_b2", "gc_b3", "adaptive_range"))
        cw4 = sb("cw4", [64, P])
        gw3 = sb("gw3", [64, P])
        hb4, hg3 = sb("hb4", [P, 1]), sb("hg3", [P, 1])
        slope, shift = sb("slope", [P, 1]), sb("shift", [P, 1])

        def rows(v):
            return v.rearrange("(k p) n -> p k n", p=P)

        def layer_norm(s, tag, src, dst, st, mv, ve, rs, nb, src_ready, dst_free, on=VE):
            for c in range(NC):
                s.do(VE, f"{tag}_st{c}", lambda e, b, c=c: e.bn_stats(st[:, c, :], src(c)), *src_ready(c),
                     f"{tag}_ve@-1")
            for c in range(NC):
                s.do(VE, f"{tag}_mv{c}", lambda e, b, c=c: e.bn_aggr(mv[:, c, :], st[:, c, :]), alone=True, *[f"{tag}_st{c}",
                     f"{tag}_n{NC - 1}@-1"])
            s.do(VE, f"{tag}_ve", lambda e, b: e.tensor_scalar(ve[:, :], mv[:, :, 1], EPS, None, ALU.add),
                 f"{tag}_mv{NC - 1}", f"{tag}_rs@-1")
            s.do(PO, f"{tag}_rs", lambda e, b: e.tensor_tensor(rs[:, :], ve[:, :], mhalf[:, :], ALU.pow),
                 f"{tag}_ve", f"{tag}_n{NC - 1}@-1")
            if on == SA:
                s.gap(2)
                s.do(VE, f"{tag}_nb", lambda e, b: e.scalar_tensor_tensor(nb[:, :], mv[:, :, 0], -1.0, rs[:, :], ALU.mult, ALU.mult), f"{tag}_rs")
            s.gap(4)
            for c in range(NC):
                if on == SA:
                    s.do(SA, f"{tag}_n{c}", lambda e, b, c=c: e.activation(dst(c), src(c), ACT.Identity, bias=nb[:, c:c + 1], scale=rs[:, c:c + 1]),
                         f"{tag}_nb", *dst_free)
                else:
                    s.do(VE, f"{tag}_n{c}", lambda e, b, c=c: e.tensor_scalar(
                        dst(c), src(c), mv[:, c, 0:1], rs[:, c:c + 1], ALU.subtract, ALU.mult), f"{tag}_rs", *dst_free)

        with ExitStack() as pa:
            def a(name, shape, dt=F32):
                return sb(name, shape, dt, within=pa)

            def two(name, shape, dt=F32):
                return [a(f"{name}{q}", shape, dt) for q in (0, 1)]

            Wh, Wl = a("Wh", [P, KD, DIN], F32R), a("Wl", [P, KD, DIN], F32R)
            W_out = a("W_out", [P, DI // P, DM])
            cw, cb = vec_at["conv_w"].rearrange("p (m j) -> p m j", m=NX), vec_at["conv_b"]
            nw, dtb1, D1 = vec_at["norm_w"], vec_at["dt_bias"], vec_at["D"]
            dtb, negA = a("dtb", [P, NC, NH]), a("negA", [P, NC, NH])
            expA = a("expA", [P, NH])
            belowr = a("belowr", [P, P], F32R)
            S, raw = a("S", [DS, DI]), a("raw", [P, NX, TB + TAPS - 1])

            consts = 6
            c_sem, v_sem, w_sem, wa_sem, wa_act = (top.sem(n) for n in ("const", "vectors", "weights", "wa_sem", "wa_act"))
            vectors = [(everywhere, d["everywhere"].rearrange("(a n) -> a n", a=1).to_broadcast([P, everywhere.shape[1]])),
                       (columns, d["columns"])]
            early = [(cn_w1, rows(d["cn_w1"])), (cn_w2, rows(d["cn_w2"])),
                     (cn_w3[:, :], d["cn_w3"]), (gc_w1, rows(d["gc_w1"])), (gc_w2[:, :], d["gc_w2"])]
            with ExitStack() as pw:
                W_in, W_raw = sb("W_in", [P, KD, DIN], within=pw), sb("W_raw", [P, DI // P, DM], within=pw)
                with nc.Block() as block:
                    @block.sync
                    def _(e):
                        for dst, src in vectors:
                            e.dma_start(dst[:, :], src).then_inc(v_sem, DMAS)
                        e.dma_start(W_in[:, :, :], rows(d["W_inT"])).then_inc(wa_sem, DMAS)
                        e.dma_start(W_raw[:, :, :], rows(d["W_outT"])).then_inc(wa_sem, DMAS)
                        for dst, src in early:
                            e.dma_start(dst, src).then_inc(w_sem, DMAS)
                        e.wait_ge(v_sem, DMAS * len(vectors))
                        e.wait_ge(wa_sem, 2 * DMAS)
                        e.wait_ge(w_sem, DMAS * len(early))

                    @block.scalar
                    def _(e):
                        e.preload_act_table_set("natural_log_exp_and_others")
                        e.wait_ge(v_sem, DMAS * len(vectors))
                        e.activation(expA[:, :], vec_at["A_log"], ACT.Exp).then_inc(wa_act, 1)
                        e.wait_ge(wa_sem, 2 * DMAS)
                        for k in range(KD):
                            e.activation(Wh[:, k, :], W_in[:, k, :], ACT.Copy).then_inc(wa_act, 1)

                    @block.vector
                    def _(e):
                        e.memset(S[:, :], 0.0)
                        e.memset(raw[:, :, TB:TB + TAPS - 1], 0.0)
                        e.wait_ge(v_sem, DMAS * len(vectors))
                        e.tensor_copy(cw4[:, :], vec_at["cn_w4"][0:64, :].to_broadcast([64, P]))
                        e.tensor_copy(gw3[:, :], vec_at["gc_w3"][0:64, :].to_broadcast([64, P]))
                        e.tensor_scalar(hb4[:, :], cn_b4, 0.5, None, ALU.mult)
                        e.tensor_scalar(hg3[:, :], gc_b3, 0.5, None, ALU.mult)
                        for c in range(NC):
                            e.tensor_copy(dtb[:, c, :], dtb1)
                        e.wait_ge(wa_act, 1)
                        for c in range(NC):
                            e.tensor_scalar(negA[:, c, :], expA[:, :], -1.0, None, ALU.mult)
                        e.wait_ge(c_sem, consts + 1)
                        e.tensor_copy(belowr[:, :], below[:, :])
                        for k in range(KD):
                            e.wait_ge(wa_act, 2 + k)
                            e.tensor_tensor(Wl[:, k, :], W_in[:, k, :], Wh[:, k, :].bitcast(F32), ALU.subtract)

                    @block.gpsimd
                    def _(e):
                        e.memset(ident[:, :], 0.0).then_inc(c_sem, 1)
                        for full, value in ((upper, 1.0), (below, 1.0), (ones, 1.0), (mhalf, -0.5), (sign, 1.0)):
                            e.memset(full[:, :], value).then_inc(c_sem, 1)
                        e.wait_ge(c_sem, consts)
                        e.affine_select(out=below[:, :], in_=below[:, :], compare_op=ALU.is_ge, fill=0.0,
                                        base=-1, pattern=[[-1, P]], channel_multiplier=1).then_inc(c_sem, 1)
                        e.affine_select(out=ident[:, :], in_=ident[:, :], compare_op=ALU.not_equal, fill=1.0,
                                        base=0, pattern=[[-1, P]], channel_multiplier=1)
                        e.affine_select(out=upper[:, :], in_=upper[:, :], compare_op=ALU.is_ge, fill=0.0,
                                        base=0, pattern=[[1, P]], channel_multiplier=-1)
                        e.affine_select(out=sign[:, :], in_=sign[:, :], compare_op=ALU.is_ge, fill=-1.0,
                                        base=P // 2 - 1, pattern=[[0, 1]], channel_multiplier=-1)
                        e.wait_ge(v_sem, DMAS * len(vectors))
                        e.wait_ge(wa_sem, 2 * DMAS)
                        for k in range(DI // P):
                            e.tensor_scalar(W_out[:, k, :], W_raw[:, k, :], nw[:, k:k + 1], None, ALU.mult)

            uT, u = a("uT", [P, KD, TB]), two("u", [P, NC, DM])
            uh, ul = two("uh", [P, KD, TB], F32R), two("ul", [P, KD, TB], F32R)
            xf, Cf, zs = two("xf", [P, NX, TB]), two("Cf", [DS, TB]), two("zs", [P, NC, DI])
            sp_x, sp_a, sp_y, sp_l, sp_d, sp_r = (a(n, [P, NC * NH]) for n in ("sp_x", "sp_a", "sp_y", "sp_l", "sp_d", "sp_r"))
            dt, dA = two("dt", [P, NC, NH]), two("dA", [P, NC, NH])
            dAh, dAl = two("dAh", [P, NC, NH], F32R), two("dAl", [P, NC, NH], F32R)
            dec = two("dec", [P, 3, NC, NH])
            aUh, aUl = a("aUh", [P, NH, CH], F32R), a("aUl", [P, NH, CH], F32R)
            L, M = a("L", [P, NH, CH]), a("M", [P, NH, CH])
            xt, xs, xd, xD = a("xt", [P, DI]), two("xs", [P, DI]), two("xd", [P, DI]), two("xD", [P, DI])
            Bt, CB = two("Bt", [P, DS]), a("CB", [P, CH])
            Sd = a("Sd", [DS, DI])
            yo, y1, y2, sq = a("yo", [P, DI]), a("y1", [P, DI]), a("y2", [P, DI]), a("sq", [P, DI])
            yT = a("yT", [P, DI // P, CH])
            ssq, ssn, rms = a("ssq", [P, 1]), a("ssn", [P, 1]), a("rms", [P, 1])
            r1, x1 = two("r1", [P, DM]), two("x1", [P, DM])
            st1, mv1, ve1, rs1 = two("st1", [P, 6]), two("mv1", [P, 2]), two("ve1", [P, 1]), two("rs1", [P, 1])
            pb = psum(pa, "pa")

            def loads(s, q):
                s.do(SP, "uT", lambda e, b: e.dma_start(
                    uT[:, :, :], d["uT"].rearrange("(k p) t -> p k t", p=P)[:, :, bass.ds(b.token(), TB)]), "proj.ul@-1", dmas=1)

            def load_u(s, q):
                s.do(SP, "u", lambda e, b: e.dma_start(
                    u[q][:, :, :], d["u"].rearrange("(n p) f -> p n f", p=P)[:, bass.ds(b.chunk(), NC), :]),
                    f"tail.r{NC - 1}@-2", dmas=1)

            def proj(s, q):
                s.do(VE, "uh", lambda e, b: e.tensor_copy(uh[q][:, :, :], uT[:, :, :]), "loads.uT", "dt@-2")
                s.do(PO, "ul", lambda e, b: e.tensor_tensor(ul[q][:, :, :], uT[:, :, :], uh[q][:, :, :].bitcast(F32), ALU.subtract), "uh", "dt@-2")
                for m in range(NX):
                    ws = slice(DI + m * P, DI + (m + 1) * P)
                    free = f"c{m - 2}" if m > 1 else "spx@-1" if m == (NX + NC) % 2 else f"zc{NC - 1}@-1"
                    s.do(PE, f"x{m}", lambda e, b, m=m, ws=ws: passes(e, pb[m % 2][:, :], [
                        (w[:, k, ws], x[:, k, :]) for w, x in ((Wh, uh[q]), (Wl, uh[q]), (Wh, ul[q])) for k in range(KD)]), "uh", "ul", free)
                    s.do(PO, f"halo{m}", lambda e, b, m=m: e.tensor_copy(raw[:, m, 0:TAPS - 1], raw[:, m, TB:TB + TAPS - 1]), f"t{m}_0@-1")
                    s.do(SA, f"ev{m}", lambda e, b, m=m: e.activation(raw[:, m, TAPS - 1:TB + TAPS - 1], pb[m % 2][:, :], ACT.Copy),
                         f"x{m}", f"halo{m}")
                    s.do(SA, f"c{m}", lambda e, b, m=m: e.activation(xf[q][:, m, :], pb[m % 2][:, :], ACT.Identity, bias=cb[:, m:m + 1],
                                                                     scale=cw[:, m, TAPS - 1:TAPS]), f"x{m}", f"pre.xt{NC - 1}@-2", f"pre.cb{NC - 1}@-2", "act.C@-2")
                    for j in range(TAPS - 2, -1, -1):
                        s.do(VE, f"t{m}_{j}", lambda e, b, m=m, j=j: e.scalar_tensor_tensor(
                            xf[q][:, m, :], raw[:, m, j:j + TB], cw[:, m, j:j + 1], xf[q][:, m, :], ALU.mult, ALU.add),
                            f"c{m}", f"t{m}_{j + 1}" if j < TAPS - 2 else f"ev{m}")
                for c in range(NC):
                    cs = slice(c * CH, (c + 1) * CH)
                    s.do(PE, f"z{c}", lambda e, b, c=c, cs=cs: passes(e, pb[(NX + c) % 2][:, :], [
                        (x[:, k, cs], w[:, k, 0:DI]) for w, x in ((Wh, uh[q]), (Wl, uh[q]), (Wh, ul[q])) for k in range(KD)]),
                        f"zc{c - 2}" if c > 1 else f"c{NX - 2 + c}")
                    s.do(SA, f"zc{c}", lambda e, b, c=c: e.activation(zs[q][:, c, :], pb[(NX + c) % 2][:, :], ACT.Copy),
                         f"z{c}", f"post.gate{c}@-2")

                def dt_mm(e, b):
                    for c in range(NC):
                        i = passes(e, pb[(NX + NC) % 2][:, c * NH:(c + 1) * NH], [
                            (x[:, k, c * CH:(c + 1) * CH], w[:, k, DIN - NH:DIN]) for w, x in ((Wh, uh[q]), (Wl, uh[q]), (Wh, ul[q])) for k in range(KD)])
                    return i
                s.do(PE, "dt", dt_mm, f"zc{NC - 2}")
                s.do(VE, "spx", lambda e, b: e.tensor_tensor(sp_x[:, :], pb[(NX + NC) % 2][:, 0:NC * NH],
                                                             dtb[:, :, :].rearrange("p c h -> p (c h)"), ALU.add), "dt", "spa@-1", "spr@-1")
                s.do(SA, "spa", lambda e, b: e.activation(sp_a[:, :], sp_x[:, :], ACT.Abs), "spx", "spy@-1")
                s.do(SA, "spy", lambda e, b: e.activation(sp_y[:, :], sp_a[:, :], ACT.Exp, scale=-1.0), "spa", "spe@-1")
                s.do(SA, "spl", lambda e, b: e.activation(sp_l[:, :], sp_y[:, :], ACT.Ln, bias=1.0), "spy", "sps@-1")
                s.do(VE, "spd", lambda e, b: e.tensor_scalar(sp_d[:, :], sp_y[:, :], 1.0, -1.0, ALU.add, ALU.add), "spy", "sps@-1")
                s.do(VE, "spr", lambda e, b: e.tensor_scalar(sp_r[:, :], sp_x[:, :], 0.0, None, ALU.max), "spx", "spt@-1")
                s.do(VE, "spe", lambda e, b: e.tensor_tensor(sp_d[:, :], sp_y[:, :], sp_d[:, :], ALU.subtract), "spd")
                s.do(VE, "sps", lambda e, b: e.tensor_tensor(sp_d[:, :], sp_l[:, :], sp_d[:, :], ALU.add), "spl", "spe")
                s.do(VE, "spt", lambda e, b: e.tensor_tensor(dt[q][:, :, :].rearrange("p c h -> p (c h)"), sp_r[:, :],
                                                             sp_d[:, :], ALU.add), "sps", "spr", f"pre.xs{NC - 1}@-2", "spA@-2")
                s.do(VE, "spA", lambda e, b: e.tensor_tensor(dA[q][:, :, :], dt[q][:, :, :], negA[:, :, :], ALU.mult), "spt", "pre.sums@-2")
                s.do(VE, "dAh", lambda e, b: e.tensor_copy(dAh[q][:, :, :], dA[q][:, :, :]), "spA", f"pre.auh{NC - 1}@-2")
                s.do(VE, "dAl", lambda e, b: e.tensor_tensor(dAl[q][:, :, :], dA[q][:, :, :], dAh[q][:, :, :].bitcast(F32), ALU.subtract),
                     "dAh", f"pre.aul{NC - 1}@-2")

            def act(s, q):
                for m in range(NX - 1, -1, -1):
                    s.do(SA, f"x{m}", lambda e, b, m=m: e.activation(xf[q][:, m, :], xf[q][:, m, :], ACT.Silu), f"proj.t{m}_0")
                    if m == NX - 1:
                        s.do(SP, "C", lambda e, b: e.dma_start(Cf[q][:, :], xf[q][DS:2 * DS, NX - 1, :]), f"x{NX - 1}",
                             f"post.off{NC - 1}@-2", f"pre.cb{NC - 1}@-2", dmas=1)
                for c in range(NC):
                    s.do(SA, f"z{c}", lambda e, b, c=c: e.activation(zs[q][:, c, :], zs[q][:, c, :], ACT.Silu), f"proj.zc{c}")

            def heads(x):
                return x.rearrange("p (h f) -> p h f", h=NH)

            def by_head(v, n, parts=P):
                return v.rearrange("p (h o) -> p h o", o=1).to_broadcast([parts, NH, n])

            def prev(name, c, back=1):
                return f"{name}{(c - back) % NC}@{(c - back) // NC}"

            def pre(s, q):
                def sums(e, b):
                    v = dA[q][:, :, :].rearrange("p c h -> p (c h)")
                    for n, w in enumerate((below, upper, ones)):
                        i = e.matmul(pb[3][:, 256 + n * NC * NH:256 + (n + 1) * NC * NH], w[:, :], v, start=True, stop=True)
                    return i
                s.do(PE, "sums", sums, "proj.spA", f"cbm{NC - 1}@-1")
                s.do(SA, "dec", lambda e, b: e.activation(dec[q][:, :, :, :].rearrange("p a c h -> p (a c h)"),
                                                          pb[3][:, 256:256 + 3 * NC * NH], ACT.Exp),
                     "sums", f"post.Sd{NC - 1}@-2", f"post.yo{NC - 1}@-2", f"xd{NC - 1}@-2")
                upper_all = upper[:, :].rearrange("p (o l) -> p o l", o=1).to_broadcast([P, NH, CH])
                for c in range(NC):
                    cs, r = slice(c * CH, (c + 1) * CH), c % 2
                    for part, src, dst in (("auh", dAh, aUh), ("aul", dAl, aUl)):
                        s.do(PO, f"{part}{c}", lambda e, b, c=c, src=src, dst=dst: e.tensor_tensor(
                            dst[:, :, :], by_head(src[q][:, c, :].bitcast(F32), CH), upper_all, ALU.mult), "proj.dAl", prev("seg1_", c))
                    def tx(e, b, cs=cs):
                        for m in range(NX - 1):
                            i = e.transpose(pb[2][:, m * P:(m + 1) * P], xf[q][:, m, cs], ident[:, :])
                        return i
                    s.do(PE, f"xt{c}", tx, "act.x0", prev("xtc", c), "tail." + prev("o", c, 3))
                    s.do(SA, f"xtc{c}", lambda e, b: e.activation(xt[:, :], pb[2][:, :], ACT.Copy), f"xt{c}", prev("xs", c), prev("xD", c))
                    s.do(PE, f"bt{c}", lambda e, b, cs=cs: e.transpose(pb[3][:, 0:P], xf[q][:, NX - 1, cs], ident[:, :]),
                         f"act.x{NX - 1}", prev("cbm", c), "dec")
                    s.do(PE, f"cb{c}", lambda e, b, cs=cs: e.matmul(pb[3][:, P:2 * P], xf[q][0:DS, NX - 1, cs], Cf[q][:, cs],
                                                                    start=True, stop=True), "act.C")
                    s.do(SA, f"btc{c}", lambda e, b, r=r: e.activation(Bt[r][:, :], pb[3][:, 0:DS], ACT.Copy), f"cb{c}", "post." + prev("new", c, 2))
                    s.do(VE, f"cbm{c}", lambda e, b: e.tensor_tensor(CB[:, :], pb[3][:, P:2 * P], upper[:, :], ALU.mult),
                         f"btc{c}", prev("M", c))
                    s.do(PO, f"xs{c}", lambda e, b, c=c, r=r: e.tensor_tensor(heads(xs[r][:, :]), heads(xt[:, :]), by_head(dt[q][:, c, :], HD), ALU.mult),
                         f"xtc{c}", "post." + prev("diag", c, 2), prev("xd", c, 2))
                    s.do(PO, f"xd{c}", lambda e, b, c=c, r=r: e.tensor_tensor(heads(xd[r][:, :]), heads(xs[r][:, :]), by_head(dec[q][:, 0, c, :], HD), ALU.mult),
                         f"xs{c}", "dec", "post." + prev("new", c, 2))
                    s.do(PO, f"xD{c}", lambda e, b, c=c, r=r: e.tensor_tensor(heads(xD[r][:, :]), heads(xt[:, :]), by_head(D1, HD), ALU.mult),
                         f"xtc{c}", "post." + prev("y1_", c, 2))
                    for g in (0, 1):
                        hs = slice(g * NH // 2, (g + 1) * NH // 2)
                        s.do(PE, f"seg{g}_{c}", lambda e, b, g=g, hs=hs: passes(e, pb[4 + g][:, :], [
                            (belowr[:, :], x[:, hs, :].rearrange("p h l -> p (h l)")) for x in (aUh, aUl)]), f"auh{c}", f"aul{c}", prev(f"L{g}_", c))
                        s.do(SA, f"L{g}_{c}", lambda e, b, g=g, hs=hs: e.activation(
                            L[:, hs, :].rearrange("p h l -> p (h l)"), pb[4 + g][:, :], ACT.Exp), f"seg{g}_{c}", prev("M", c))
                    s.do(VE, f"M{c}", lambda e, b: e.tensor_tensor(
                        M[:, :, :], L[:, :, :], CB[:, :].rearrange("p (o l) -> p o l", o=1).to_broadcast([P, NH, CH]), ALU.mult),
                        f"L1_{c}", f"cbm{c}", "post." + prev("diag", c))

            def post(s, q):
                for c in range(NC):
                    cs, r = slice(c * CH, (c + 1) * CH), c % 2
                    s.do(PE, f"off{c}", lambda e, b, cs=cs: e.matmul(pb[6][:, :], Cf[q][:, cs], S[:, :], start=True, stop=True),
                         "act.C", prev("S", c), prev("y1a", c))
                    s.do(PE, f"new{c}", lambda e, b, r=r: e.matmul(pb[7][0:DS, :], Bt[r][:, :], xd[r][:, :], start=True, stop=True),
                         f"pre.btc{c}", f"pre.xd{c}", "tail." + prev("r", c))
                    s.do(VE, f"yo{c}", lambda e, b, c=c: e.tensor_tensor(heads(yo[:, :]), heads(pb[6][:, :]), by_head(dec[q][:, 1, c, :], HD), ALU.mult),
                         f"off{c}", "pre.dec", prev("y1_", c))

                    def diag(e, b, r=r):
                        for h in range(NH):
                            i = e.matmul(pb[6][:, h * HD:(h + 1) * HD], M[:, h, :], xs[r][:, h * HD:(h + 1) * HD], start=True, stop=True)
                        return i
                    s.do(PE, f"diag{c}", diag, f"pre.M{c}", f"pre.xs{c}", f"yo{c}")
                    s.do(VE, f"Sd{c}", lambda e, b, c=c: e.tensor_tensor(heads(Sd[:, :]), heads(S[:, :]), by_head(dec[q][0:DS, 2, c, :], HD, DS), ALU.mult),
                         "pre.dec", prev("S", c))
                    s.do(VE, f"S{c}", lambda e, b: e.tensor_tensor(S[:, :], Sd[:, :], pb[7][0:DS, :], ALU.add), f"Sd{c}", f"new{c}", f"off{c}")
                    s.do(PO, f"y1_{c}", lambda e, b, r=r: e.tensor_tensor(y1[:, :], yo[:, :], xD[r][:, :], ALU.add), f"yo{c}", f"pre.xD{c}", prev("y1a", c))
                    s.do(VE, f"y1a{c}", lambda e, b: e.tensor_tensor(y2[:, :], y1[:, :], pb[6][:, :], ALU.add), f"y1_{c}", f"diag{c}", prev("tyT", c), prev("sq", c))
                    s.do(VE, f"gate{c}", lambda e, b, c=c: e.tensor_tensor(y2[:, :], y2[:, :], zs[q][:, c, :], ALU.mult), f"y1a{c}", f"act.z{c}")

                    def ty(e, b):
                        for m in range(DI // P):
                            i = e.transpose(pb[7][:, m * P:(m + 1) * P], y2[:, m * P:(m + 1) * P], ident[:, :])
                        return i
                    s.do(PE, f"tyT{c}", ty, f"gate{c}", f"S{c}")
                    s.do(SA, f"yT{c}", lambda e, b: e.activation(yT[:, :, :].rearrange("p k l -> p (k l)"), pb[7][:, :], ACT.Copy),
                         f"tyT{c}", "tail." + prev("op", c))
                    s.do(SA, f"sq{c}", lambda e, b: e.activation(sq[:, :], y2[:, :], ACT.Square, accum_out=ssq[:, :]), f"gate{c}", prev("ssn", c), prev("sq", c))
                    s.do(VE, f"ssn{c}", lambda e, b: e.tensor_scalar(ssn[:, :], ssq[:, :], 1.0 / DI, EPS, ALU.mult, ALU.add), f"sq{c}", prev("rms", c))
                    s.do(PO, f"rms{c}", lambda e, b: e.tensor_tensor(rms[:, :], ssn[:, :], mhalf[:, 0:1], ALU.pow), f"ssn{c}", "tail." + prev("r", c))

            def tail(s, q):
                for c in range(NC):
                    r = c % 2

                    def op(e, b):
                        for k in range(DI // P):
                            i = e.matmul(pb[7][:, 0:DM], yT[:, k, :], W_out[:, k, :], start=(k == 0), stop=(k == DI // P - 1))
                        return i
                    s.do(PE, f"op{c}", op, f"post.yT{c}")
                    s.do(VE, f"r{c}", lambda e, b, c=c, r=r: e.scalar_tensor_tensor(r1[r][:, :], pb[7][:, 0:DM], rms[:, 0:1], u[q][:, c, :], ALU.mult, ALU.add),
                         f"op{c}", f"post.rms{c}", "load_u.u", prev("n", c, 2))
                    s.do(VE, f"st{c}", lambda e, b, r=r: e.bn_stats(st1[r][:, :], r1[r][:, :]), f"r{c}", prev("mv", c, 2))
                    s.do(VE, f"mv{c}", lambda e, b, r=r: e.bn_aggr(mv1[r][:, :], st1[r][:, :]), f"st{c}", prev("n", c, 2), alone=True)
                    s.do(VE, f"ve{c}", lambda e, b, r=r: e.tensor_scalar(ve1[r][:, :], mv1[r][:, 1:2], EPS, None, ALU.add), f"mv{c}", prev("rs", c, 2))
                    s.do(PO, f"rs{c}", lambda e, b, r=r: e.tensor_tensor(rs1[r][:, :], ve1[r][:, :], mhalf[:, 0:1], ALU.pow), f"ve{c}", prev("n", c, 2))
                    s.do(VE, f"n{c}", lambda e, b, r=r: e.tensor_scalar(x1[r][:, :], r1[r][:, :], mv1[r][:, 0:1], rs1[r][:, 0:1], ALU.subtract, ALU.mult),
                         f"rs{c}", prev("tx", c, 2))

                    def tx1(e, b, r=r):
                        for k in range(KD):
                            i = e.transpose(pb[2][:, k * P:(k + 1) * P], x1[r][:, k * P:(k + 1) * P], ident[:, :])
                        return i
                    s.do(PE, f"tx{c}", tx1, f"n{c}", "pre." + prev("xtc", c, -2), prev("o", c))
                    s.do(SA, f"o{c}", lambda e, b, c=c: e.activation(
                        x1T[:, :, bass.ds(b.token() + c * CH, CH)], pb[2][:, 0:DM].rearrange("p (k t) -> p k t", k=KD), ACT.Copy), f"tx{c}")

            for name, fn in (("loads", loads), ("load_u", load_u), ("proj", proj), ("act", act), ("pre", pre), ("post", post), ("tail", tail)):
                Stage(top, name, fn)
            plan = [("loads", 0.300, 0.400), ("load_u", 1.600, 1.700), ("proj", 1.008, 1.902), ("act", 2.004, 2.004 + POINT),
                    ("pre", 2.017, 3.001), ("post", 2.261, 3.261), ("tail", 2.500, 3.500)]
            with nc.Block() as block:
                block.sync(lambda e: top.run(SP, e, plan))
                block.tensor(lambda e: top.run(PE, e, plan))
                block.vector(lambda e: top.run(VE, e, plan))
                block.gpsimd(lambda e: top.run(PO, e, plan))
                block.scalar(lambda e: top.run(SA, e, plan))


        def vec(x):
            return x.rearrange("p k t -> p (k t)")

        w_xz, w_dt, w_bc, w_o = sb("w_xz", [P, KD, 2 * DM]), sb("w_dt", [P, KD, DM]), sb("w_bc", [P, KD, 3, 2, NS]), sb("w_o", [P, KD, DM])
        b_in, b_dt, b_bc, Dc, lg, lb, b1 = (vec_at[n] for n in ("c_b_in", "c_b_dt", "c_b_bc", "c_D", "f_gamma", "f_beta", "f_b1"))
        gam, bet, b_o = (vec_at[n] for n in ("c_gamma", "c_beta", "c_b_out"))
        A = sb("A", [P, KD, NS])
        w1, w2, hb2 = sb("w1", [P, KD, FF]), sb("w2", [P, KF, DM]), sb("hb2", [P, DM])
        sel = sb("sel", [3 * 2 * NS, 2 * NS, P], BF16)

        mean, g1, g2 = sb("mean", [P, KD]), sb("g1", [P, 1]), sb("g2", [64, 1])
        gt, k0 = sb("gt", [P, 1]), sb("k0", [P, 1])
        x2_tokens = x2_dram.rearrange("(n p) f -> p n f", p=P)
        with ExitStack() as pc:
            def t(name, shape, dt=F32):
                return sb(name, shape, dt, within=pc)

            def three(name, shape):
                return [t(f"{name}{y}", shape) for y in range(3)]

            q1, s1, f1 = t("q1", [P, KD, FF], I32), t("s1", [P, KD, FF]), t("f1", [P, KD, FF])
            q2, s2, f2 = t("q2", [P, KF, DM], I32), t("s2", [P, KF, DM]), t("f2", [P, KF, DM])
            o = [three(f"o{q}_", [P, KD, TB]) for q in (0, 1)]
            h1, h2, h3 = three("h1", [P, KD, TB]), three("h2", [P, TB]), three("h3", [64, TB])
            cS, tw = three("cS", [P, TB]), three("tw", [P, KD, TB])
            x2s = [t(f"x2s{q}", [P, NC, DM]) for q in (0, 1)]
            ln2 = [t(n, sh) for n, sh in (("st2", [P, NC, 6]), ("mv2", [P, NC, 2]), ("ve2", [P, NC]), ("rs2", [P, NC]), ("nb2", [P, NC]))]
            pb = psum(pc, "pc")

            def cycle(y):
                def build(s, q):
                    src = (lambda b, k: x1T[:, k, bass.ds(b.token(), TB)]) if y == 0 else (lambda b, k: o[q][y - 1][:, k, :])
                    dst, b0, b1_ = o[q][y], pb[2 * y], pb[2 * y + 1]
                    ready = [f"cycle{y - 1}.add", f"cycle{y - 1}.ad"] if y else []
                    for m in range(KD):
                        bank = (b0, b1_)[m]
                        s.do(PE, f"m1_{m}", lambda e, b, m=m, bank=bank: passes(e, bank[:, :], [
                            (cn_w1[:, k, m * P:(m + 1) * P], src(b, k)) for k in range(KD)]), *ready, ("a2@-1", "ta@-1")[m])
                        s.do(SA, f"a1_{m}", lambda e, b, m=m, bank=bank: e.activation(h1[y][:, m, :], bank[:, :], ACT.Gelu, bias=cn_b1[:, m:m + 1]),
                             f"m1_{m}", "m2@-1")
                    s.do(PE, "m2", lambda e, b: passes(e, b0[:, :], [(cn_w2[:, k, :], h1[y][:, k, :]) for k in range(KD)]), "a1_1", "a1_0")
                    s.do(SA, "a2", lambda e, b: e.activation(h2[y][:, :], b0[:, :], ACT.Gelu, bias=cn_b2[:, 0:1]), "m2", "m3@-1")
                    s.do(PE, "m3", lambda e, b: e.matmul(b1_[0:64, :], cn_w3[:, :], h2[y][:, :], start=True, stop=True), "a2")
                    s.do(SA, "a3", lambda e, b: e.activation(h3[y][:, :], b1_[0:64, :], ACT.Gelu, bias=cn_b3[0:64, :]), "m3", "m4@-1")
                    s.do(PE, "m4", lambda e, b: e.matmul(b1_[:, :], cw4[:, :], h3[y][:, :], start=True, stop=True), "a3")
                    s.do(SA, "ta", lambda e, b: e.activation(cS[y][:, :], b1_[:, :], ACT.Tanh, bias=hb4[:, 0:1], scale=0.5), "m4", "t1@-1")
                    s.do(VE, "cs", lambda e, b: e.tensor_scalar(cS[y][:, :], cS[y][:, :], slope[:, 0:1], shift[:, 0:1], ALU.mult, ALU.add), "ta")
                    for k in range(KD):
                        s.do(VE, f"t{k}", lambda e, b, k=k: e.tensor_tensor(tw[y][:, k, :], cS[y][:, :], src(b, 1 - k), ALU.mult), "cs", "add@-1", "ad@-1")
                    free = f"cycle{y + 1}.add@-2" if y < 2 else f"norm.bt{NC - 1}@-2"
                    s.do(PO, "ad", lambda e, b: e.tensor_tensor(dst[:, 0, :], src(b, 0), tw[y][:, 0, :], ALU.add), "t0", free)
                    s.do(PO, "add", lambda e, b: e.tensor_tensor(dst[:, 1, :], src(b, 1), tw[y][:, 1, :], ALU.subtract), "t1", free)
                    if y == 2:
                        s.do(PO, "res", lambda e, b: e.tensor_tensor(dst[:, :, :], dst[:, :, :], x1T[:, :, bass.ds(b.token(), TB)], ALU.add), "add", "ad")
                return build

            def norm(s, q):
                for c in range(NC):
                    def tr(e, b, c=c):
                        for k in range(KD):
                            i = e.transpose(pb[6 + c // 2][:, (c % 2) * DM + k * P:(c % 2) * DM + (k + 1) * P], o[q][2][:, k, c * CH:(c + 1) * CH], ident[:, :])
                        return i
                    s.do(PE, f"bt{c}", tr, "cycle2.res", f"bTe{NC - 2 + c // 2}@-1")
                layer_norm(s, "l2", lambda c: pb[6 + c // 2][:, (c % 2) * DM:(c % 2 + 1) * DM], lambda c: x2s[q][:, c, :], *ln2,
                           lambda c: [f"bt{c | 1}"], ["store@-2", f"bT{NC - 1}@-2"], on=SA)
                s.do(SP, "store", lambda e, b: e.dma_start(x2_tokens[:, bass.ds(b.chunk(), NC), :], x2s[q][:, :, :]), f"l2_n{NC - 1}", dmas=1)
                for c in range(NC):
                    bank = pb[6 + c % 2]

                    def tr(e, b, c=c, bank=bank):
                        for k in range(KD):
                            i = e.transpose(bank[:, k * P:(k + 1) * P], x2s[q][:, c, k * P:(k + 1) * P], ident[:, :])
                        return i
                    s.do(PE, f"bT{c}", tr, f"l2_n{NC - 1}", *([f"bTe{c - 2}"] if c > 1 else []))
                    s.do(SA, f"bTe{c}", lambda e, b, c=c, bank=bank: e.activation(
                        x1T[:, :, bass.ds(b.token() + c * CH, CH)], bank[:, 0:DM].rearrange("p (k t) -> p k t", k=KD), ACT.Copy), f"bT{c}", "cycle2.res")

            for y in range(3):
                Stage(top, f"cycle{y}", cycle(y))
            Stage(top, "norm", norm)
            plan = [("cycle0", 0.000, 0.700), ("cycle1", 0.660, 1.360),
                    ("cycle2", 1.340, 2.040), ("norm", 2.050, 2.950)]
            gv, gp, ga, gm, ld, aa, pv = (top.sem(n) for n in ("gv", "gp", "ga", "gm", "ld", "aa", "pv"))
            loaded = [(w_xz, rows(d["c_w_inT"])), (w_dt, rows(d["c_w_dtT"])), (w_o, rows(d["c_w_outT"])), (q1, rows(d["f_q1"])), (q2, rows(d["f_q2"]))]
            loaded += [(s1[:, k, :], d["f_s1"][k:k + 1, :].to_broadcast([P, FF])) for k in range(KD)]
            loaded += [(s2[:, k, :], d["f_s2"][k:k + 1, :].to_broadcast([P, DM])) for k in range(KF)]
            loaded += [(w_bc[:, :, g, m, :], rows(d[w + "T"])) for g in range(3) for m, w in enumerate(("c_w_B", "c_w_C"))]
            net = pb[6], pb[7], pb[6]
            with nc.Block() as block:
                @block.sync
                def _(e):
                    for dst, src in loaded:
                        e.dma_start(dst[tuple(slice(None) for _ in dst.shape)], src).then_inc(ld, DMAS)
                    top.run(SP, e, plan)
                    e.wait_ge(ld, DMAS * len(loaded))
                    for q in (0, 1):
                        e.wait_ge(top.stages["norm"].sem["store"][q], DMAS * (NB // 2 + 1))

                @block.gpsimd
                def _(e):
                    e.memset(sel[:, :, :], 0.0).then_inc(aa, 1)
                    for g in range(3):
                        e.wait_ge(aa, g + 1)
                        e.affine_select(out=sel[:, :, :], in_=sel[:, :, :], compare_op=ALU.not_equal, fill=1.0,
                                        base=-2 * NS * g, pattern=[[-1, 2 * NS], [0, P]], channel_multiplier=1).then_inc(aa, 1)
                    top.run(PO, e, plan)

                @block.vector
                def _(e):
                    e.reduce_sum(mean[:, 0:1], x1T[:, 0, :], mybir.AxisListType.X).then_inc(gv, 1)
                    e.tensor_scalar(slope[:, :], rng, 0.3, None, ALU.mult).then_inc(gv, 1)
                    e.wait_ge(gv, 2)
                    e.tensor_tensor(slope[:, :], slope[:, :], sign[:, :], ALU.mult).then_inc(gv, 1)
                    e.wait_ge(ga, 3)
                    e.tensor_scalar(k0[:, :], gt[:, :], 0.7, None, ALU.mult).then_inc(gv, 1)
                    e.wait_ge(gv, 4)
                    e.tensor_scalar(shift[:, :], k0[:, :], rng[:, 0:1], 0.1, ALU.mult, ALU.add).then_inc(gv, 1)
                    e.wait_ge(gv, 5)
                    e.tensor_tensor(k0[:, :], shift[:, :], sign[:, :], ALU.mult).then_inc(gv, 1)
                    e.wait_ge(gv, 6)
                    e.tensor_copy(shift[:, :], k0[:, :]).then_inc(gv, 1)
                    e.wait_ge(gv, 7)
                    top.run(VE, e, plan)
                    e.wait_ge(ld, DMAS * len(loaded))
                    e.tensor_scalar(f1[:, :, :], q1[:, :, :], -128.0, None, ALU.add).then_inc(pv, 1)
                    e.tensor_scalar(f2[:, :, :], q2[:, :, :], -128.0, None, ALU.add).then_inc(pv, 1)
                    e.tensor_scalar(hb2[:, :], vec_at["f_b2"], 0.5, None, ALU.mult)
                    e.wait_ge(pv, 2)
                    e.tensor_tensor(w1[:, :, :], f1[:, :, :], s1[:, :, :], ALU.mult)
                    e.scalar_tensor_tensor(w2[:, :, :], f2[:, :, :], 0.5, s2[:, :, :], ALU.mult, ALU.mult)
                    e.wait_ge(ga, 4)
                    e.tensor_scalar(A[:, :, :], A[:, :, :], -1.0, None, ALU.mult)

                @block.tensor
                def _(e):
                    e.wait_ge(gv, 1)
                    e.wait_ge(gm, 1)
                    passes(e, net[0][:, 0:1], [(gc_w1[:, k, :], mean[:, k:k + 1]) for k in range(KD)]).then_inc(gp, 1)
                    e.wait_ge(ga, 1)
                    e.matmul(net[1][0:64, 0:1], gc_w2[:, :], g1[:, :], start=True, stop=True).then_inc(gp, 1)
                    e.wait_ge(ga, 2)
                    e.matmul(net[2][:, 0:1], gw3[:, :], g2[:, :], start=True, stop=True).then_inc(gp, 1)
                    top.run(PE, e, plan)

                @block.scalar
                def _(e):
                    e.activation(x1T[:, 1, :], x1T[:, 1, :], ACT.Copy, accum_out=mean[:, 1:2]).then_inc(gm, 1)
                    e.wait_ge(gp, 1)
                    e.activation(g1[:, :], net[0][:, 0:1], ACT.Gelu, bias=gc_b1[:, 0:1], scale=1.0 / T).then_inc(ga, 1)
                    e.wait_ge(gp, 2)
                    e.activation(g2[:, :], net[1][0:64, 0:1], ACT.Gelu, bias=gc_b2[0:64, :]).then_inc(ga, 1)
                    e.wait_ge(gp, 3)
                    e.activation(gt[:, :], net[2][:, 0:1], ACT.Tanh, bias=hg3[:, 0:1], scale=0.5).then_inc(ga, 1)
                    top.run(SA, e, plan)
                    e.activation(A[:, :, :].rearrange("p k n -> p (k n)"), vec_at["c_A_log"], ACT.Exp).then_inc(ga, 1)

        x2T = x1T
        with ExitStack() as pd:
            def t(name, shape, dt=F32):
                return sb(name, shape, dt, within=pd)

            def many(name, shape, n=2, dt=F32):
                return [t(f"{name}{i}", shape, dt) for i in range(n)]

            lnb = [[t(f"{n}_{i}", sh) for n, sh in (("st", [P, NC, 6]), ("mv", [P, NC, 2]), ("ve", [P, NC]), ("rs", [P, NC]), ("nb", [P, NC]))] for i in range(4)]
            x2 = t("x2", [P, NC, DM])
            xc, zc, gated = t("xc", [P, KD, TB]), many("zc", [P, KD, TB]), t("gated", [P, KD, TB])
            va, vl, vd = (t(n, [P, KD, TB]) for n in ("va", "vl", "vd"))
            dtc, uc, acc = many("dtc", [P, KD, TB]), many("uc", [P, KD, TB]), many("acc", [P, KD, TB])
            bcf, parts = t("bcf", [96, TB]), many("parts", [96, TB], dt=BF16)
            h0 = t("h0", [P, NS, KD])
            av, bv, gv_ = many("av", [P, KD, TB], AHEAD), [nets, *many("bv", [P, KD, TB])], many("gv", [P, KD, TB])
            xl, x3 = t("xl", [P, NC, DM]), many("x3_", [P, NC, DM])
            xn, nT, f_h, x3b = xl, t("nT", [P, KD, TB]), t("f_h", [P, KF, TB]), t("x3b", [P, NC, DM])
            pb = psum(pd, "pd")
            p_in, p_out, p_ffn, p_B, p_C = pb[0], pb[1], pb[2:4], pb[4:6], pb[6:8]

            def load_x2(s, q):
                s.do(SP, "x2", lambda e, b: e.dma_start(x2[:, :, :], x2_tokens[:, bass.ds(b.chunk(), NC), :]), "scan_out.xl_b@-1", dmas=1)

            def scan_in(s, q):
                def project(m):
                    return lambda e, b: passes(e, p_in[:, :], [(w_xz[:, k, m * P:(m + 1) * P], x2T[:, k, bass.ds(b.token(), TB)]) for k in range(KD)])
                for m in range(KD):
                    s.do(PE, f"x{m}", project(m), f"xe{m - 1}" if m else f"ze{KD - 1}@-1")
                    s.do(SA, f"xe{m}", lambda e, b, m=m: e.activation(xc[:, m, :], p_in[:, :], ACT.Identity, bias=b_in[:, m:m + 1]),
                         f"x{m}", "u@-1", "bc@-1")
                for m in range(KD):
                    s.do(PE, f"d{m}", lambda e, b, m=m: passes(e, p_in[:, :], [(w_dt[:, k, m * P:(m + 1) * P], xc[:, k, :]) for k in range(KD)]),
                         f"xe{KD - 1}", *([f"vr{m - 1}"] if m else []))
                    s.do(SA, f"va{m}", lambda e, b, m=m: e.activation(va[:, m, :], p_in[:, :], ACT.Abs, bias=b_dt[:, m:m + 1]), f"d{m}", "ve@-1")
                    s.do(SA, f"vr{m}", lambda e, b, m=m: e.activation(dtc[q][:, m, :], p_in[:, :], ACT.Relu, bias=b_dt[:, m:m + 1]), f"d{m}",
                         f"core.a{NS - 1}_1@-2", "u@-2")
                s.do(PE, "bc", lambda e, b: passes(e, p_in[0:96, :], [
                    (w_bc[:, k, :, :, :].rearrange("p g m n -> p (g m n)"), xc[:, k, :]) for k in range(KD)]), f"vr{KD - 1}")
                s.do(SA, "bce", lambda e, b: e.activation(bcf[:, :], p_in[0:96, :], ACT.Identity, bias=b_bc[0:96, :]), "bc", "p3@-1")
                s.do(SA, "vy", lambda e, b: e.activation(vec(va[:, :, :]), vec(va[:, :, :]), ACT.Exp, scale=-1.0), f"va{KD - 1}", "va0")
                s.do(SA, "vl", lambda e, b: e.activation(vec(vl[:, :, :]), vec(va[:, :, :]), ACT.Ln, bias=1.0), "vy", "vs@-1")
                s.do(SA, "vd", lambda e, b: e.activation(vec(vd[:, :, :]), vec(va[:, :, :]), ACT.Identity, bias=1.0), "vy", "vs@-1")
                s.do(VE, "ve", lambda e, b: e.scalar_tensor_tensor(vec(vd[:, :, :]), vec(vd[:, :, :]), -1.0, vec(va[:, :, :]), ALU.add, ALU.subtract), "vd")
                s.do(PO, "vs", lambda e, b: e.tensor_tensor(vec(vl[:, :, :]), vec(vl[:, :, :]), vec(vd[:, :, :]), ALU.subtract), "vl", "ve")
                s.do(SA, "ph", lambda e, b: e.activation(parts[q][:, :], p_in[0:96, :], ACT.Identity, bias=b_bc[0:96, :]), "bc", f"core.C{NS - 1}@-2", "p3@-2")
                s.do(PO, "pr", lambda e, b: e.tensor_tensor(bcf[:, :], bcf[:, :], parts[q][:, :], ALU.subtract), "ph", "bce")
                s.do(PO, "vt", lambda e, b: e.tensor_tensor(vec(dtc[q][:, :, :]), vec(dtc[q][:, :, :]), vec(vl[:, :, :]), ALU.add), "vs", f"vr{KD - 1}", "vr0")
                s.do(VE, "p1", lambda e, b: e.tensor_copy(parts[q][32:64, :], bcf[32:64, :]), "pr")
                s.do(VE, "p2", lambda e, b: e.tensor_copy(parts[q][64:96, :], bcf[64:96, :]), "pr")
                s.do(PO, "u", lambda e, b: e.tensor_tensor(vec(uc[q][:, :, :]), vec(dtc[q][:, :, :]), vec(xc[:, :, :]), ALU.mult), "vt", f"core.b{NS - 1}@-2")
                s.do(VE, "pl", lambda e, b: e.tensor_tensor(bcf[64:96, :], bcf[64:96, :], parts[q][64:96, :], ALU.subtract), "p2")
                s.do(VE, "p3", lambda e, b: e.tensor_copy(parts[q][64:96, :], bcf[64:96, :]), "pl", "p1")
                for m in range(KD):
                    s.do(SA, f"dx{m}", lambda e, b, m=m: e.activation(acc[q][:, m, :], xc[:, m, :], ACT.Copy, scale=Dc[:, m:m + 1]),
                         f"xe{m}", "scan_out.gate@-2")
                for m in range(KD):
                    s.do(PE, f"z{m}", project(KD + m), f"ze{m - 1}" if m else "ph")
                    s.do(SA, f"ze{m}", lambda e, b, m=m: e.activation(zc[q][:, m, :], p_in[:, :], ACT.Identity, bias=b_in[:, KD + m:KD + m + 1]),
                         f"z{m}", "scan_out.gate@-2")

            def scan_z(s, q):
                s.do(SA, "z", lambda e, b: e.activation(vec(zc[q][:, :, :]), vec(zc[q][:, :, :]), ACT.Silu), "scan_in.ze1", "scan_in.ze0")

            def core(s, q):
                def back(label, n, by=2):
                    return f"{label.format((n - by) % NS)}@{(n - by) // NS}"

                def wide(x):
                    return x.rearrange("p (o t) -> p o t", o=1).to_broadcast([P, KD, TB])

                def decay(n):
                    for k in range(KD):
                        s.do(SA, f"a{n}_{k}", lambda e, b, n=n, k=k: e.activation(av[n % AHEAD][:, k, :], dtc[q][:, k, :], ACT.Exp, scale=A[:, k, n:n + 1]),
                             "scan_in.vt", back("s{}_%d" % k, n, AHEAD))
                def into(n):
                    s.do(PE, f"B{n}", lambda e, b, n=n: e.matmul(p_B[n % 2][:, :], sel[:, n, :], parts[q][:, :], start=True, stop=True),
                         "scan_in.p3", back("b{}", n))

                def product(n):
                    s.do(VE, f"b{n}", lambda e, b, n=n: e.tensor_tensor(
                        bv[n % 3][:, :, :], uc[q][:, :, :], wide(p_B[n % 2][:, :]), ALU.mult),
                         "scan_in.u", f"B{n}", *(f"{l}{n - 3}" if n >= 3 else f"{l}{max(m for m in range(NS) if m % 3 == n)}@-1" for l in ("g", "hs")))
                for n in range(3):
                    decay(n)
                into(0)
                product(0)
                for n in range(NS):
                    if n + 1 < NS:
                        into(n + 1)
                    s.do(PE, f"C{n}", lambda e, b, n=n: e.matmul(p_C[n % 2][:, :], sel[:, NS + n, :], parts[q][:, :], start=True, stop=True), back("g{}", n))
                    if n + 3 < NS:
                        decay(n + 3)
                    for k in range(KD):
                        s.do(VE, f"s{n}_{k}", lambda e, b, n=n, k=k: e.tensor_tensor_scan(
                            bv[n % 3][:, k, :], av[n % AHEAD][:, k, :], bv[n % 3][:, k, :], h0[:, n, k:k + 1], ALU.mult, ALU.add),
                            f"b{n}", f"a{n}_{k}", f"hs{n}@-1")
                    if n + 1 < NS:
                        product(n + 1)
                    s.do(VE, f"hs{n}", lambda e, b, n=n: e.tensor_copy(h0[:, n, :], bv[n % 3][:, :, TB - 1]), f"s{n}_1")
                    s.do(VE, f"g{n}", lambda e, b, n=n: e.tensor_tensor(gv_[n % 2][:, :, :], bv[n % 3][:, :, :], wide(p_C[n % 2][:, :]), ALU.mult),
                         f"s{n}_1", f"C{n}", back("+{}", n))
                    s.do(PO, f"+{n}", lambda e, b, n=n: e.tensor_tensor(vec(acc[q][:, :, :]), vec(acc[q][:, :, :]), vec(gv_[n % 2][:, :, :]), ALU.add),
                         f"g{n}", f"+{n - 1}" if n else "scan_in.dx1")

            def scan_out(s, q):
                s.do(VE, "gate", lambda e, b: e.tensor_tensor(vec(gated[:, :, :]), vec(acc[q][:, :, :]), vec(zc[q][:, :, :]), ALU.mult),
                     f"core.+{NS - 1}", "scan_z.z", f"o{NC - 1}@-1")
                for c in range(NC):
                    s.do(PE, f"o{c}", lambda e, b, c=c: passes(e, p_out[:, 0:DM], [
                        (gated[:, k, c * CH:(c + 1) * CH], w_o[:, k, :]) for k in range(KD)]), "gate", f"pre{c - 1}" if c else f"pre{NC - 1}@-1")
                    if c == 0:
                        s.gap(2)
                        s.do(PO, "xb", lambda e, b: e.tensor_tensor(xl[:, :, :], x2[:, :, :], every(b_o), ALU.add), "load_x2.x2", f"l4_n{NC - 1}@-1", f"ffn_in.fT{NC - 1}@-1")
                    s.gap(2)
                    s.do(VE, f"pre{c}", lambda e, b, c=c: e.tensor_tensor(xl[:, c, :], p_out[:, 0:DM], xl[:, c, :], ALU.add), f"o{c}", "xb")
                layer_norm(s, "l3", lambda c: xl[:, c, :], lambda c: xl[:, c, :], *lnb[0], lambda c: [f"pre{c}"], [f"pre{NC - 1}"])
                s.do(PO, "xl_g", lambda e, b: e.tensor_tensor(xl[:, :, :], xl[:, :, :], every(gam), ALU.mult), f"l3_n{NC - 1}")
                s.do(PO, "xl_a", lambda e, b: e.tensor_tensor(xl[:, :, :], xl[:, :, :], every(bet), ALU.add), "xl_g")
                s.do(PO, "xl_b", lambda e, b: e.tensor_tensor(xl[:, :, :], xl[:, :, :], x2[:, :, :], ALU.add), "xl_a")
                s.gap(14)
                layer_norm(s, "l4", lambda c: xl[:, c, :], lambda c: x3[q][:, c, :], *lnb[1], lambda c: ["xl_b"], ["ffn_in.l5_n3@-2", "ffn_up.xb@-2"], on=SA)

            def every(v):
                return v.rearrange("p (o f) -> p o f", o=1).to_broadcast([P, NC, DM])

            def ffn_in(s, q):
                layer_norm(s, "l5", lambda c: x3[q][:, c, :], lambda c: xn[:, c, :], *lnb[2], lambda c: [f"scan_out.l4_n{NC - 1}"], [f"fT{NC - 1}@-1"], on=SA)
                for c in range(NC):
                    bank = p_ffn[c % 2]

                    def tr(e, b, c=c, bank=bank):
                        for k in range(KD):
                            i = e.transpose(bank[:, k * P:(k + 1) * P], xn[:, c, k * P:(k + 1) * P], ident[:, :])
                        return i
                    s.do(PE, f"fT{c}", tr, f"l5_n{NC - 1}", f"fTe{c - 2}_1" if c > 1 else f"ffn_out.w{c}@-1")
                    for k in range(KD):
                        s.do(SA, f"fTe{c}_{k}", lambda e, b, c=c, k=k, bank=bank: e.activation(
                            nT[:, k, c * CH:(c + 1) * CH], bank[:, k * P:(k + 1) * P], ACT.Identity, bias=lb[:, k:k + 1], scale=lg[:, k:k + 1]),
                            f"fT{c}", f"ffn_up.u{KF - 1}@-1")

            def ffn_up(s, q):
                s.do(PO, "xa", lambda e, b: e.tensor_tensor(x3b[:, :, :], x3[q][:, :, :], every(hb2[:, :]), ALU.add), f"scan_out.l4_n{NC - 1}", "ffn_out.store@-1")
                s.do(PO, "xb", lambda e, b: e.tensor_tensor(x3b[:, :, :], x3b[:, :, :], x3[q][:, :, :], ALU.add), "xa")
                for m in range(KF):
                    bank = p_ffn[m % 2]
                    s.do(PE, f"u{m}", lambda e, b, m=m, bank=bank: passes(e, bank[:, :], [
                        (w1[:, k, m * P:(m + 1) * P], nT[:, k, :]) for k in range(KD)]), f"ffn_in.fTe{NC - 1}_1", *([f"ue{m - 2}"] if m > 1 else []))
                    s.do(SA, f"ue{m}", lambda e, b, m=m, bank=bank: e.activation(f_h[:, m, :], bank[:, :], ACT.Identity, bias=b1[:, m:m + 1]),
                         f"u{m}", f"ffn_out.o{NC - 1}@-1")

            def ffn_act(s, q):
                for g in (0, 1):
                    s.do(SA, f"si{g}", lambda e, b, g=g: e.activation(vec(f_h[:, g * KF // 2:(g + 1) * KF // 2, :]), vec(f_h[:, g * KF // 2:(g + 1) * KF // 2, :]), ACT.Silu),
                         f"ffn_up.ue{KF - 1}")

            def ffn_out(s, q):
                for c in range(NC):
                    bank = p_ffn[c // 2]
                    s.do(PE, f"o{c}", lambda e, b, c=c, bank=bank: passes(e, bank[:, (c % 2) * DM:(c % 2 + 1) * DM], [
                        *((f_h[:, k, c * CH:(c + 1) * CH], w2[:, k, :]) for k in range(KF)), (ident[:, :], x3b[:, c, :])]),
                        "ffn_act.si1", "ffn_up.xb")
                    if c % 2:
                        s.gap(3)
                        s.do(SA, f"w{c // 2}", lambda e, b, c=c, bank=bank: e.activation(
                            x3b[:, c - 1:c + 1, :], bank[:, :].rearrange("p (c f) -> p c f", c=2), ACT.Copy), f"o{c}")
                layer_norm(s, "l6", lambda c: x3b[:, c, :], lambda c: x3b[:, c, :], *lnb[3], lambda c: [f"w{c // 2}"], [], on=SA)
                s.do(SP, "store", lambda e, b: e.dma_start(
                    out.rearrange("(n p) f -> p n f", p=P)[:, bass.ds(b.chunk(), NC), :], x3b[:, :, :]), f"l6_n{NC - 1}", dmas=1)

            for name, fn in (("load_x2", load_x2), ("scan_in", scan_in), ("scan_z", scan_z), ("core", core), ("scan_out", scan_out),
                             ("ffn_in", ffn_in), ("ffn_up", ffn_up), ("ffn_act", ffn_act), ("ffn_out", ffn_out)):
                Stage(top, name, fn)
            plan = [("load_x2", 1.600, 1.700), ("scan_in", 0.000, 0.850), ("scan_z", 1.400, 1.400 + POINT), ("core", 1.000, 1.986), ("scan_out", 2.050, 2.750),
                    ("ffn_in", 2.763, 2.995), ("ffn_up", 2.993, 3.393), ("ffn_act", 3.400, 3.400 + POINT), ("ffn_out", 3.534, 4.000)]
            with nc.Block() as block:
                block.vector(lambda e: e.memset(h0[:, :, :], 0.0))
            with nc.Block() as block:
                def sp(e):
                    top.run(SP, e, plan)
                    for q in (0, 1):
                        e.wait_ge(top.stages["ffn_out"].sem["store"][q], DMAS * (NB // 2 + 1))
                block.sync(sp)
                block.tensor(lambda e: top.run(PE, e, plan))
                block.vector(lambda e: top.run(VE, e, plan))
                block.gpsimd(lambda e: top.run(PO, e, plan))
                block.scalar(lambda e: top.run(SA, e, plan))


def kernel(**inputs):
    import numpy as np
    import concourse.bacc as bacc
    from concourse.bass_utils import run_bass_kernel_spmd

    a = {k: np.asarray(v) for k, v in inputs.items()}
    L0, L1 = "L0_attn_", "L1_attn_"
    F0, F1 = "L0_ffn_", "L1_ffn_"

    def column(v):
        v = v.reshape(v.shape[0], -1)
        if v.shape[0] < P:
            v = np.concatenate([v, np.zeros((P - v.shape[0], v.shape[1]), v.dtype)])
        return v.reshape(-1, P, v.shape[1]).transpose(1, 0, 2).reshape(P, -1)

    down = {"cn_b1": a[F0 + "cn_b1"], "cn_b2": a[F0 + "cn_b2"], "cn_b3": a[F0 + "cn_b3"], "cn_w4": a[F0 + "cn_w4"],
            "gc_b1": a[F0 + "gc_b1"], "gc_b2": a[F0 + "gc_b2"], "gc_w3": a[F0 + "gc_w3"],
            "conv_b": a[L0 + "conv_b"], "conv_w": a[L0 + "conv_w"], "norm_w": a[L0 + "norm_w"],
            "c_b_in": a[L1 + "b_in"], "c_b_dt": a[L1 + "b_dt"], "c_b_bc": np.concatenate([a[L1 + "b_B"], a[L1 + "b_C"]] * 3),
            "c_D": a[L1 + "D"], "c_A_log": a[L1 + "A_log"],
            "f_gamma": a[F1 + "ln_gamma"], "f_beta": a[F1 + "ln_beta"], "f_b1": a[F1 + "fc1_bias"]}
    every = {"cn_b4": a[F0 + "cn_b4"], "gc_b3": a[F0 + "gc_b3"], "adaptive_range": a[F0 + "adaptive_range"],
             "dt_bias": a[L0 + "dt_bias"], "A_log": a[L0 + "A_log"], "D": a[L0 + "D"],
             "c_gamma": a[L1 + "gamma"], "c_beta": a[L1 + "beta"], "c_b_out": a[L1 + "b_out"], "f_b2": a[F1 + "fc2_bias"]}
    arrays = {
        "u": a[L0 + "u"][0], "uT": a[L0 + "u"][0].T, "W_inT": a[L0 + "W_in"].T, "W_outT": a[L0 + "W_out"].T,
        **{n: a[F0 + n] for n in ("cn_w1", "cn_w2", "cn_w3", "gc_w1", "gc_w2")},
        **{f"c_{n}T": a[L1 + n].T for n in ("w_in", "w_dt", "w_B", "w_C", "w_out")},
        "f_q1": a[F1 + "fc1_q"], "f_s1": a[F1 + "fc1_scales"], "f_q2": a[F1 + "fc2_q"], "f_s2": a[F1 + "fc2_scales"],
        "columns": np.concatenate([column(down[n]) for n, _ in COLUMNS], axis=1),
        "everywhere": np.concatenate([every[n].reshape(-1) for n, _ in EVERYWHERE]),
    }
    arrays = {f"in_{k}": np.ascontiguousarray(v) for k, v in arrays.items()}
    nc = bacc.Bacc("TRN2", target_bir_lowering=False, num_devices=1)
    dram = {k[3:]: nc.dram_tensor(k, v.shape, mybir.dt.from_np(v.dtype), kind="ExternalInput").ap() for k, v in arrays.items()}
    out = nc.dram_tensor("out", (T, DM), F32, kind="ExternalOutput").ap()
    build(nc, dram, out, nc.dram_tensor("x2_tokens", (T, DM), F32, kind="Internal").ap())
    r = run_bass_kernel_spmd(nc, [arrays], core_ids=[0])
    return r.results[0]["out"].reshape(1, T, DM)
```
